# Optimizing a Trainium2 kernel written in Bass

```python
import numpy as np
import jax
import jax.numpy as jnp

def _softmax(x, axis=-1):
    return jax.nn.softmax(x, axis=axis)

def _gelu(x):
    return jax.nn.gelu(x, approximate=True)

def _silu(x):
    return jax.nn.silu(x)

def _sigmoid(x):
    return jax.nn.sigmoid(x)

def _layernorm(x, axis=-1, eps=1e-05):
    m = jnp.mean(x, axis=axis, keepdims=True)
    v = jnp.var(x, axis=axis, keepdims=True)
    return (x - m) / jnp.sqrt(v + eps)

def _scatter_add(tgt, idx, src, axis=0):
    return tgt.at[idx].add(src)

def _segment_sum(src, seg, n):
    return jax.ops.segment_sum(src, seg, n)
kernel_name = 'mk_adaln_d2_jaxref_r8_f3e6c4'

def setup_inputs(seed: int=0):
    np.random.seed(seed)
    _w = jnp.asarray

    def _L0_attn_setup():
        import jax, jax.numpy as jnp
        import numpy as np
        EMB_DIM = 256
        NUM_HEADS = 16
        HEAD_DIM = EMB_DIM // NUM_HEADS
        B, T = (4, 256)
        key = jax.random.key(seed)
        ks = jax.random.split(key, 6)
        s = lambda fan_in: 1.0 / np.sqrt(fan_in)
        return {'x': jax.random.normal(ks[0], (B, T, EMB_DIM), dtype=jnp.float32), 'Wq': jax.random.normal(ks[1], (EMB_DIM, EMB_DIM), dtype=jnp.float32) * s(EMB_DIM), 'Wk': jax.random.normal(ks[2], (EMB_DIM, HEAD_DIM), dtype=jnp.float32) * s(EMB_DIM), 'Wv': jax.random.normal(ks[3], (EMB_DIM, HEAD_DIM), dtype=jnp.float32) * s(EMB_DIM), 'Wo': jax.random.normal(ks[4], (EMB_DIM, EMB_DIM), dtype=jnp.float32) * s(EMB_DIM), 'bo': jax.random.normal(ks[5], (EMB_DIM,), dtype=jnp.float32) * 0.01}
    _L0_attn_in = _L0_attn_setup()

    def _L0_ffn_setup():
        import math
        import jax, jax.numpy as jnp
        import numpy as np
        NUM_EXPERTS = 8
        HIDDEN = 256
        INTER = 1024
        CAP_FACTOR = 1.25
        MIN_CAP = 4
        B, S = (4, 256)

        def _capacity(num_tokens: int, num_experts: int) -> int:
            cap = math.floor(CAP_FACTOR * num_tokens / num_experts)
            cap += cap % 2
            return max(cap, MIN_CAP)
        key = jax.random.key(seed)
        k1, k2, k3, k4 = jax.random.split(key, 4)
        std_h = math.sqrt(0.1 / HIDDEN)
        std_i = math.sqrt(0.1 / INTER)
        inputs = jax.random.normal(k1, (B, S, HIDDEN), dtype=jnp.float32)
        gate_weight = jax.random.normal(k2, (NUM_EXPERTS, HIDDEN), dtype=jnp.float32) * std_h
        wi = jax.random.normal(k3, (NUM_EXPERTS, HIDDEN, INTER), dtype=jnp.float32) * std_h
        wo = jax.random.normal(k4, (NUM_EXPERTS, INTER, HIDDEN), dtype=jnp.float32) * std_i
        return {'inputs': inputs, 'gate_weight': gate_weight, 'wi': wi, 'wo': wo}
    _L0_ffn_in = _L0_ffn_setup()
    _L0_c = _w((lambda *s: np.random.randn(*s).astype(np.float32) * 0.05)(1, 256))
    _L0_wmod = _w((lambda *s: np.random.randn(*s).astype(np.float32) * 0.05)(256, 6 * 256) * 256 ** (-0.5))

    def _L1_attn_setup():
        import jax, jax.numpy as jnp
        import numpy as np
        B, S, D = (4, 512, 256)
        IDENTITY_WEIGHT = 0.5
        ROT_DIM = D // 2

        def _layernorm(x, gamma, beta, eps=1e-05):
            mu = jnp.mean(x, axis=-1, keepdims=True)
            var = jnp.var(x, axis=-1, keepdims=True)
            return (x - mu) * jax.lax.rsqrt(var + eps) * gamma + beta

        def _rotary(t, rot_dim, theta=10000.0):
            seq = t.shape[-2]
            inv_freq = 1.0 / theta ** (jnp.arange(0, rot_dim, 2, dtype=jnp.float32) / rot_dim)
            freqs = jnp.arange(seq, dtype=jnp.float32)[:, None] * inv_freq[None, :]
            freqs = jnp.repeat(freqs, 2, axis=-1)
            cos, sin = (jnp.cos(freqs), jnp.sin(freqs))
            t_rot, t_pass = (t[..., :rot_dim], t[..., rot_dim:])
            x1, x2 = (t_rot[..., 0::2], t_rot[..., 1::2])
            rot_half = jnp.stack([-x2, x1], axis=-1).reshape(t_rot.shape)
            return jnp.concatenate([t_rot * cos + rot_half * sin, t_pass], axis=-1)

        def _cos_sim(x):
            return x / jnp.linalg.norm(x, axis=-1, keepdims=True)
        key = jax.random.key(seed)
        ks = jax.random.split(key, 3)
        scale = 0.02
        return {'X': jax.random.normal(ks[0], (B, S, D), jnp.float32), 'W_in': jax.random.normal(ks[1], (D, 3 * D), jnp.float32) * scale, 'b_in': jnp.zeros((3 * D,), jnp.float32), 'W_out': jax.random.normal(ks[2], (D, D), jnp.float32) * scale, 'b_out': jnp.zeros((D,), jnp.float32), 'gamma': jnp.ones((D,), jnp.float32), 'beta': jnp.zeros((D,), jnp.float32)}
    _L1_attn_in = _L1_attn_setup()

    def _L1_ffn_setup():
        import jax, jax.numpy as jnp
        import numpy as np
        E = 8
        H = 256
        F = 512
        B, S = (2, 128)
        JITTER = 0.01
        TOP_K = 2

        def _masked_sampling_omp(scores):
            vals, idx = jax.lax.top_k(scores, TOP_K)
            abs_s = jnp.abs(scores)
            thr1 = vals[:, 0:1]
            factor1 = jnp.maximum(abs_s, thr1)
            mask1 = (thr1 - scores) / factor1 > 2.0 * JITTER
            p1 = jax.nn.softmax(jnp.where(mask1, -jnp.inf, scores), axis=-1)
            m1 = jnp.take_along_axis(p1, idx[:, 0:1], axis=-1)
            thr2 = vals[:, 1:2]
            factor2 = jnp.maximum(abs_s, thr2)
            mask2 = (thr2 - scores) / factor2 > 2.0 * JITTER
            is_top1 = jnp.arange(scores.shape[-1])[None, :] == idx[:, 0:1]
            p2 = jax.nn.softmax(jnp.where(is_top1 | mask2, -jnp.inf, scores), axis=-1)
            m2 = jnp.take_along_axis(p2, idx[:, 1:2], axis=-1)
            return (jnp.concatenate([m1, m2], axis=-1), idx)
        key = jax.random.key(seed)
        k0, k1, k2, k3, k4 = jax.random.split(key, 5)
        s = 0.02
        return {'hidden_states': jax.random.normal(k0, (B, S, H), jnp.float32), 'gate_w': jax.random.normal(k1, (E, H), jnp.float32) * s, 'w1': jax.random.normal(k2, (E, F, H), jnp.float32) * s, 'w2': jax.random.normal(k3, (E, H, F), jnp.float32) * s, 'w3': jax.random.normal(k4, (E, F, H), jnp.float32) * s}
    _L1_ffn_in = _L1_ffn_setup()
    _L1_c = _w((lambda *s: np.random.randn(*s).astype(np.float32) * 0.05)(1, 256))
    _L1_wmod = _w((lambda *s: np.random.randn(*s).astype(np.float32) * 0.05)(256, 6 * 256) * 256 ** (-0.5))
    _d = {'L0_attn_x': _L0_attn_in['x'], 'L0_attn_Wq': _L0_attn_in['Wq'], 'L0_attn_Wk': _L0_attn_in['Wk'], 'L0_attn_Wv': _L0_attn_in['Wv'], 'L0_attn_Wo': _L0_attn_in['Wo'], 'L0_attn_bo': _L0_attn_in['bo'], 'L0_ffn_gate_weight': _L0_ffn_in['gate_weight'], 'L0_ffn_wi': _L0_ffn_in['wi'], 'L0_ffn_wo': _L0_ffn_in['wo'], 'L0_c': _L0_c, 'L0_wmod': _L0_wmod, 'L1_attn_W_in': _L1_attn_in['W_in'], 'L1_attn_b_in': _L1_attn_in['b_in'], 'L1_attn_W_out': _L1_attn_in['W_out'], 'L1_attn_b_out': _L1_attn_in['b_out'], 'L1_attn_gamma': _L1_attn_in['gamma'], 'L1_attn_beta': _L1_attn_in['beta'], 'L1_ffn_gate_w': _L1_ffn_in['gate_w'], 'L1_ffn_w1': _L1_ffn_in['w1'], 'L1_ffn_w2': _L1_ffn_in['w2'], 'L1_ffn_w3': _L1_ffn_in['w3'], 'L1_c': _L1_c, 'L1_wmod': _L1_wmod}
    _x0 = _d['L0_attn_x']
    _d['L0_attn_x'] = jax.random.normal(jax.random.fold_in(jax.random.key(seed), 1), (1, 2048, 256), dtype=_x0.dtype)
    del _x0
    return _d

def reference(L0_attn_x, L0_attn_Wq, L0_attn_Wk, L0_attn_Wv, L0_attn_Wo, L0_attn_bo, L0_ffn_gate_weight, L0_ffn_wi, L0_ffn_wo, L0_c, L0_wmod, L1_attn_W_in, L1_attn_b_in, L1_attn_W_out, L1_attn_b_out, L1_attn_gamma, L1_attn_beta, L1_ffn_gate_w, L1_ffn_w1, L1_ffn_w2, L1_ffn_w3, L1_c, L1_wmod):

    def _L0_attn_ref(x, Wq, Wk, Wv, Wo, bo):
        import jax, jax.numpy as jnp
        import numpy as np
        EMB_DIM = 256
        NUM_HEADS = 16
        HEAD_DIM = EMB_DIM // NUM_HEADS
        B, T = (4, 256)
        Bsz, Tlen, C = x.shape
        H, D = (NUM_HEADS, HEAD_DIM)
        q = (x @ Wq).reshape(Bsz, Tlen, H, D)
        k = x @ Wk
        v = x @ Wv
        scores = jnp.einsum('bihd,bjd->bhij', q, k) / jnp.sqrt(jnp.float32(D))
        i = jnp.arange(Tlen)[:, None]
        j = jnp.arange(Tlen)[None, :]
        causal = j <= i
        scores = jnp.where(causal, scores, -jnp.inf)
        attn = jax.nn.softmax(scores, axis=-1)
        out = jnp.einsum('bhij,bjd->bihd', attn, v).reshape(Bsz, Tlen, C)
        return out @ Wo + bo

    def _L0_ffn_ref(inputs, gate_weight, wi, wo):
        import math
        import jax, jax.numpy as jnp
        import numpy as np
        NUM_EXPERTS = 8
        HIDDEN = 256
        INTER = 1024
        CAP_FACTOR = 1.25
        MIN_CAP = 4
        B, S = (4, 256)

        def _capacity(num_tokens: int, num_experts: int) -> int:
            cap = math.floor(CAP_FACTOR * num_tokens / num_experts)
            cap += cap % 2
            return max(cap, MIN_CAP)
        b, s, h = inputs.shape
        tokens = inputs.reshape(-1, h)
        T = tokens.shape[0]
        E = gate_weight.shape[0]
        C = _capacity(T, E)
        logits = tokens.astype(jnp.float32) @ gate_weight.astype(jnp.float32).T
        probs = jax.nn.softmax(logits, axis=-1)
        top1 = jnp.argmax(logits, axis=-1)
        mask = jax.nn.one_hot(top1, E, dtype=jnp.int32)
        ranks = jnp.cumsum(mask, axis=0) - 1
        mask = mask * (ranks < C).astype(jnp.int32)
        ranks_tok = jnp.sum(mask * ranks, axis=-1)
        ranks_oh = jax.nn.one_hot(ranks_tok, C, dtype=jnp.float32)
        weight = mask.astype(probs.dtype) * probs
        combine_weights = weight[:, :, None] * ranks_oh[:, None, :]
        sec_mask = jax.lax.stop_gradient(combine_weights != 0).astype(inputs.dtype)
        dispatch = jnp.einsum('tec,th->ech', sec_mask, tokens)
        hmid = jnp.einsum('ech,ehi->eci', dispatch, wi)
        hmid = jax.nn.gelu(hmid, approximate=False)
        eout = jnp.einsum('eci,eih->ech', hmid, wo)
        out = jnp.einsum('tec,ech->th', combine_weights.astype(inputs.dtype), eout)
        return out.reshape(b, s, h)

    def _L1_attn_ref(X, W_in, b_in, W_out, b_out, gamma, beta):
        import jax, jax.numpy as jnp
        import numpy as np
        B, S, D = (4, 512, 256)
        IDENTITY_WEIGHT = 0.5
        ROT_DIM = D // 2

        def _layernorm(x, gamma, beta, eps=1e-05):
            mu = jnp.mean(x, axis=-1, keepdims=True)
            var = jnp.var(x, axis=-1, keepdims=True)
            return (x - mu) * jax.lax.rsqrt(var + eps) * gamma + beta

        def _rotary(t, rot_dim, theta=10000.0):
            seq = t.shape[-2]
            inv_freq = 1.0 / theta ** (jnp.arange(0, rot_dim, 2, dtype=jnp.float32) / rot_dim)
            freqs = jnp.arange(seq, dtype=jnp.float32)[:, None] * inv_freq[None, :]
            freqs = jnp.repeat(freqs, 2, axis=-1)
            cos, sin = (jnp.cos(freqs), jnp.sin(freqs))
            t_rot, t_pass = (t[..., :rot_dim], t[..., rot_dim:])
            x1, x2 = (t_rot[..., 0::2], t_rot[..., 1::2])
            rot_half = jnp.stack([-x2, x1], axis=-1).reshape(t_rot.shape)
            return jnp.concatenate([t_rot * cos + rot_half * sin, t_pass], axis=-1)

        def _cos_sim(x):
            return x / jnp.linalg.norm(x, axis=-1, keepdims=True)
        Xn = _layernorm(X, gamma, beta)
        QKV = Xn @ W_in + b_in
        Q, K, V = jnp.split(QKV, 3, axis=-1)
        K = _rotary(K, ROT_DIM)
        V = _rotary(V, ROT_DIM)
        A = jnp.sum(_cos_sim(K) * _cos_sim(V), axis=-2)
        A = (1.0 - IDENTITY_WEIGHT) * A + IDENTITY_WEIGHT
        Y = A[:, None, :] * Q
        Y = Y @ W_out + b_out
        return Y + X

    def _L1_ffn_ref(hidden_states, gate_w, w1, w2, w3):
        import jax, jax.numpy as jnp
        import numpy as np
        E = 8
        H = 256
        F = 512
        B, S = (2, 128)
        JITTER = 0.01
        TOP_K = 2

        def _masked_sampling_omp(scores):
            vals, idx = jax.lax.top_k(scores, TOP_K)
            abs_s = jnp.abs(scores)
            thr1 = vals[:, 0:1]
            factor1 = jnp.maximum(abs_s, thr1)
            mask1 = (thr1 - scores) / factor1 > 2.0 * JITTER
            p1 = jax.nn.softmax(jnp.where(mask1, -jnp.inf, scores), axis=-1)
            m1 = jnp.take_along_axis(p1, idx[:, 0:1], axis=-1)
            thr2 = vals[:, 1:2]
            factor2 = jnp.maximum(abs_s, thr2)
            mask2 = (thr2 - scores) / factor2 > 2.0 * JITTER
            is_top1 = jnp.arange(scores.shape[-1])[None, :] == idx[:, 0:1]
            p2 = jax.nn.softmax(jnp.where(is_top1 | mask2, -jnp.inf, scores), axis=-1)
            m2 = jnp.take_along_axis(p2, idx[:, 1:2], axis=-1)
            return (jnp.concatenate([m1, m2], axis=-1), idx)
        Bd, Sd, Hd = hidden_states.shape
        x = hidden_states.reshape(-1, Hd)
        scores = x @ gate_w.T
        mult, sel = _masked_sampling_omp(scores)
        h = jax.nn.silu(jnp.einsum('th,efh->etf', x, w1)) * jnp.einsum('th,efh->etf', x, w3)
        y = jnp.einsum('etf,ehf->eth', h, w2)
        coef = (jax.nn.one_hot(sel, gate_w.shape[0], dtype=x.dtype) * mult[..., None]).sum(axis=1)
        out = jnp.einsum('te,eth->th', coef, y)
        return out.reshape(Bd, Sd, Hd)
    x = L0_attn_x
    mod = (_silu(L0_c) @ L0_wmod).reshape(L0_c.shape[0], 6, 1, -1)
    sa, ca, ga, sb, cb, gb = (mod[:, 0], mod[:, 1], mod[:, 2], mod[:, 3], mod[:, 4], mod[:, 5])
    ga = (2 * (ga >= 0) - 1) * jnp.maximum(jnp.abs(ga), 0.25)
    gb = (2 * (gb >= 0) - 1) * jnp.maximum(jnp.abs(gb), 0.25)
    h = _layernorm(x, axis=-1) * (1 + ca) + sa
    x = x + ga * _L0_attn_ref(h, L0_attn_Wq, L0_attn_Wk, L0_attn_Wv, L0_attn_Wo, L0_attn_bo)
    h = _layernorm(x, axis=-1) * (1 + cb) + sb
    x = x + gb * _L0_ffn_ref(h, L0_ffn_gate_weight, L0_ffn_wi, L0_ffn_wo)
    mod = (_silu(L1_c) @ L1_wmod).reshape(L1_c.shape[0], 6, 1, -1)
    sa, ca, ga, sb, cb, gb = (mod[:, 0], mod[:, 1], mod[:, 2], mod[:, 3], mod[:, 4], mod[:, 5])
    ga = (2 * (ga >= 0) - 1) * jnp.maximum(jnp.abs(ga), 0.25)
    gb = (2 * (gb >= 0) - 1) * jnp.maximum(jnp.abs(gb), 0.25)
    h = _layernorm(x, axis=-1) * (1 + ca) + sa
    x = x + ga * _L1_attn_ref(h, L1_attn_W_in, L1_attn_b_in, L1_attn_W_out, L1_attn_b_out, L1_attn_gamma, L1_attn_beta)
    h = _layernorm(x, axis=-1) * (1 + cb) + sb
    x = x + gb * _L1_ffn_ref(h, L1_ffn_gate_w, L1_ffn_w1, L1_ffn_w2, L1_ffn_w3)
    return x

_drawn_inputs = setup_inputs


def setup_inputs(seed=0):
    import zlib

    import numpy as np

    out = dict(_drawn_inputs(seed))
    spreads = {'L1_attn_b_in': (0.0, 0.8),
     'L1_attn_b_out': (0.0, 0.34),
     'L1_attn_gamma': (1.0, 0.6),
     'L1_attn_beta': (0.0, 0.8)}
    factors = {'L0_attn_bo': 8.0,
     'L0_ffn_gate_weight': 8.0,
     'L0_ffn_wi': 8.0,
     'L0_ffn_wo': 8.0,
     'L1_attn_W_in': 3.443,
     'L1_attn_W_out': 3.28,
     'L1_ffn_gate_w': 8.0,
     'L1_ffn_w1': 7.206,
     'L1_ffn_w2': 7.12,
     'L1_ffn_w3': 7.128}
    for name, (base, spread) in spreads.items():
        noise = np.random.default_rng([zlib.crc32(name.encode()), seed]).standard_normal(out[name].shape)
        drawn = base * np.exp(spread * noise) if base else spread * noise
        out[name] = jnp.asarray(drawn.astype(out[name].dtype))
    for name, factor in factors.items():
        out[name] = (out[name] * factor).astype(out[name].dtype)
    return out
```

```python
import concourse.bass as bass
from concourse import mybir
from contextlib import ExitStack

FP = mybir.dt.float32
BF = mybir.dt.bfloat16
U32 = mybir.dt.uint32
ALU = mybir.AluOpType
ACT = mybir.ActivationFunctionType
AX = mybir.AxisListType

P = 128
T = 2048
D = 256
NT = T // P
KH = D // P
H, HD = 16, 16
GH = 4
NG = H // GH
QC = 512
NC = T // QC
TQ = QC // P
MODS = 6
SA, CA, GA, SB, CB, GB = range(MODS)
EPS = 1e-5
NEG = -1e30
E = 8
F0, CAP = 1024, 320
F1 = 512
BLK = 128
NB = (2 * T + E * (BLK - 1)) // BLK
PROD = 7
KROWS = PROD * HD
BROW = KROWS
KALL = KROWS + 2
ROT = 64


class Named:
    pass


def bcast(ap, n):
    return ap.unsqueeze(1).to_broadcast([ap.shape[0], n, ap.shape[1]])


def last_bcast(ap, n):
    return ap.unsqueeze(2).to_broadcast([ap.shape[0], ap.shape[1], n])


def stepper(eng, sem):
    count = [0]

    def step(ins):
        count[0] += 1
        ins.then_inc(sem, 1)
        eng.wait_ge(sem, count[0])
    return step


def quarter(ap, q):
    return ap[:, TQ * q:TQ * (q + 1), :]


def ln_stats(nc, dve, step, k, q, var_ready):
    tiles = range(TQ * q, TQ * (q + 1))
    for i in tiles:
        last = nc.vector.bn_stats(k.stats[:, i, :], k.x[:, i, :])
    step(last)
    for i in tiles:
        last = nc.vector.bn_aggr(k.mv[:, i, :], k.stats[:, i, :])
    step(last)
    nc.vector.tensor_scalar_add(k.var[:, TQ * q:TQ * (q + 1)], k.mv[:, TQ * q:TQ * (q + 1), 1],
                                EPS).then_inc(var_ready, 1)


def ln_rstd(nc, pool, k, q, var_ready, rstd_ready):
    pool.wait_ge(var_ready, q + 1)
    s = slice(TQ * q, TQ * (q + 1))
    nc.gpsimd.tensor_tensor(k.rstd[:, s], k.var[:, s], k.mhalf[:, s], ALU.pow).then_inc(rstd_ready, 1)


def ln_apply(nc, dve, step, k, q, scale, shift, rstd_ready, h_ready):
    if rstd_ready is not None:
        dve.wait_ge(rstd_ready, q + 1)
    for i in range(TQ * q, TQ * (q + 1)):
        last = nc.vector.tensor_scalar(k.h[:, i, :], k.x[:, i, :], k.mv[:, i, 0:1], k.rstd[:, i:i + 1],
                                       ALU.subtract, ALU.mult)
    step(last)
    hq = quarter(k.h, q)
    step(nc.vector.tensor_tensor(hq, hq, bcast(scale, TQ), ALU.mult))
    nc.vector.tensor_tensor(hq, hq, bcast(shift, TQ), ALU.add).then_inc(h_ready, 1)


def transpose_quarter(nc, k, src, q, banks):
    out = []
    for half in range(KH):
        for i in range(TQ):
            last = nc.tensor.transpose(banks[half][:, P * i:P * (i + 1)],
                                       src[:, TQ * q + i, P * half:P * (half + 1)], k.ident[:, :])
        out.append(last)
    return out


def phase_setup(nc, k, a, sem):
    with nc.psum_tensor("p0_mod", [P, 2, MODS * D], FP) as mod_ps, \
            nc.sbuf_tensor("silu_c", [P, 2, KH, P], FP) as silu_c, \
            nc.sbuf_tensor("c_col", [P, 2, KH], FP) as c_col, \
            nc.sbuf_tensor("wmod", [P, 2, KH, MODS * D], FP) as wmod, \
            nc.sbuf_tensor("gate_mag", [P, 2, D], FP) as gate_mag, \
            nc.sbuf_tensor("gate_sgn", [P, 2, D], FP) as gate_sgn, \
            nc.Block() as block:
        x_in = sem("x_in")
        mod_in = sem("mod_in")
        silu_done = sem("silu_done")
        mod_done = sem("mod_done")
        mod_copied = sem("mod_copied")
        dve_step = sem("p0_dve_step")
        pool_step = sem("p0_pool_step")
        half_set = sem("half_set")
        var_ready = sem("p0_var_ready")
        rstd_ready = sem("p0_rstd_ready")
        const_in = sem("const_in")

        @block.sync
        def _(sp):
            for layer, c in enumerate((a.L0_c, a.L1_c)):
                sp.dma_start(c_col[:, layer, :], c.rearrange("a (t p) -> p (a t)", p=P),
                             allow_slow_non_contiguous=True).then_inc(mod_in, 16)
            for layer, w in enumerate((a.L0_wmod, a.L1_wmod)):
                sp.dma_start(wmod[:, layer, :, :], w.rearrange("(t p) n -> p t n", p=P)).then_inc(mod_in, 16)
            for w, dst in ((a.L0_attn_Wq, k.wq), (a.L0_attn_Wv, k.wv), (a.L0_attn_Wo, k.wo)):
                sp.dma_start(dst[:, :, :], w.rearrange("(t p) n -> p t n", p=P)).then_inc(const_in, 16)
            sp.dma_start(k.wk1[:, :, :], a.L0_attn_Wk.rearrange("(t p) n -> p t n", p=P)).then_inc(const_in, 16)
            sp.dma_start(k.bo[:, :], a.L0_attn_bo.partition_broadcast(P)).then_inc(const_in, 16)
            sp.dma_start(k.kpart[:, :], a.kpart).then_inc(const_in, 16)
            sp.wait_ge(const_in, 16 * 6)

        @block.scalar
        def _(act):
            xv = a.L0_attn_x[0, :, :].rearrange("(i p) d -> p i d", p=P)
            for q in range(NC):
                act.dma_start(quarter(k.x, q), xv[:, TQ * q:TQ * (q + 1), :]).then_inc(x_in, 16)
            act.wait_ge(mod_in, 16 * 4)
            nc.scalar.activation(silu_c[:, :, :, :].rearrange("p l t n -> p (l t) n"),
                                 last_bcast(c_col[:, :, :].rearrange("p l t -> p (l t)"), P),
                                 ACT.Silu).then_inc(silu_done, 1)
            for layer in range(2):
                act.wait_ge(mod_done, layer + 1)
                nc.scalar.copy(k.mod[:, layer, :, :].rearrange("p m d -> p (m d)"),
                               mod_ps[:, layer, :]).then_inc(mod_copied, 1)

        @block.tensor
        def _(pe):
            pe.wait_ge(silu_done, 1)
            for layer in range(2):
                for n in range(MODS * D // 512):
                    for t in range(KH):
                        last = nc.tensor.matmul(mod_ps[:, layer, 512 * n:512 * (n + 1)], silu_c[:, layer, t, :],
                                                wmod[:, layer, t, 512 * n:512 * (n + 1)],
                                                start=(t == 0), stop=(t == KH - 1))
                last.then_inc(mod_done, 1)

        @block.vector
        def _(dve):
            step = stepper(dve, dve_step)
            for q in range(NC):
                dve.wait_ge(x_in, 16 * NC)
                ln_stats(nc, dve, step, k, q, var_ready)
            for layer in range(2):
                dve.wait_ge(mod_copied, layer + 1)
                m = k.mod[:, layer, :, :].rearrange("p (b m) d -> p b m d", b=2)
                step(nc.vector.tensor_scalar_add(m[:, :, 1, :], m[:, :, 1, :], 1.0))
                gate = m[:, :, 2, :]
                step(nc.vector.tensor_scalar(gate_sgn[:, :, :], gate, 0.0, 2.0, ALU.is_ge, ALU.mult))
                step(nc.vector.scalar_tensor_tensor(gate_mag[:, :, :], gate, -1.0, gate, ALU.mult, ALU.max))
                step(nc.vector.tensor_scalar_max(gate_mag[:, :, :], gate_mag[:, :, :], 0.25))
                step(nc.vector.scalar_tensor_tensor(gate, gate_sgn[:, :, :], -1.0, gate_mag[:, :, :],
                                                    ALU.add, ALU.mult))
            dve.wait_ge(rstd_ready, NC)

        @block.gpsimd
        def _(pool):
            step = stepper(pool, pool_step)
            nc.gpsimd.memset(k.mhalf[:, :], -0.5).then_inc(half_set, 1)
            nc.gpsimd.memset(k.vaug[:, :, :], 0.0)
            nc.gpsimd.memset(k.ident[:, :], 0.0)
            nc.gpsimd.memset(k.ones_bf[:, :], 1.0)
            step(nc.gpsimd.memset(k.maskq[:, :], 0.0))
            nc.gpsimd.memset(k.vaug[:, :, HD:HD + 1], 1.0)
            step(nc.gpsimd.affine_select(out=k.ident[:, :], in_=k.ident[:, :], compare_op=ALU.not_equal, fill=1.0,
                                         base=0, pattern=[[-1, P]], channel_multiplier=1))
            nc.gpsimd.tensor_copy(k.ident_bf[:, :], k.ident[:, :])
            nc.gpsimd.affine_select(out=k.maskq[:, :], in_=k.maskq[:, :], compare_op=ALU.is_ge, fill=NEG,
                                    base=0, pattern=[[-1, P]], channel_multiplier=1)
            step(nc.gpsimd.affine_select(out=k.before[:, :], in_=k.ones_bf[:, :], compare_op=ALU.is_gt, fill=0.0,
                                         base=0, pattern=[[1, P]], channel_multiplier=-1))
            pool.wait_ge(half_set, 1)
            for q in range(NC):
                ln_rstd(nc, pool, k, q, var_ready, rstd_ready)


def phase_qkv(nc, k, a, sem):
    ctx = ExitStack()
    with ctx:
        tp = [[ctx.enter_context(nc.psum_tensor(f"p1_tp{s}{t}", [P, QC], FP)) for t in range(KH)] for s in range(2)]
        pj = [ctx.enter_context(nc.psum_tensor(f"p1_pj{j}", [P, QC], FP)) for j in range(3)]
        pv = ctx.enter_context(nc.psum_tensor("p1_v", [P, TQ, HD], FP))
        wk = ctx.enter_context(nc.sbuf_tensor("wk_rep", [P, KH, P], FP))
        hT = ctx.enter_context(nc.sbuf_tensor("hT0", [P, KH, T], FP))
        parts = ctx.enter_context(nc.sbuf_tensor("q_parts", [P, 3, KH, T], BF))
        kparts = ctx.enter_context(nc.sbuf_tensor("k_parts", [P, 3, QC], BF))
        rest = ctx.enter_context(nc.sbuf_tensor("rest", [P, 2, QC], FP))
        ksum = ctx.enter_context(nc.sbuf_tensor("ksum", [P, 2, QC], BF))
        dve_step = sem("p1_dve_step")
        h_ready = sem("p1_h_ready")
        tp_done = sem("p1_tp_done")
        hT_ready = sem("p1_hT_ready")
        wk_ready = sem("p1_wk_ready")
        pj_done = sem("p1_pj_done")
        hi_done = sem("p1_hi_done")
        rest_done = sem("p1_rest_done")
        mid_done = sem("p1_mid_done")
        low_done = sem("p1_low_done")
        v_done = sem("p1_v_done")
        v_copied = sem("p1_v_copied")
        spilled = sem("p1_spilled")
        k_sum = sem("p1_k_sum")
        block = ctx.enter_context(nc.Block())

        def part_of(n, part):
            c, j = divmod(n, 3)
            return kparts[:, part, :] if j == 2 else parts[:, part, j, QC * c:QC * (c + 1)]

        @block.vector
        def _(dve):
            step = stepper(dve, dve_step)

            def remainder(n):
                dve.wait_ge(hi_done, n + 1)
                if n >= 2:
                    dve.wait_ge(low_done, n - 1)
                nc.vector.tensor_tensor(rest[:, n % 2, :], pj[n % 3][:, :], part_of(n, 0),
                                        ALU.subtract).then_inc(rest_done, 1)

            def low(n):
                dve.wait_ge(mid_done, n + 1)
                dve.wait_ge(rest_done, n + 1)
                nc.vector.tensor_tensor(part_of(n, 2), rest[:, n % 2, :], part_of(n, 1),
                                        ALU.subtract).then_inc(low_done, 1)
                if n % 3 == 2:
                    c = n // 3
                    dve.wait_ge(low_done, n + 1)
                    step(nc.vector.tensor_scalar(ksum[:, 0, :], kparts[:, 0, :], k.kpart[:, 0:1], k.kpart[:, 3:4],
                                                 ALU.mult, ALU.add))
                    step(nc.vector.scalar_tensor_tensor(ksum[:, 1, :], kparts[:, 1, :], k.kpart[:, 1:2],
                                                        ksum[:, 0, :], ALU.mult, ALU.add))
                    nc.vector.scalar_tensor_tensor(k.ks[:, QC * c:QC * (c + 1)], kparts[:, 2, :],
                                                   k.kpart[:, 2:3], ksum[:, 1, :], ALU.mult, ALU.add).then_inc(k_sum, 1)

            def copy_v(c):
                dve.wait_ge(v_done, c + 1)
                nc.vector.tensor_copy(k.vaug[:, TQ * c:TQ * (c + 1), 0:HD], pv[:, :, :]).then_inc(v_copied, 1)

            nc.vector.tensor_copy(wk[:, :, :].rearrange("p t (r d) -> p t r d", r=P // HD),
                                  k.wk1[:, :, :].unsqueeze(2).to_broadcast([P, KH, P // HD, HD])).then_inc(wk_ready, 1)
            for q in range(NC):
                ln_apply(nc, dve, step, k, q, k.mod[:, 0, CA, :], k.mod[:, 0, SA, :], None, h_ready)
                if q >= 1:
                    for n in range(3 * (q - 1), 3 * q):
                        remainder(n)
                        if n >= 1:
                            low(n - 1)
                    copy_v(q - 1)
            for n in range(3 * (NC - 1), 3 * NC):
                remainder(n)
                low(n - 1)
            low(3 * NC - 1)
            copy_v(NC - 1)

        @block.tensor
        def _(pe):
            pe.wait_ge(wk_ready, 1)

            def project(c):
                pe.wait_ge(hT_ready, 2 * c + 2)
                rhs = [hT[:, t, QC * c:QC * (c + 1)] for t in range(KH)]
                for j in range(3):
                    n = 3 * c + j
                    if n >= 3:
                        pe.wait_ge(rest_done, n - 2)
                    for t in range(KH):
                        w = wk[:, t, :] if j == 2 else k.wq[:, t, P * j:P * (j + 1)]
                        last = nc.tensor.matmul(pj[j][:, :], w, rhs[t], start=(t == 0), stop=(t == KH - 1))
                    last.then_inc(pj_done, 1)
                if c >= 1:
                    pe.wait_ge(v_copied, c)
                for i in range(TQ):
                    for t in range(KH):
                        last = nc.tensor.matmul(pv[:, i, :], hT[:, t, QC * c + P * i:QC * c + P * (i + 1)],
                                                k.wv[:, t, :], start=(t == 0), stop=(t == KH - 1))
                last.then_inc(v_done, 1)

            for q in range(NC):
                pe.wait_ge(h_ready, q + 1)
                if q >= 2:
                    pe.wait_ge(hT_ready, 2 * (q - 1))
                for last in transpose_quarter(nc, k, k.h, q, tp[q % 2]):
                    last.then_inc(tp_done, 1)
                if q >= 1:
                    project(q - 1)
            project(NC - 1)

        @block.scalar
        def _(act):
            def high(n):
                act.wait_ge(pj_done, n + 1)
                if n >= 3 and n % 3 == 2:
                    act.wait_ge(k_sum, n // 3)
                nc.scalar.copy(part_of(n, 0), pj[n % 3][:, :]).then_inc(hi_done, 1)

            def mid(n):
                act.wait_ge(rest_done, n + 1)
                nc.scalar.copy(part_of(n, 1), rest[:, n % 2, :]).then_inc(mid_done, 1)

            def parts_of_chunk(c):
                for n in range(3 * c, 3 * c + 3):
                    if n % 3 != 2:
                        high(n)
                        if n % 3 == 1:
                            mid(n - 1)
                    else:
                        mid(n - 1)
                        high(n)
                        mid(n)

            for q in range(NC):
                for half in range(KH):
                    act.wait_ge(tp_done, 2 * q + half + 1)
                    nc.scalar.copy(hT[:, half, QC * q:QC * (q + 1)], tp[q % 2][half][:, :]).then_inc(hT_ready, 1)
                if q >= 1:
                    parts_of_chunk(q - 1)
            parts_of_chunk(NC - 1)

        @block.sync
        def _(sp):
            for c in range(NC):
                s = slice(QC * c, QC * (c + 1))
                sp.wait_ge(low_done, 3 * c + 2)
                for part in range(3):
                    sp.dma_start(k.q_dram[part, :, s].rearrange("(t p) n -> p t n", p=P),
                                 parts[:, part, :, s]).then_inc(spilled, 16)
                sp.wait_ge(spilled, 16 * 3 * (c + 1))
                for row, part in enumerate((0, 0, 0, 1, 1, 2, 2)):
                    sp.dma_start(k.qs[HD * row:HD * (row + 1), c, :, :],
                                 k.q_dram[part, :, s].rearrange("(h d) n -> d h n", d=HD)).then_inc(k.q_in[c], 16)


def phase_attention(nc, k, a, sem):
    units = [(c, kt) for c in range(NC) for kt in range(TQ * (c + 1))]
    chunks = [(hs, qt, ck) for c in range(NC) for hs in range(GH) for qt in range(TQ * c, TQ * (c + 1))
              for ck in range(c + 1)]
    NU, NCH = len(units), len(chunks)
    PER_U = NCH // NU
    LEAD = NU // 2

    def ahead(g, u):
        G, v = (g, u + LEAD) if u + LEAD < NU else (g + 1, u + LEAD - NU)
        if type(G) is int and G == NG:
            return G, []
        return G, list(range(PER_U * v, PER_U * (v + 1)))
    NROWDMA = 8
    ctx = ExitStack()
    with ctx:
        sc = [ctx.enter_context(nc.psum_tensor(f"p2_s{s}", [P, 2, QC], FP)) for s in range(2)]
        p1 = [ctx.enter_context(nc.psum_tensor(f"p2_p1_{s}", [P, QC], FP)) for s in range(3)]
        ot = ctx.enter_context(nc.psum_tensor("p2_o", [P, QC], FP))
        prob = ctx.enter_context(nc.sbuf_tensor("prob", [P, 2, GH, QC], FP))
        mpart = ctx.enter_context(nc.sbuf_tensor("mpart", [P, GH, NT, NC], FP))
        mneg = ctx.enter_context(nc.sbuf_tensor("mneg", [P, GH, TQ], FP))
        m2 = ctx.enter_context(nc.sbuf_tensor("m2", [P, 2, GH, TQ], BF))
        m2t = ctx.enter_context(nc.sbuf_tensor("m2t", [P, NC, 32], BF))
        p1_done = sem("p2_p1_done")
        p1_used = sem("p2_p1_used")
        dve_step = sem("p2_dve_step")
        rows_ready = sem("p2_rows_ready")
        rows_in = [sem(f"p2_rows_in{c}") for c in range(NC)]
        s_done = sem("p2_s_done")
        e_done = sem("p2_e_done")
        pv_done = sem("p2_pv_done")
        ZW = 2560
        zeros = ctx.enter_context(nc.sbuf_tensor("zeros", [P, ZW], FP))
        zero_set = sem("p2_zero_set")
        zeroed = sem("p2_zeroed")
        o_copied = sem("p2_o_copied")
        block = ctx.enter_context(nc.Block())

        @block.tensor
        def _(pe):
            def first_pass(G, n):
                hs, qt, ck = chunks[n]
                diag = ck == qt // TQ
                w = (qt % TQ + 1) * P if diag else QC
                if n >= 3:
                    pe.wait_ge(p1_used, G * NCH + n - 2)
                elif not (type(G) is int and G == 0):
                    pe.wait_ge(p1_used, G * NCH)
                last = nc.tensor.matmul(p1[n % 3][:, 0:w], k.qs[0:KROWS, qt // TQ, GH * G + hs, P * (qt % TQ):P * (qt % TQ + 1)],
                                        k.ks[0:KROWS, QC * ck:QC * ck + w], start=True, stop=not diag)
                if diag:
                    last = nc.tensor.matmul(p1[n % 3][:, w - P:w], k.ident_bf[:, :], k.maskq[:, :],
                                            start=False, stop=True)
                last.then_inc(p1_done, 1)

            def scores(g, u, pair):
                c, kt = units[u]
                off = max(0, kt - TQ * c) * P
                pe.wait_ge(e_done, g * 2 * NU + 2 * u + pair + 1)
                for i in range(2):
                    last = nc.tensor.matmul(sc[pair][:, i, off:QC], k.ks[0:KALL, P * kt:P * (kt + 1)],
                                            k.qs[0:KALL, c, GH * g + 2 * pair + i, off:QC],
                                            start=True, stop=kt < TQ * c)
                    if kt >= TQ * c:
                        last = nc.tensor.matmul(sc[pair][:, i, off:off + P], k.maskq[:, :], k.ident_bf[:, :],
                                                start=False, stop=True)
                last.then_inc(s_done, 1)

            def values(g, u):
                c, kt = units[u]
                off = max(0, kt - TQ * c) * P
                pe.wait_ge(e_done, g * 2 * NU + 2 * u + 4)
                if kt == 0:
                    pe.wait_ge(o_copied, g * NC + c + 1)
                for j in range(GH):
                    last = nc.tensor.matmul(ot[32 * j:32 * (j + 1), off:QC], k.vaug[:, kt, :],
                                            prob[:, u % 2, j, off:QC], start=(kt == 0), stop=(kt == TQ * (c + 1) - 1),
                                            tile_position=(0, 32 * j))
                last.then_inc(pv_done, 1)

            def group(g):
                for u, (c, kt) in enumerate(units):
                    G, first = ahead(g, u)
                    if kt == 0:
                        pe.wait_ge(rows_in[c], g * 16 * NROWDMA + 16 * NROWDMA)
                    scores(g, u, 0)
                    for n in first[0:1]:
                        first_pass(G, n)
                    scores(g, u, 1)
                    for n in first[1:2]:
                        first_pass(G, n)
                    if u:
                        values(g, u - 1)
                    for n in first[2:]:
                        first_pass(G, n)
                values(g, NU - 1)

            for n in range(PER_U * LEAD):
                if n == 0 or chunks[n][1] // TQ != chunks[n - 1][1] // TQ:
                    pe.wait_ge(k.q_in[chunks[n][1] // TQ], 16 * PROD)
                first_pass(0, n)
            for c in range(NC):
                pe.wait_ge(k.q_in[c], 16 * PROD)
            with pe.Fori(0, NG - 1) as g:
                group(g)
            group(NG - 1)

        @block.scalar
        def _(act):
            act.sem_inc(e_done, 2)

            def group(g):
                for u, (c, kt) in enumerate(units):
                    off = max(0, kt - TQ * c) * P
                    act.wait_ge(pv_done, g * NU + u + 1)
                    for pair in range(2):
                        act.wait_ge(s_done, g * 2 * NU + 2 * u + pair + 1)
                        nc.scalar.activation(prob[:, u % 2, 2 * pair:2 * pair + 2, off:QC], sc[pair][:, :, off:QC],
                                             ACT.Exp, scale=HD ** -0.5).then_inc(e_done, 1)

            with act.Fori(0, NG - 1) as g:
                group(g)
            group(NG - 1)

        @block.vector
        def _(dve):
            dve.sem_inc(pv_done, 2)
            dve.sem_inc(o_copied, 1)
            dve.wait_ge(pv_done, 2)
            STEPS = 3
            nc.vector.memset(mpart[:, :, :, :], NEG).then_inc(dve_step, 1)
            dve.wait_ge(dve_step, 1)

            def maxima(G, n):
                hs, qt, ck = chunks[n]
                c = qt // TQ
                w = (qt % TQ + 1) * P if ck == c else QC
                dve.wait_ge(p1_done, G * NCH + n + 1)
                nc.vector.reduce_max(mpart[:, hs, qt, ck:ck + 1], p1[n % 3][:, 0:w], AX.X).then_inc(p1_used, 1)
                if (hs, qt % TQ, ck) == (GH - 1, TQ - 1, c):
                    base = G * (STEPS * NC) + STEPS * c + 1
                    dve.wait_ge(p1_used, G * NCH + n + 1)
                    nc.vector.tensor_reduce(mneg[:, :, :], mpart[:, :, TQ * c:TQ * (c + 1), :], axis=AX.X, op=ALU.max,
                                            negate=True).then_inc(dve_step, 1)
                    dve.wait_ge(dve_step, base + 1)
                    nc.vector.tensor_copy(m2[:, 0, :, :], mneg[:, :, :]).then_inc(dve_step, 1)
                    dve.wait_ge(dve_step, base + 2)
                    nc.vector.tensor_tensor(m2[:, 1, :, :], mneg[:, :, :], m2[:, 0, :, :],
                                            ALU.subtract).then_inc(dve_step, 1)
                    dve.wait_ge(dve_step, base + 3)
                    nc.vector.transpose(m2t[:, c, :], m2[:, :, :, :].rearrange("p s h t -> p (s h t)")).then_inc(rows_ready, 1)

            def copy_out(g, c):
                dve.wait_ge(pv_done, g * NU + sum(TQ * (x + 1) for x in range(c + 1)) + 2)
                nc.vector.tensor_copy(k.oT[:, g, QC * c:QC * (c + 1)], ot[:, :]).then_inc(o_copied, 1)

            def group(g):
                for u, (c, kt) in enumerate(units):
                    G, first = ahead(g, u)
                    for n in first:
                        maxima(G, n)
                    if kt == 0 and c:
                        copy_out(g, c - 1)
                copy_out(g, NC - 1)

            for n in range(PER_U * LEAD):
                maxima(0, n)
            with dve.Fori(0, NG - 1) as g:
                group(g)
            group(NG - 1)

        @block.sync
        def _(sp):
            sp.wait_ge(zero_set, 1)
            for table, rows_n in ((k.disp[0], E * CAP), (k.disp[1], NB * BLK)):
                flat = table[0:rows_n, :].rearrange("(p r) d -> p (r d)", p=P)
                per = rows_n // P * D
                for c0 in range(0, per, ZW):
                    w = min(ZW, per - c0)
                    sp.dma_start(flat[:, c0:c0 + w], zeros[:, 0:w]).then_inc(zeroed, 16)
            zeroing = sum(-(-(n // P * D) // ZW) for n in (E * CAP, NB * BLK))

            def rows(G, c):
                sp.wait_ge(rows_ready, G * NC + c + 1)
                for b in range(4):
                    for part in range(2):
                        dst = k.qs[BROW + part:BROW + part + 1, c, bass.ds(GH * G, GH), :]\
                            .rearrange("o h (t b r) -> o (h t) b r", b=4, r=32)[:, :, b, :]
                        src = m2t[32 * b + NT * part:32 * b + NT * (part + 1), c, :]
                        sp.dma_start(dst, src).then_inc(rows_in[c], 16)

            with sp.Fori(0, NG) as G:
                for c in range(NC):
                    rows(G, c)
            for c in range(NC):
                sp.wait_ge(rows_in[c], 16 * NROWDMA * NG)
            sp.wait_ge(zeroed, 16 * zeroing)

        @block.gpsimd
        def _(pool):
            nc.gpsimd.memset(zeros[:, :], 0.0).then_inc(zero_set, 1)
            gabo = k.bo
            done = sem("p2_pool_done")
            nc.gpsimd.tensor_tensor(gabo[:, :], k.bo[:, :], k.mod[:, 0, GA, :], ALU.mult).then_inc(done, 1)
            pool.wait_ge(done, 1)
            for q in range(NC):
                nc.gpsimd.tensor_tensor(quarter(k.x, q), quarter(k.x, q), bcast(gabo[:, :], TQ), ALU.add).then_inc(done, 1)
            pool.wait_ge(done, 1 + NC)


def phase_project(nc, k, a, sem):
    ctx = ExitStack()
    with ctx:
        pa = [ctx.enter_context(nc.psum_tensor(f"p3_a{s}", [P, NG * P], FP)) for s in range(2)]
        pb = [ctx.enter_context(nc.psum_tensor(f"p3_b{s}", [P, KH, P], FP)) for s in range(2)]
        pc = [ctx.enter_context(nc.psum_tensor(f"p3_c{s}", [P, D], FP)) for s in range(2)]
        inv = ctx.enter_context(nc.sbuf_tensor("inv_sum", [P, 2, H], FP))
        on = ctx.enter_context(nc.sbuf_tensor("o_norm", [P, 2, D], FP))
        onT = ctx.enter_context(nc.sbuf_tensor("o_normT", [P, 2, KH, P], FP))
        gated = ctx.enter_context(nc.sbuf_tensor("gated", [P, 2, D], FP))
        a_done = sem("p3_a_done")
        inv_done = sem("p3_inv_done")
        on_ready = sem("p3_on_ready")
        b_done = sem("p3_b_done")
        onT_ready = sem("p3_onT_ready")
        c_done = sem("p3_c_done")
        gated_ready = sem("p3_gated_ready")
        x_ready = sem("p3_x_ready")
        block = ctx.enter_context(nc.Block())

        @block.tensor
        def _(pe):
            for i in range(NT + 2):
                if i < NT:
                    if i >= 2:
                        pe.wait_ge(on_ready, i - 1)
                    for g in range(NG):
                        last = nc.tensor.transpose(pa[i % 2][:, P * g:P * (g + 1)], k.oT[:, g, P * i:P * (i + 1)],
                                                   k.ident[:, :])
                    last.then_inc(a_done, 1)
                if 1 <= i <= NT:
                    n = i - 1
                    pe.wait_ge(on_ready, n + 1)
                    if n >= 2:
                        pe.wait_ge(onT_ready, n - 1)
                    for t in range(KH):
                        last = nc.tensor.transpose(pb[n % 2][:, t, :], on[:, n % 2, P * t:P * (t + 1)], k.ident[:, :])
                    last.then_inc(b_done, 1)
                if i >= 2:
                    n = i - 2
                    pe.wait_ge(onT_ready, n + 1)
                    if n >= 2:
                        pe.wait_ge(gated_ready, n - 1)
                    for t in range(KH):
                        last = nc.tensor.matmul(pc[n % 2][:, :], onT[:, n % 2, t, :], k.wo[:, t, :],
                                                start=(t == 0), stop=(t == KH - 1))
                    last.then_inc(c_done, 1)

        @block.vector
        def _(dve):
            for i in range(NT + 2):
                if i < NT:
                    dve.wait_ge(a_done, i + 1)
                    if i >= 2:
                        dve.wait_ge(b_done, i - 1)
                    heads = pa[i % 2][:, :].rearrange("p (h d) -> p h d", d=32)
                    nc.vector.reciprocal(inv[:, i % 2, :], heads[:, :, HD]).then_inc(inv_done, 1)
                    dve.wait_ge(inv_done, i + 1)
                    nc.vector.tensor_tensor(on[:, i % 2, :].rearrange("p (h d) -> p h d", d=HD), heads[:, :, 0:HD],
                                            last_bcast(inv[:, i % 2, :], HD), ALU.mult).then_inc(on_ready, 1)
                if i >= 2:
                    n = i - 2
                    dve.wait_ge(c_done, n + 1)
                    if n >= 2:
                        dve.wait_ge(x_ready, n - 1)
                    nc.vector.tensor_tensor(gated[:, n % 2, :], pc[n % 2][:, :], k.mod[:, 0, GA, :],
                                            ALU.mult).then_inc(gated_ready, 1)

        @block.scalar
        def _(act):
            for i in range(NT):
                act.wait_ge(b_done, i + 1)
                if i >= 2:
                    act.wait_ge(c_done, i - 1)
                nc.scalar.copy(onT[:, i % 2, :, :], pb[i % 2][:, :, :]).then_inc(onT_ready, 1)

        @block.gpsimd
        def _(pool):
            for i in range(NT):
                pool.wait_ge(gated_ready, i + 1)
                nc.gpsimd.tensor_tensor(k.x[:, i, :], k.x[:, i, :], gated[:, i % 2, :], ALU.add).then_inc(x_ready, 1)


def load_weights0(sp, k, a, e, s):
    sp.dma_start(k.wi[:, s, :, :], a.L0_ffn_wi[e, :, :].rearrange("(t p) n -> p t n", p=P)).then_inc(k.w_in0[s], 16)
    sp.dma_start(k.wo_e[:, s, :, :], a.L0_ffn_wo[e, :, :].rearrange("(t p) n -> p t n", p=P)).then_inc(k.w_in0[s], 16)


def phase_router(nc, k, a, sem, layer, gate_w):
    ctx = ExitStack()
    L = f"r{layer}_"
    with ctx:
        def sb(name, shape, dt=FP):
            return ctx.enter_context(nc.sbuf_tensor(L + name, shape, dt))

        tp = [[ctx.enter_context(nc.psum_tensor(f"{L}tp{s}{t}", [P, QC], FP)) for t in range(KH)] for s in range(2)]
        plog = ctx.enter_context(nc.psum_tensor(L + "plog", [P, NT, E], FP))
        prank = ctx.enter_context(nc.psum_tensor(L + "prank", [P, NT, E], FP))
        ptot = ctx.enter_context(nc.psum_tensor(L + "ptot", [P, NT, E], FP))
        gT = sb("gT", [P, KH, E])
        hT = sb("hT", [P, 2, KH, QC])
        logits = sb("logits", [P, NT, E])
        top = sb("top", [P, NT, 8])
        top_i = sb("top_i", [P, NT, 8], U32)
        top_f = sb("top_f", [P, NT, 2])
        iota_e = sb("iota_e", [P, E])
        iota_b = sb("iota_b", [P, NB])
        tok = sb("tok", [P, NT])
        cont = sb("cont", [P, E, NT])
        one_hot = [sb(f"one_hot{j}", [P, NT, E]) for j in range(2)]
        chosen = sb("chosen", [P, NT, E])
        chosen_bf = sb("chosen_bf", [P, NT, E], BF)
        ex = [sb(f"ex{j}", [P, NT, E]) for j in range(2)]
        tmp = [sb(f"tmp{j}", [P, NT, E]) for j in range(4)]
        tot = sb("tot", [P, E, NT])
        run = sb("run", [P, E, NT])
        rank = sb("rank", [P, NT, E])
        small = [sb(f"small{j}", [P, NT]) for j in range(4)]
        cnt_i = sb("cnt_i", [P, E], mybir.dt.int32)
        blk = [sb(f"blk{j}", [P, E]) for j in range(3)]
        cmp_b = sb("cmp_b", [P, NB, E])
        blk_e = sb("blk_e", [P, NB])
        scat = sb("scat", [P, 2, NT], U32)
        if layer == 1:
            raw = sb("raw", [P, 2, 3, 1024])
            raw_in = [sem(f"{L}raw_in{s}") for s in range(2)]
            w_done = sem(L + "w_done")
            w_copied = sem(L + "w_copied")
        dve_step = sem(L + "dve_step")
        var_ready = sem(L + "var_ready")
        rstd_ready = sem(L + "rstd_ready")
        h_ready = sem(L + "h_ready")
        gate_in = sem(L + "gate_in")
        tp_done = sem(L + "tp_done")
        hT_ready = sem(L + "hT_ready")
        log_done = sem(L + "log_done")
        delta_ready = sem(L + "delta_ready")
        exp_done = sem(L + "exp_done")
        chosen_ready = sem(L + "chosen_ready")
        rank_done = sem(L + "rank_done")
        iota_ready = sem(L + "iota_ready")
        slots_ready = sem(L + "slots_ready")
        sent = sem(L + "sent")
        block = ctx.enter_context(nc.Block())
        KSEL = layer + 1

        @block.sync
        def _(sp):
            with nc.allow_non_contiguous_dma(reason="2048 numbers, off the critical path"):
                for t in range(KH):
                    sp.dma_start(gT[:, t, :], gate_w[:, P * t:P * (t + 1)].rearrange("e p -> p e")).then_inc(gate_in, 16)
            if layer == 0:
                for e in range(2):
                    load_weights0(sp, k, a, e, e)
            else:
                for e in range(E):
                    s = e % 2
                    if e >= 2:
                        sp.wait_ge(w_copied, 6 * (e - 1))
                    for m, w in enumerate((a.L1_ffn_w1, a.L1_ffn_w3)):
                        sp.dma_start(raw[:, s, m, :].rearrange("p (f d) -> p f d", f=F1 // P),
                                     w[e, :, :].rearrange("(f p) d -> p f d", p=P)).then_inc(raw_in[s], 16)
                    sp.dma_start(raw[:, s, 2, :].rearrange("p (t f) -> p t f", t=KH),
                                 a.L1_ffn_w2[e, :, :].rearrange("(t p) f -> p t f", p=P)).then_inc(raw_in[s], 16)
            sp.wait_ge(gate_in, 16 * KH)

        @block.tensor
        def _(pe):
            def turn_weights(e):
                s = e % 2
                pe.wait_ge(raw_in[s], 48 * (e // 2 + 1))
                for m in range(3):
                    n = 3 * e + m
                    if n >= 2:
                        pe.wait_ge(w_copied, 2 * (n - 1))
                    for half in range(2):
                        for j in range(4):
                            if m < 2:
                                src = raw[:, s, m, D * j + P * half:D * j + P * (half + 1)]
                            else:
                                f0 = F1 * (j % 2) + P * (2 * half + j // 2)
                                src = raw[:, s, 2, f0:f0 + P]
                            last = nc.tensor.transpose(tp[n % 2][half][:, P * j:P * (j + 1)], src, k.ident[:, :])
                    last.then_inc(w_done, 1)

            def logit(q):
                pe.wait_ge(hT_ready, 2 * q + 2)
                for i in range(TQ):
                    for t in range(KH):
                        last = nc.tensor.matmul(plog[:, TQ * q + i, :], hT[:, q % 2, t, P * i:P * (i + 1)],
                                                gT[:, t, :], start=(t == 0), stop=(t == KH - 1))
                last.then_inc(log_done, 1)

            pe.wait_ge(gate_in, 16 * KH)
            for q in range(NC):
                pe.wait_ge(h_ready, q + 1)
                if q >= 2:
                    pe.wait_ge(hT_ready, 2 * (q - 1))
                for last in transpose_quarter(nc, k, k.h, q, tp[q % 2]):
                    last.then_inc(tp_done, 1)
                if q >= 1:
                    logit(q - 1)
            logit(NC - 1)
            if layer == 1:
                pe.wait_ge(hT_ready, 2 * NC)
                for e in range(2):
                    turn_weights(e)
            pe.wait_ge(chosen_ready, 1)
            rhs = chosen_bf[:, :, :].rearrange("p i e -> p (i e)")
            nc.tensor.matmul(prank[:, :, :].rearrange("p i e -> p (i e)"), k.before[:, :], rhs, start=True, stop=True)
            nc.tensor.matmul(ptot[:, :, :].rearrange("p i e -> p (i e)"), k.ones_bf[:, :], rhs,
                             start=True, stop=True).then_inc(rank_done, 1)
            if layer == 1:
                for e in range(2, E):
                    turn_weights(e)

        @block.scalar
        def _(act):
            for q in range(NC):
                if q >= 2:
                    act.wait_ge(log_done, q - 1)
                for half in range(KH):
                    act.wait_ge(tp_done, 2 * q + half + 1)
                    nc.scalar.copy(hT[:, q % 2, half, :], tp[q % 2][half][:, :]).then_inc(hT_ready, 1)

            def copy_weights(e):
                for m in range(3):
                    act.wait_ge(w_done, 3 * e + m + 1)
                    for half in range(2):
                        nc.scalar.copy(k.w1T[:, e, m, 512 * half:512 * (half + 1)],
                                       tp[(3 * e + m) % 2][half][:, :]).then_inc(w_copied, 1)

            if layer == 1:
                for e in range(2):
                    copy_weights(e)
            for j in range(KSEL):
                act.wait_ge(delta_ready, j + 1)
                nc.scalar.activation(ex[j][:, :, :], tmp[j][:, :, :], ACT.Exp).then_inc(exp_done, 1)
            if layer == 1:
                for e in range(2, E):
                    copy_weights(e)

        @block.vector
        def _(dve):
            step = stepper(dve, dve_step)
            tt, ts = nc.vector.tensor_tensor, nc.vector.tensor_scalar
            nc.vector.memset(cont[:, :, :], 1.0)
            step(nc.vector.memset(one_hot[1][:, :, :], 0.0))
            step(nc.vector.memset(cont[:, :, 0], 0.0))
            ln_stats(nc, dve, step, k, 0, var_ready)
            for q in range(NC):
                if q + 1 < NC:
                    ln_stats(nc, dve, step, k, q + 1, var_ready)
                ln_apply(nc, dve, step, k, q, k.mod[:, layer, CB, :], k.mod[:, layer, SB, :], rstd_ready, h_ready)
            dve.wait_ge(log_done, NC)
            dve.wait_ge(iota_ready, 3)
            step(nc.vector.tensor_copy(logits[:, :, :], plog[:, :, :]))
            for i in range(NT):
                last = nc.vector.max(top[:, i, :], logits[:, i, :])
            step(last)
            for i in range(NT):
                last = nc.vector.max_index(top_i[:, i, :], top[:, i, :], logits[:, i, :])
            step(last)
            step(nc.vector.tensor_copy(top_f[:, :, :], top_i[:, :, 0:2]))
            for j in range(KSEL):
                step(tt(one_hot[j][:, :, :], bcast(iota_e[:, :], NT), last_bcast(top_f[:, :, j], E), ALU.is_equal))
            if layer == 0:
                chosen_t = one_hot[0]
            else:
                chosen_t = chosen
                step(tt(chosen[:, :, :], one_hot[0][:, :, :], one_hot[1][:, :, :], ALU.add))
            nc.vector.tensor_copy(chosen_bf[:, :, :], chosen_t[:, :, :]).then_inc(chosen_ready, 1)
            for j in range(KSEL):
                step(tt(tmp[j][:, :, :], logits[:, :, :], last_bcast(top[:, :, j], E), ALU.subtract))
                nc.vector.tensor_scalar_min(tmp[j][:, :, :], tmp[j][:, :, :], 0.0).then_inc(delta_ready, 1)
            dve.wait_ge(rank_done, 1)
            step(nc.vector.tensor_copy(tot[:, :, :], ptot[:, :, :].rearrange("p i e -> p e i")))
            flat = "p e i -> p (e i)"
            step(nc.vector.tensor_tensor_scan(run[:, :, :].rearrange(flat), cont[:, :, :].rearrange(flat),
                                              tot[:, :, :].rearrange(flat), 0.0, ALU.mult, ALU.add))
            step(tt(tot[:, :, :], run[:, :, :], tot[:, :, :], ALU.subtract))
            step(tt(rank[:, :, :], tot[:, :, :].rearrange("p e i -> p i e"), prank[:, :, :], ALU.add))
            if layer == 0:
                step(ts(tmp[1][:, :, :], rank[:, :, :], float(CAP), None, ALU.is_lt))
                step(tt(tmp[1][:, :, :], tmp[1][:, :, :], one_hot[0][:, :, :], ALU.mult))
                kept = small[0]
                step(nc.vector.reduce_sum(kept[:, :], tmp[1][:, :, :], AX.X))
                step(ts(blk[0][:, :], iota_e[:, :], float(CAP), None, ALU.mult))
                step(tt(tmp[2][:, :, :], rank[:, :, :], bcast(blk[0][:, :], NT), ALU.add))
                step(tt(tmp[2][:, :, :], tmp[2][:, :, :], one_hot[0][:, :, :], ALU.mult))
                step(nc.vector.reduce_sum(small[1][:, :], tmp[2][:, :, :], AX.X))
                step(ts(small[2][:, :], tok[:, :], float(E * CAP), None, ALU.add))
                step(tt(small[3][:, :], small[1][:, :], small[2][:, :], ALU.subtract))
                step(tt(small[3][:, :], small[3][:, :], kept[:, :], ALU.mult))
                step(tt(small[3][:, :], small[3][:, :], small[2][:, :], ALU.add))
                nc.vector.tensor_copy(scat[:, 0, :], small[3][:, :]).then_inc(slots_ready, 1)
                step(tt(small[1][:, :], small[1][:, :], kept[:, :], ALU.mult))
                step(nc.vector.tensor_copy(k.slot[:, 0, :], small[1][:, :]))
                dve.wait_ge(exp_done, 1)
                step(nc.vector.reduce_sum(small[2][:, :], ex[0][:, :, :], AX.X))
                step(nc.vector.reciprocal(small[2][:, :], small[2][:, :]))
                step(tt(k.weight[:, 0, :], small[2][:, :], kept[:, :], ALU.mult))
            else:
                step(ts(blk[0][:, :], run[:, :, NT - 1], float(BLK - 1), None, ALU.add))
                step(nc.vector.tensor_copy(cnt_i[:, :], blk[0][:, :]))
                step(ts(cnt_i[:, :], cnt_i[:, :], 7, None, ALU.arith_shift_right))
                step(nc.vector.tensor_copy(blk[0][:, :], cnt_i[:, :]))
                step(nc.vector.tensor_tensor_scan(blk[1][:, :], cont[:, 0:1, 1:E + 1].rearrange(flat), blk[0][:, :], 0.0,
                                                  ALU.mult, ALU.add))
                step(tt(blk[2][:, :], blk[1][:, :], blk[0][:, :], ALU.subtract))
                step(ts(blk[2][:, :], blk[2][:, :], float(BLK), None, ALU.mult))
                step(tt(rank[:, :, :], rank[:, :, :], bcast(blk[2][:, :], NT), ALU.add))
                for j in range(2):
                    step(tt(tmp[2][:, :, :], rank[:, :, :], one_hot[j][:, :, :], ALU.mult))
                    step(nc.vector.reduce_sum(small[j][:, :], tmp[2][:, :, :], AX.X))
                    step(nc.vector.tensor_copy(k.slot[:, j, :], small[j][:, :]))
                    nc.vector.tensor_copy(scat[:, j, :], small[j][:, :]).then_inc(slots_ready, 1)
                step(tt(cmp_b[:, :, :], bcast(blk[1][:, :], NB), last_bcast(iota_b[:, :], E), ALU.is_le))
                step(nc.vector.reduce_sum(blk_e[:, :], cmp_b[:, :, :], AX.X))
                step(nc.vector.tensor_scalar_min(blk_e[:, :], blk_e[:, :], float(E - 1)))
                step(nc.vector.tensor_copy(k.block_expert[:, :], blk_e[:, :]))
                step(nc.vector.scalar_tensor_tensor(tmp[3][:, :, :], logits[:, :, :], -1.0, logits[:, :, :],
                                                    ALU.mult, ALU.max))
                for j in range(2):
                    thr = last_bcast(top[:, :, j], E)
                    step(tt(tmp[2][:, :, :], tmp[3][:, :, :], thr, ALU.max))
                    step(ts(tmp[2][:, :, :], tmp[2][:, :, :], 0.02, None, ALU.mult))
                    dve.wait_ge(exp_done, j + 1)
                    step(tt(tmp[j][:, :, :], thr, logits[:, :, :], ALU.subtract))
                    step(tt(tmp[2][:, :, :], tmp[j][:, :, :], tmp[2][:, :, :], ALU.is_le))
                    step(tt(ex[j][:, :, :], ex[j][:, :, :], tmp[2][:, :, :], ALU.mult))
                    if j == 1:
                        step(ts(tmp[2][:, :, :], one_hot[0][:, :, :], -1.0, 1.0, ALU.mult, ALU.add))
                        step(tt(ex[j][:, :, :], ex[j][:, :, :], tmp[2][:, :, :], ALU.mult))
                    step(nc.vector.reduce_sum(small[2][:, :], ex[j][:, :, :], AX.X))
                    step(nc.vector.reciprocal(k.weight[:, j, :], small[2][:, :]))

        @block.gpsimd
        def _(pool):
            nc.gpsimd.iota(iota_e[:, :], pattern=[[1, E]], base=0, channel_multiplier=0,
                           allow_small_or_imprecise_dtypes=True).then_inc(iota_ready, 1)
            nc.gpsimd.iota(iota_b[:, :], pattern=[[1, NB]], base=0, channel_multiplier=0,
                           allow_small_or_imprecise_dtypes=True).then_inc(iota_ready, 1)
            nc.gpsimd.iota(tok[:, :], pattern=[[P, NT]], base=0, channel_multiplier=1,
                           allow_small_or_imprecise_dtypes=True).then_inc(iota_ready, 1)
            for q in range(NC):
                ln_rstd(nc, pool, k, q, var_ready, rstd_ready)
            pool.wait_ge(h_ready, NC)
            for j in range(KSEL):
                pool.wait_ge(slots_ready, j + 1)
                for i in range(NT):
                    nc.gpsimd.indirect_dma_start(
                        out=k.disp[layer], out_offset=bass.IndirectOffsetOnAxis(ap=scat[:, j, i:i + 1], axis=0),
                        in_=k.h[:, i, :], in_offset=None).then_inc(sent, 16)
            pool.wait_ge(sent, 16 * NT * KSEL)


def phase_experts0(nc, k, a, sem):
    NI = F0 // P
    RT = [(0, P), (P, P), (2 * P, CAP - 2 * P)]
    ctx = ExitStack()
    with ctx:
        pt = [ctx.enter_context(nc.psum_tensor(f"p5_t{t}", [P, CAP], FP)) for t in range(KH)]
        ph = [ctx.enter_context(nc.psum_tensor(f"p5_h{s}", [P, CAP], FP)) for s in range(2)]
        po = [ctx.enter_context(nc.psum_tensor(f"p5_o{s}", [P, D], FP)) for s in range(2)]
        wi, wo = k.wi, k.wo_e
        rows = ctx.enter_context(nc.sbuf_tensor("rows0", [P, 2, 3, D], FP))
        rowsT = ctx.enter_context(nc.sbuf_tensor("rowsT0", [P, 2, KH, CAP], FP))
        mid = ctx.enter_context(nc.sbuf_tensor("mid0", [P, NI, CAP], FP))
        outr = ctx.enter_context(nc.sbuf_tensor("outr0", [P, 2, 3, D], FP))
        slot_in = [sem(f"p5_slot_in{s}") for s in range(2)]
        slot_free = sem("p5_slot_free")
        t_done = sem("p5_t_done")
        rowsT_ready = sem("p5_rowsT_ready")
        h_done = sem("p5_h_done")
        gelu_done = sem("p5_gelu_done")
        o_done = sem("p5_o_done")
        o_copied = sem("p5_o_copied")
        stored = [sem(f"p5_stored{s}") for s in range(2)]
        block = ctx.enter_context(nc.Block())
        LOADS = 2
        STORES = 3
        src = k.disp[0][0:E * CAP, :].rearrange("(e r) d -> e r d", r=CAP)
        dst = k.eout[0][0:E * CAP, :].rearrange("(e r) d -> e r d", r=CAP)

        @block.sync
        def _(sp):
            def load_rows(e, s):
                sp.dma_start(rows[:, s, 0:2, :], src[e, 0:2 * P, :].rearrange("(r p) d -> p r d", p=P)).then_inc(slot_in[s], 16)
                sp.dma_start(rows[0:RT[2][1], s, 2, :], src[e, 2 * P:CAP, :]).then_inc(slot_in[s], 16)

            for s in range(2):
                load_rows(s, s)
            with sp.Fori(1, E // 2) as i:
                for s in range(2):
                    e = 2 * i + s
                    sp.wait_ge(slot_free, e - 1)
                    load_rows(e, s)
                    load_weights0(sp, k, a, e, s)

        @block.tensor
        def _(pe):
            def transposes(i, s):
                e = 2 * i + s
                pe.wait_ge(slot_in[s], i * 16 * LOADS + 16 * LOADS)
                if not (type(e) is int and e == 0):
                    pe.wait_ge(rowsT_ready, e)
                for t in range(KH):
                    for r, (r0, rn) in enumerate(RT):
                        last = nc.tensor.transpose(pt[t][:, r0:r0 + rn], rows[0:rn, s, r, P * t:P * (t + 1)],
                                                   k.ident[0:rn, 0:rn])
                last.then_inc(t_done, 1)

            def expert(i, s, more):
                e = 2 * i + s
                pe.wait_ge(rowsT_ready, e + 1)
                pe.wait_ge(k.w_in0[s], i * 16 * LOADS + 16 * LOADS)
                for n in range(NI):
                    pe.wait_ge(gelu_done, e * NI + n + 1)
                    for t in range(KH):
                        last = nc.tensor.matmul(ph[n % 2][:, :], wi[:, s, t, P * n:P * (n + 1)], rowsT[:, s, t, :],
                                                start=(t == 0), stop=(t == KH - 1))
                    last.then_inc(h_done, 1)
                if more:
                    transposes(i + s, 1 - s)
                pe.wait_ge(gelu_done, e * NI + NI + 2)
                for r, (r0, rn) in enumerate(RT):
                    b = (3 * s + r) % 2
                    pe.wait_ge(o_copied, e * 3 + r + 1)
                    for n in range(NI):
                        if rn == P:
                            last = nc.tensor.matmul(po[b][:, :], mid[:, n, r0:r0 + rn], wo[:, s, n, :],
                                                    start=(n == 0), stop=(n == NI - 1))
                        else:
                            for t in range(KH):
                                last = nc.tensor.matmul(po[b][rn * t:rn * (t + 1), 0:P], mid[:, n, r0:r0 + rn],
                                                        wo[:, s, n, P * t:P * (t + 1)], start=(n == 0),
                                                        stop=(n == NI - 1), tile_position=(0, rn * t))
                    last.then_inc(o_done, 1)
                pe.drain().then_inc(slot_free, 1)

            transposes(0, 0)
            with pe.Fori(0, E // 2 - 1) as i:
                expert(i, 0, True)
                expert(i, 1, True)
            expert(E // 2 - 1, 0, True)
            expert(E // 2 - 1, 1, False)

        @block.scalar
        def _(act):
            act.sem_inc(gelu_done, 2)
            with act.Fori(0, E // 2) as i:
                for s in range(2):
                    e = 2 * i + s
                    act.wait_ge(t_done, e + 1)
                    nc.scalar.copy(rowsT[:, s, 0, :], pt[0][:, :])
                    nc.scalar.copy(rowsT[:, s, 1, :], pt[1][:, :]).then_inc(rowsT_ready, 1)
                    for n in range(NI):
                        act.wait_ge(h_done, e * NI + n + 1)
                        nc.scalar.activation(mid[:, n, :], ph[n % 2][:, :], ACT.Gelu).then_inc(gelu_done, 1)

        @block.vector
        def _(dve):
            dve.sem_inc(o_copied, 2)

            def pair(i, first):
                for s in range(2):
                    e = 2 * i + s
                    if not first:
                        dve.wait_ge(stored[s], i * 16 * STORES)
                    for r, (r0, rn) in enumerate(RT):
                        dve.wait_ge(o_done, e * 3 + r + 1)
                        w = D if rn == P else P
                        nc.vector.tensor_copy(outr[:, s, r, 0:w], po[(3 * s + r) % 2][:, 0:w]).then_inc(o_copied, 1)

            pair(0, True)
            with dve.Fori(1, E // 2) as i:
                pair(i, False)

        @block.gpsimd
        def _(pool):
            with pool.Fori(0, E // 2) as i:
                for s in range(2):
                    e = 2 * i + s
                    pool.wait_ge(o_copied, e * 3 + 3 + 2)
                    pool.dma_start(dst[e, 0:2 * P, :].rearrange("(r p) d -> p r d", p=P), outr[:, s, 0:2, :]).then_inc(stored[s], 16)
                    for t in range(KH):
                        rn = RT[2][1]
                        pool.dma_start(dst[e, 2 * P:CAP, P * t:P * (t + 1)],
                                       outr[rn * t:rn * (t + 1), s, 2, 0:P]).then_inc(stored[s], 16)
            for s in range(2):
                pool.wait_ge(stored[s], 16 * STORES * (E // 2))


def phase_combine(nc, k, a, sem, layer, out):
    KSEL = layer + 1
    L = f"c{layer}_"
    with nc.sbuf_tensor(L + "got", [P, 2, NT, D], FP) as got, nc.sbuf_tensor(L + "sum", [P, 2, D], FP) as acc, \
            nc.Block() as block:
        got_in = [sem(f"{L}got_in{q}") for q in range(NC)]
        dve_step = sem(L + "dve_step")
        x_ready = sem(L + "x_ready")
        if layer == 1:
            written = sem(L + "written")

        @block.gpsimd
        def _(pool):
            for i in range(NT):
                for j in range(KSEL):
                    nc.gpsimd.indirect_dma_start(
                        out=got[:, j, i, :], out_offset=None, in_=k.eout[layer],
                        in_offset=bass.IndirectOffsetOnAxis(ap=k.slot[:, j, i:i + 1], axis=0)).then_inc(got_in[i // TQ], 16)

        @block.vector
        def _(dve):
            step = stepper(dve, dve_step)
            for i in range(NT):
                dve.wait_ge(got_in[i // TQ], 16 * KSEL * TQ)
                gate = k.mod[:, layer, GB, :]
                if layer == 0:
                    step(nc.vector.scalar_tensor_tensor(acc[:, 0, :], got[:, 0, i, :], k.weight[:, 0, i:i + 1], gate,
                                                        ALU.mult, ALU.mult))
                else:
                    step(nc.vector.tensor_scalar(acc[:, 1, :], got[:, 0, i, :], k.weight[:, 0, i:i + 1], None, ALU.mult))
                    step(nc.vector.scalar_tensor_tensor(acc[:, 0, :], got[:, 1, i, :], k.weight[:, 1, i:i + 1],
                                                        acc[:, 1, :], ALU.mult, ALU.add))
                    step(nc.vector.tensor_tensor(acc[:, 0, :], acc[:, 0, :], gate, ALU.mult))
                nc.vector.tensor_tensor(k.x[:, i, :], k.x[:, i, :], acc[:, 0, :], ALU.add).then_inc(x_ready, 1)
                dve.wait_ge(x_ready, i + 1)

        if layer == 1:
            @block.sync
            def _(sp):
                ov = out[0, :, :].rearrange("(i p) d -> p i d", p=P)
                for q in range(NC):
                    sp.wait_ge(x_ready, TQ * (q + 1))
                    sp.dma_start(ov[:, TQ * q:TQ * (q + 1), :], quarter(k.x, q)).then_inc(written, 16)
                sp.wait_ge(written, 16 * NC)


def phase_mix(nc, k, a, sem):
    ctx = ExitStack()
    with ctx:
        def sb(name, shape, dt=FP):
            return ctx.enter_context(nc.sbuf_tensor("m_" + name, shape, dt))

        def ps(name, shape):
            return ctx.enter_context(nc.psum_tensor("m_" + name, shape, FP))

        tp = [[ps(f"tp{s}{t}", [P, QC]) for t in range(KH)] for s in range(1)][0]
        pkv = [ps(f"kv{s}", [P, 2 * D]) for s in range(2)]
        pA = [ps(f"A{t}", [P, 1]) for t in range(KH)]
        pw = [ps(f"w{s}", [P, 2 * D]) for s in range(2)]
        xn = sb("xn", [P, NT, D])
        xnT = sb("xnT", [P, KH, T])
        w_in = sb("w_in", [P, KH, 3 * D])
        w_out = sb("w_out", [P, KH, D])
        wqT = sb("wqT", [P, KH, D])
        w_sc = sb("w_sc", [P, KH, D])
        w_c = sb("w_c", [P, KH, D])
        b_kv = sb("b_kv", [P, 2 * D])
        b_out = sb("b_out", [P, D])
        bq = sb("bq", [P, KH])
        bq_rep = sb("bq_rep", [P, KH, P])
        gamma = sb("gamma", [P, D])
        beta = sb("beta", [P, D])
        rot_t = sb("rot_t", [P, NT, 2, 2 * ROT])
        kv = sb("kv", [P, 2, 2, D])
        rc = sb("rc", [P, 2, 2, 2 * ROT])
        rs = sb("rs", [P, 2, 2, 2 * ROT])
        sq = sb("sq", [P, 4, D])
        norm2 = sb("norm2", [P, NT, 2])
        inv_n = sb("inv_n", [P, NT, 2])
        w_tok = sb("w_tok", [P, NT])
        A = sb("A", [P, KH])
        b_all = sb("b_all", [P, D])
        prods = sb("prods", [P, NT, D])
        mv2 = sb("mv2", [P, NT, 2])
        var2 = sb("var2", [P, NT])
        rstd2 = sb("rstd2", [P, NT])
        inner = Named()
        inner.x, inner.h, inner.stats, inner.mv = k.h, xn, k.stats, mv2
        inner.var, inner.rstd, inner.mhalf = var2, rstd2, k.mhalf
        dve_step = sem("m_dve_step")
        var_ready = sem("m_var_ready")
        rstd_ready = sem("m_rstd_ready")
        var2_ready = sem("m_var2_ready")
        rstd2_ready = sem("m_rstd2_ready")
        h_ready = sem("m_h_ready")
        xn_ready = sem("m_xn_ready")
        weights_in = sem("m_weights_in")
        q_done = sem("m_q_done")
        wqT_ready = sem("m_wqT_ready")
        tp_done = sem("m_tp_done")
        xnT_ready = sem("m_xnT_ready")
        kv_done = sem("m_kv_done")
        kv_ready = sem("m_kv_ready")
        norm_ready = sem("m_norm_ready")
        rot_ready = sem("m_rot_ready")
        prod_ready = sem("m_prod_ready")
        inv_ready = sem("m_inv_ready")
        w_ready = sem("m_w_ready")
        A_done = sem("m_A_done")
        wsc_ready = sem("m_wsc_ready")
        wc_done = sem("m_wc_done")
        wc_ready = sem("m_wc_ready")
        gh_ready = sem("m_gh_ready")
        hb_ready = sem("m_hb_ready")
        y_done = sem("m_y_done")
        y_used = sem("m_y_used")
        sum_ready = sem("m_sum_ready")
        block = ctx.enter_context(nc.Block())
        WEIGHTS = 8

        @block.sync
        def _(sp):
            load = lambda dst, src: sp.dma_start(dst, src).then_inc(weights_in, 16)
            load(gamma[:, :], a.L1_attn_gamma.partition_broadcast(P))
            load(beta[:, :], a.L1_attn_beta.partition_broadcast(P))
            load(w_in[:, :, :], a.L1_attn_W_in.rearrange("(t p) n -> p t n", p=P))
            load(b_kv[:, :], a.L1_attn_b_in[D:3 * D].partition_broadcast(P))
            load(rot_t[:, :, :, :], a.rot_t.rearrange("(i p) s n -> p i s n", p=P))
            load(w_out[:, :, :], a.L1_attn_W_out.rearrange("(t p) n -> p t n", p=P))
            load(b_out[:, :], a.L1_attn_b_out.partition_broadcast(P))
            sp.dma_start(bq[:, :], a.L1_attn_b_in[0:D].rearrange("(t p) -> p t", p=P),
                         allow_slow_non_contiguous=True).then_inc(weights_in, 16)
            sp.wait_ge(weights_in, 16 * WEIGHTS)

        @block.gpsimd
        def _(pool):
            for q in range(NC):
                ln_rstd(nc, pool, k, q, var_ready, rstd_ready)
            for q in range(NC):
                ln_rstd(nc, pool, inner, q, var2_ready, rstd2_ready)

            def invert(q):
                pool.wait_ge(norm_ready, 2 * TQ * (q + 1))
                s = slice(TQ * q, TQ * (q + 1))
                nc.gpsimd.tensor_tensor(inv_n[:, s, :].rearrange("p i s -> p (i s)"),
                                        norm2[:, s, :].rearrange("p i s -> p (i s)"),
                                        k.mhalf[:, 0:2 * TQ], ALU.pow).then_inc(inv_ready, 1)

            pool.wait_ge(weights_in, 16 * WEIGHTS)
            for i in range(NT):
                pool.wait_ge(kv_ready, i + 1)
                if i >= 2:
                    pool.wait_ge(prod_ready, i - 1)
                pairs = kv[:, i % 2, :, 0:2 * ROT].rearrange("p s (n two) -> p s n two", two=2)
                sin = rot_t[:, i, 1, :].rearrange("p (n two) -> p n two", two=2)
                dst = rs[:, i % 2, :, :].rearrange("p s (n two) -> p s n two", two=2)
                for two in range(2):
                    last = nc.gpsimd.tensor_tensor(dst[:, :, :, two], pairs[:, :, :, 1 - two],
                                                   bcast(sin[:, :, two], 2), ALU.mult)
                last.then_inc(rot_ready, 1)
                if i % TQ == TQ - 1:
                    invert(i // TQ)
            for q in range(NC):
                nc.gpsimd.tensor_tensor(quarter(k.h, q), quarter(k.h, q), bcast(k.mod[:, 1, GA, :], TQ),
                                        ALU.mult).then_inc(gh_ready, 1)
                pool.wait_ge(gh_ready, q + 1)
                nc.gpsimd.tensor_tensor(quarter(k.x, q), quarter(k.x, q), quarter(k.h, q), ALU.add).then_inc(hb_ready, 1)

        @block.vector
        def _(dve):
            step = stepper(dve, dve_step)
            tt = nc.vector.tensor_tensor
            ln_stats(nc, dve, step, k, 0, var_ready)
            for q in range(NC):
                if q + 1 < NC:
                    ln_stats(nc, dve, step, k, q + 1, var_ready)
                ln_apply(nc, dve, step, k, q, k.mod[:, 1, CA, :], k.mod[:, 1, SA, :], rstd_ready, h_ready)
                dve.wait_ge(h_ready, q + 1)
                ln_stats(nc, dve, step, inner, q, var2_ready)
            dve.wait_ge(weights_in, 16 * WEIGHTS)
            step(nc.vector.tensor_copy(bq_rep[:, :, :], last_bcast(bq[:, :], P)))
            for q in range(NC):
                ln_apply(nc, dve, step, inner, q, gamma[:, :], beta[:, :], rstd2_ready, xn_ready)

            def products(i):
                s = i % 2
                x2 = kv[:, s, :, 0:2 * ROT]
                step(tt(rc[:, s, :, :], x2, bcast(rot_t[:, i, 0, :], 2), ALU.mult))
                dve.wait_ge(rot_ready, i + 1)
                step(tt(rc[:, s, :, :], rc[:, s, :, :], rs[:, s, :, :], ALU.add))
                tt(prods[:, i, 2 * ROT:D], kv[:, s, 0, 2 * ROT:D], kv[:, s, 1, 2 * ROT:D], ALU.mult)
                tt(prods[:, i, 0:2 * ROT], rc[:, s, 0, :], rc[:, s, 1, :], ALU.mult).then_inc(prod_ready, 1)

            for i in range(NT + 1):
                if i < NT:
                    dve.wait_ge(kv_done, i + 1)
                    if i >= 2:
                        dve.wait_ge(norm_ready, 2 * (i - 1))
                        dve.wait_ge(prod_ready, i - 1)
                    tt(kv[:, i % 2, :, :].rearrange("p s d -> p (s d)"), pkv[i % 2][:, :], b_kv[:, :],
                       ALU.add).then_inc(kv_ready, 1)
                if i >= 1:
                    dve.wait_ge(kv_ready, i)
                    products(i - 1)
                if i % TQ == 0 and i >= TQ:
                    q = i // TQ - 1
                    dve.wait_ge(inv_ready, q + 1)
                    tt(w_tok[:, TQ * q:TQ * (q + 1)], inv_n[:, TQ * q:TQ * (q + 1), 0],
                       inv_n[:, TQ * q:TQ * (q + 1), 1], ALU.mult).then_inc(w_ready, 1)
            gate = k.mod[:, 1, GA, :]
            step(tt(w_out[:, :, :], w_out[:, :, :], bcast(gate, KH), ALU.mult))
            step(tt(b_out[:, :], b_out[:, :], gate, ALU.mult))
            dve.wait_ge(A_done, 1)
            for t in range(KH):
                last = nc.vector.tensor_scalar(A[:, t:t + 1], pA[t][:, :], 0.5, 0.5, ALU.mult, ALU.add)
            step(last)
            for t in range(KH):
                last = nc.vector.tensor_scalar(w_sc[:, t, :], w_out[:, t, :], A[:, t:t + 1], None, ALU.mult)
            last.then_inc(wsc_ready, 1)
            dve.wait_ge(wc_done, 1)
            nc.vector.tensor_copy(w_c[:, :, :].rearrange("p t n -> p (t n)"), pw[0][:, :]).then_inc(wc_ready, 1)
            dve.wait_ge(wc_done, 2)
            tt(b_all[:, :], pw[1][:, 0:D], b_out[:, :], ALU.add).then_inc(wc_ready, 1)
            dve.wait_ge(wc_ready, 2)
            for i in range(NT):
                if i % TQ == 0:
                    q = i // TQ
                    dve.wait_ge(hb_ready, q + 1)
                    tt(quarter(k.x, q), quarter(k.x, q), bcast(b_all[:, :], TQ), ALU.add).then_inc(sum_ready, 1)
                    dve.wait_ge(sum_ready, q + 1)
                dve.wait_ge(y_done, i + 1)
                tt(k.x[:, i, :], k.x[:, i, :], pkv[i % 2][:, 0:D], ALU.add).then_inc(y_used, 1)
            dve.wait_ge(y_used, NT)

        @block.scalar
        def _(act):
            for t in range(KH):
                act.wait_ge(q_done, 1)
                last = nc.scalar.copy(wqT[:, t, :], pw[0][:, D * t:D * (t + 1)])
            last.then_inc(wqT_ready, 1)

            def squares(i):
                act.wait_ge(kv_ready, i + 1)
                for s in range(2):
                    n = 2 * i + s
                    if n >= 4:
                        act.wait_ge(norm_ready, n - 3)
                    nc.scalar.activation(sq[:, n % 4, :], kv[:, i % 2, s, :], ACT.Square,
                                         accum_out=norm2[:, i, s:s + 1]).then_inc(norm_ready, 1)

            for q in range(NC):
                for half in range(KH):
                    act.wait_ge(tp_done, 2 * q + half + 1)
                    nc.scalar.copy(xnT[:, half, QC * q:QC * (q + 1)], tp[half][:, :]).then_inc(xnT_ready, 1)
                if q >= 1:
                    for i in range(TQ * (q - 1), TQ * q):
                        squares(i)
            for i in range(TQ * (NC - 1), NT):
                squares(i)

        @block.tensor
        def _(pe):
            pe.wait_ge(weights_in, 16 * WEIGHTS)
            for m in range(KH):
                for t in range(KH):
                    last = nc.tensor.transpose(pw[0][:, D * m + P * t:D * m + P * (t + 1)],
                                               w_in[:, t, P * m:P * (m + 1)], k.ident[:, :])
            last.then_inc(q_done, 1)

            def keys_values(i):
                pe.wait_ge(xnT_ready, 2 * (i // TQ) + 2)
                if i >= 2:
                    pe.wait_ge(kv_ready, i - 1)
                for t in range(KH):
                    last = nc.tensor.matmul(pkv[i % 2][:, :], xnT[:, t, P * i:P * (i + 1)], w_in[:, t, D:3 * D],
                                            start=(t == 0), stop=(t == KH - 1))
                last.then_inc(kv_done, 1)

            for q in range(NC):
                pe.wait_ge(xn_ready, q + 1)
                if q >= 1:
                    pe.wait_ge(xnT_ready, 2 * q)
                for last in transpose_quarter(nc, k, xn, q, tp):
                    last.then_inc(tp_done, 1)
                if q >= 1:
                    for i in range(TQ * (q - 1), TQ * q):
                        keys_values(i)
            for i in range(TQ * (NC - 1), NT):
                keys_values(i)
            pe.wait_ge(prod_ready, NT)
            pe.wait_ge(w_ready, NC)
            for t in range(KH):
                for i in range(NT):
                    last = nc.tensor.matmul(pA[t][:, :], prods[:, i, P * t:P * (t + 1)], w_tok[:, i:i + 1],
                                            start=(i == 0), stop=(i == NT - 1))
            last.then_inc(A_done, 1)
            pe.wait_ge(wqT_ready, 1)
            pe.wait_ge(wsc_ready, 1)
            for t in range(KH):
                for m in range(KH):
                    last = nc.tensor.matmul(pw[0][:, D * t:D * (t + 1)], wqT[:, m, P * t:P * (t + 1)], w_sc[:, m, :],
                                            start=(m == 0), stop=(m == KH - 1))
            last.then_inc(wc_done, 1)
            for m in range(KH):
                last = nc.tensor.matmul(pw[1][:, 0:D], bq_rep[:, m, :], w_sc[:, m, :], start=(m == 0), stop=(m == KH - 1))
            last.then_inc(wc_done, 1)
            pe.wait_ge(wc_ready, 1)
            pe.wait_ge(kv_ready, NT)
            for i in range(NT):
                if i >= 2:
                    pe.wait_ge(y_used, i - 1)
                for t in range(KH):
                    last = nc.tensor.matmul(pkv[i % 2][:, 0:D], xnT[:, t, P * i:P * (i + 1)], w_c[:, t, :],
                                            start=(t == 0), stop=(t == KH - 1))
                last.then_inc(y_done, 1)


def phase_experts1(nc, k, a, sem):
    FT = F1 // P
    ctx = ExitStack()
    with ctx:
        px = ctx.enter_context(nc.psum_tensor("e1_x", [P, KH, P], FP))
        pg = [ctx.enter_context(nc.psum_tensor(f"e1_g{s}", [P, F1], FP)) for s in range(2)]
        pu = [ctx.enter_context(nc.psum_tensor(f"e1_u{s}", [P, F1], FP)) for s in range(2)]
        pm = ctx.enter_context(nc.psum_tensor("e1_m", [P, F1], FP))
        py = ctx.enter_context(nc.psum_tensor("e1_y", [P, D], FP))
        xb = ctx.enter_context(nc.sbuf_tensor("xb", [P, 2, D], FP))
        xT = ctx.enter_context(nc.sbuf_tensor("xT1", [P, 2, KH, P], FP))
        g = ctx.enter_context(nc.sbuf_tensor("silu_g", [P, 2, F1], FP))
        m = ctx.enter_context(nc.sbuf_tensor("mid1", [P, 2, F1], FP))
        mT = ctx.enter_context(nc.sbuf_tensor("mid1T", [P, 2, F1], FP))
        y = ctx.enter_context(nc.sbuf_tensor("y1", [P, 2, D], FP))
        x_in = [sem(f"e1_x_in{s}") for s in range(2)]
        t_done = sem("e1_t_done")
        xT_ready = sem("e1_xT_ready")
        g_done = sem("e1_g_done")
        u_done = sem("e1_u_done")
        silu_ready = sem("e1_silu_ready")
        m_ready = sem("e1_m_ready")
        mt_done = sem("e1_mt_done")
        mT_ready = sem("e1_mT_ready")
        y_done = sem("e1_y_done")
        y_ready = sem("e1_y_ready")
        stored = [sem(f"e1_stored{s}") for s in range(2)]
        block = ctx.enter_context(nc.Block())
        src = k.disp[1].rearrange("(b p) d -> b p d", p=BLK)
        dst = k.eout[1].rearrange("(b p) d -> b p d", p=BLK)
        assert NB % 2 == 1
        PAIRS = NB // 2

        def run(eng, body, first=0):
            body(0, 0, True)
            body(0, 1, True)
            with eng.Fori(1, PAIRS) as i:
                body(i, 0, False)
                body(i, 1, False)
            body(PAIRS, 0, False)

        @block.sync
        def _(sp):
            def load(i, s, peeled):
                b = 2 * i + s
                if not peeled:
                    sp.wait_ge(t_done, b - 1)
                sp.dma_start(xb[:, s, :], src[b, :, :]).then_inc(x_in[s], 16)
            run(sp, load)

        @block.tensor
        def _(pe):
            def expert_of(b):
                return pe.value_load(k.block_expert[0:1, bass.ds(b, 1)], min_val=0, max_val=E - 1)

            def transpose_rows(i, s):
                b = 2 * i + s
                pe.wait_ge(x_in[s], i * 16 + 16)
                if not (type(b) is int and b == 0):
                    pe.wait_ge(xT_ready, b)
                for t in range(KH):
                    last = nc.tensor.transpose(px[:, t, :], xb[:, s, P * t:P * (t + 1)], k.ident[:, :])
                last.then_inc(t_done, 1)

            def product(out, s, e, mat, done):
                for t in range(KH):
                    last = nc.tensor.matmul(out[:, :], xT[:, s, t, :], k.w1T[:, e, mat, 512 * t:512 * (t + 1)],
                                            start=(t == 0), stop=(t == KH - 1))
                last.then_inc(done, 1)

            def back(i, s, first):
                b = 2 * i + s
                pe.wait_ge(m_ready, b + 1)
                if not (type(b) is int and b == 0):
                    pe.wait_ge(mT_ready, b)
                for f in range(FT):
                    last = nc.tensor.transpose(pm[:, P * f:P * (f + 1)], m[:, s, P * f:P * (f + 1)], k.ident[:, :])
                last.then_inc(mt_done, 1)

            def second(i, s, e, first):
                b = 2 * i + s
                pe.wait_ge(mT_ready, b + 1)
                if not (type(b) is int and b == 0):
                    pe.wait_ge(y_ready, b)
                for f in range(FT):
                    last = nc.tensor.matmul(py[:, :], mT[:, s, P * f:P * (f + 1)], k.w1T[:, e, 2, D * f:D * (f + 1)],
                                            start=(f == 0), stop=(f == FT - 1))
                last.then_inc(y_done, 1)

            def body(i, s, peeled, head=False, tail=False):
                b = 2 * i + s
                e = expert_of(b)
                pe.wait_ge(xT_ready, b + 1)
                if not peeled:
                    pe.wait_ge(m_ready, b - 1)
                product(pg[s], s, e, 0, g_done)
                if not head:
                    pi, psl = (i, 0) if s else (i - 1, 1)
                    ep = expert_of(b - 1)
                    back(pi, psl, peeled)
                product(pu[s], s, e, 1, u_done)
                if not tail:
                    transpose_rows(i + s, 1 - s)
                if not head:
                    second(pi, psl, ep, peeled)

            transpose_rows(0, 0)
            body(0, 0, True, head=True)
            body(0, 1, True)
            with pe.Fori(1, PAIRS) as i:
                body(i, 0, False)
                body(i, 1, False)
            body(PAIRS, 0, False, tail=True)
            e = expert_of(NB - 1)
            back(PAIRS, 0, False)
            second(PAIRS, 0, e, False)

        @block.scalar
        def _(act):
            def rows(i, s):
                b = 2 * i + s
                act.wait_ge(t_done, b + 1)
                nc.scalar.copy(xT[:, s, :, :], px[:, :, :]).then_inc(xT_ready, 1)

            def silu(i, s, peeled):
                b = 2 * i + s
                act.wait_ge(g_done, b + 1)
                if not peeled:
                    act.wait_ge(m_ready, b - 1)
                nc.scalar.activation(g[:, s, :], pg[s][:, :], ACT.Silu).then_inc(silu_ready, 1)

            def hidden(i, s):
                b = 2 * i + s
                act.wait_ge(mt_done, b + 1)
                nc.scalar.copy(mT[:, s, :], pm[:, :]).then_inc(mT_ready, 1)

            def body(i, s, peeled, head=False, tail=False):
                silu(i, s, peeled)
                if not head:
                    hidden(*((i, 0) if s else (i - 1, 1)))
                if not tail:
                    rows(i + s, 1 - s)

            rows(0, 0)
            body(0, 0, True, head=True)
            body(0, 1, True)
            with act.Fori(1, PAIRS) as i:
                body(i, 0, False)
                body(i, 1, False)
            body(PAIRS, 0, False, tail=True)
            hidden(PAIRS, 0)

        @block.vector
        def _(dve):
            def gate(i, s, peeled):
                b = 2 * i + s
                dve.wait_ge(silu_ready, b + 1)
                dve.wait_ge(u_done, b + 1)
                if not peeled:
                    dve.wait_ge(mt_done, b - 1)
                nc.vector.tensor_tensor(m[:, s, :], g[:, s, :], pu[s][:, :], ALU.mult).then_inc(m_ready, 1)

            def copy_y(i, s, peeled):
                b = 2 * i + s
                dve.wait_ge(y_done, b + 1)
                if not peeled:
                    dve.wait_ge(stored[s], i * 16)
                nc.vector.tensor_copy(y[:, s, :], py[:, :]).then_inc(y_ready, 1)

            gate(0, 0, True)
            gate(0, 1, True)
            copy_y(0, 0, True)
            gate(1, 0, False)
            copy_y(0, 1, True)
            gate(1, 1, False)
            copy_y(1, 0, False)
            with dve.Fori(2, PAIRS) as i:
                gate(i, 0, False)
                copy_y(i - 1, 1, False)
                gate(i, 1, False)
                copy_y(i, 0, False)
            gate(PAIRS, 0, False)
            copy_y(PAIRS - 1, 1, False)
            copy_y(PAIRS, 0, False)

        @block.gpsimd
        def _(pool):
            def store(i, s, peeled):
                b = 2 * i + s
                pool.wait_ge(y_ready, b + 1)
                pool.dma_start(dst[b, :, :], y[:, s, :]).then_inc(stored[s], 16)
            run(pool, store)
            pool.wait_ge(stored[0], 16 * (PAIRS + 1))
            pool.wait_ge(stored[1], 16 * PAIRS)


def named_inputs(aps):
    a = Named()
    a.L0_attn_x = aps["L0_attn_x"]
    a.L0_attn_Wq = aps["L0_attn_Wq"]
    a.L0_attn_Wk = aps["L0_attn_Wk"]
    a.L0_attn_Wv = aps["L0_attn_Wv"]
    a.L0_attn_Wo = aps["L0_attn_Wo"]
    a.L0_attn_bo = aps["L0_attn_bo"]
    a.L0_ffn_gate_weight = aps["L0_ffn_gate_weight"]
    a.L0_ffn_wi = aps["L0_ffn_wi"]
    a.L0_ffn_wo = aps["L0_ffn_wo"]
    a.L0_c = aps["L0_c"]
    a.L0_wmod = aps["L0_wmod"]
    a.L1_attn_W_in = aps["L1_attn_W_in"]
    a.L1_attn_b_in = aps["L1_attn_b_in"]
    a.L1_attn_W_out = aps["L1_attn_W_out"]
    a.L1_attn_b_out = aps["L1_attn_b_out"]
    a.L1_attn_gamma = aps["L1_attn_gamma"]
    a.L1_attn_beta = aps["L1_attn_beta"]
    a.L1_ffn_gate_w = aps["L1_ffn_gate_w"]
    a.L1_ffn_w1 = aps["L1_ffn_w1"]
    a.L1_ffn_w2 = aps["L1_ffn_w2"]
    a.L1_ffn_w3 = aps["L1_ffn_w3"]
    a.L1_c = aps["L1_c"]
    a.L1_wmod = aps["L1_wmod"]
    a.kpart = aps["kpart"]
    a.rot_t = aps["rot_t"]
    return a


def build(nc, a, out, upto=99):
    ctx = ExitStack()
    with ctx:
        def sem(name):
            return ctx.enter_context(nc.semaphore(name))

        def sbuf(stack, name, shape, dt=FP):
            return stack.enter_context(nc.sbuf_tensor("k_" + name, shape, dt))

        k = Named()
        k.disp = [nc.dram_tensor("disp0", [E * CAP + T, D], FP).ap(), nc.dram_tensor("disp1", [NB * BLK, D], FP).ap()]
        k.q_dram = nc.dram_tensor("q_dram", [3, D, T], BF).ap()
        k.q_in = [sem(f"q_in{c}") for c in range(NC)]
        k.eout = [nc.dram_tensor("eout0", [E * CAP, D], FP).ap(), nc.dram_tensor("eout1", [NB * BLK, D], FP).ap()]
        k.x = sbuf(ctx, "x", [P, NT, D])
        k.h = sbuf(ctx, "h", [P, NT, D])
        k.mod = sbuf(ctx, "mod", [P, 2, MODS, D])
        k.mv = sbuf(ctx, "mv", [P, NT, 2])
        k.var = sbuf(ctx, "var", [P, NT])
        k.rstd = sbuf(ctx, "rstd", [P, NT])
        k.mhalf = sbuf(ctx, "mhalf", [P, NT])
        k.slot = sbuf(ctx, "slot", [P, 2, NT], U32)
        k.weight = sbuf(ctx, "weight", [P, 2, NT])
        k.block_expert = sbuf(ctx, "block_expert", [P, NB], U32)
        k.ident = sbuf(ctx, "ident", [P, P])
        k.ident_bf = sbuf(ctx, "ident_bf", [P, P], BF)
        k.maskq = sbuf(ctx, "maskq", [P, P], BF)
        k.before = sbuf(ctx, "before", [P, P], BF)
        k.ones_bf = sbuf(ctx, "ones_bf", [P, P], BF)
        k.stats = sbuf(ctx, "stats", [P, NT, 6])
        attn = ExitStack()
        with attn:
            k.wq = sbuf(attn, "wq", [P, KH, D])
            k.wk1 = sbuf(attn, "wk1", [P, KH, HD])
            k.wv = sbuf(attn, "wv", [P, KH, HD])
            k.wo = sbuf(attn, "wo", [P, KH, D])
            k.bo = sbuf(attn, "bo", [P, D])
            k.kpart = sbuf(attn, "kpart", [P, 4])
            k.ks = sbuf(attn, "ks", [P, T], BF)
            k.vaug = sbuf(attn, "vaug", [P, NT, 32])
            k.qs = sbuf(attn, "qs", [P, NC, H, QC], BF)
            phase_setup(nc, k, a, sem)
            if upto >= 1:
                phase_qkv(nc, k, a, sem)
            k.oT = sbuf(attn, "oT", [P, NG, T])
            if upto >= 2:
                phase_attention(nc, k, a, sem)
            if upto >= 3:
                phase_project(nc, k, a, sem)
        experts0 = ExitStack()
        with experts0:
            k.wi = sbuf(experts0, "wi", [P, 2, KH, F0])
            k.wo_e = sbuf(experts0, "wo_e", [P, 2, F0 // P, D])
            k.w_in0 = [sem(f"w_in0_{s}") for s in range(2)]
            if upto >= 4:
                phase_router(nc, k, a, sem, 0, a.L0_ffn_gate_weight)
            if upto >= 5:
                phase_experts0(nc, k, a, sem)
        if upto >= 6:
            phase_combine(nc, k, a, sem, 0, out)
        if upto >= 7:
            phase_mix(nc, k, a, sem)
        experts1 = ExitStack()
        with experts1:
            k.w1T = sbuf(experts1, "w1T", [P, E, 3, 1024])
            if upto >= 8:
                phase_router(nc, k, a, sem, 1, a.L1_ffn_gate_w)
            if upto >= 9:
                phase_experts1(nc, k, a, sem)
            if upto >= 10:
                phase_combine(nc, k, a, sem, 1, out)


def consts():
    import numpy as np
    kpart = np.zeros((P, 4), np.float32)
    for g, part in enumerate((0, 1, 2, 0, 1, 0, 1)):
        kpart[HD * g:HD * (g + 1), part] = 1.0
    kpart[BROW:KALL, 3] = 1.0
    inv = (np.float32(1.0) / np.float32(10000.0) ** (np.arange(0, 2 * ROT, 2, dtype=np.float32)
                                                     / np.float32(2 * ROT))).astype(np.float32)
    angle = np.arange(T, dtype=np.float32)[:, None] * inv[None, :]
    rot = np.zeros((T, 2, ROT, 2), np.float32)
    rot[:, 0, :, :] = np.cos(angle)[:, :, None]
    rot[:, 1, :, 0] = -np.sin(angle)
    rot[:, 1, :, 1] = np.sin(angle)
    return {"kpart": kpart, "rot_t": rot.reshape(T, 2, 2 * ROT)}


_INS = ['L0_attn_x', 'L0_attn_Wq', 'L0_attn_Wk', 'L0_attn_Wv', 'L0_attn_Wo', 'L0_attn_bo', 'L0_ffn_gate_weight',
        'L0_ffn_wi', 'L0_ffn_wo', 'L0_c', 'L0_wmod', 'L1_attn_W_in', 'L1_attn_b_in', 'L1_attn_W_out',
        'L1_attn_b_out', 'L1_attn_gamma', 'L1_attn_beta', 'L1_ffn_gate_w', 'L1_ffn_w1', 'L1_ffn_w2', 'L1_ffn_w3',
        'L1_c', 'L1_wmod']


def kernel(**inputs):
    import numpy as _np
    import concourse.bacc as _bacc
    from concourse import mybir as _mybir
    from concourse.bass_utils import run_bass_kernel_spmd as _run

    nc = _bacc.Bacc("TRN2", target_bir_lowering=False, num_devices=1)
    arrays, aps = {}, {}
    for name, value in [(n, inputs[n]) for n in _INS] + list(consts().items()):
        arr = _np.ascontiguousarray(value)
        arrays[f"in_{name}_dram"] = arr
        aps[name] = nc.dram_tensor(f"in_{name}_dram", arr.shape, _mybir.dt.from_np(arr.dtype), kind="ExternalInput").ap()
    out = nc.dram_tensor("out_0_dram", (1, T, D), FP, kind="ExternalOutput").ap()
    build(nc, named_inputs(aps), out)
    r = _run(nc, [arrays], core_ids=[0])
    return r.results[0]["out_0_dram"]
```

```python
import concourse.bass as bass
from concourse import mybir
from contextlib import ExitStack

FP = mybir.dt.float32
BF = mybir.dt.bfloat16
U32 = mybir.dt.uint32
ALU = mybir.AluOpType
ACT = mybir.ActivationFunctionType
AX = mybir.AxisListType

P = 128
T = 2048
D = 256
NT = T // P
KH = D // P
H, HD = 16, 16
GH = 4
NG = H // GH
QC = 512
NC = T // QC
TQ = QC // P
MODS = 6
SA, CA, GA, SB, CB, GB = range(MODS)
EPS = 1e-5
NEG = -1e30
E = 8
F0, CAP = 1024, 320
F1 = 512
BLK = 128
NB = (2 * T + E * (BLK - 1)) // BLK
PROD = 7
KROWS = PROD * HD
BROW = KROWS
KALL = KROWS + 2
ROT = 64


class Named:
    pass


def bcast(ap, n):
    return ap.unsqueeze(1).to_broadcast([ap.shape[0], n, ap.shape[1]])


def last_bcast(ap, n):
    return ap.unsqueeze(2).to_broadcast([ap.shape[0], ap.shape[1], n])


def stepper(eng, sem, count):
    def step(ins):
        count[0] += 1
        ins.then_inc(sem, 1)
        eng.wait_ge(sem, count[0])
    return step


def quarter(ap, q):
    return ap[:, TQ * q:TQ * (q + 1), :]


def ln_stats(nc, dve, step, k, q, var_ready):
    tiles = range(TQ * q, TQ * (q + 1))
    for i in tiles:
        last = nc.vector.bn_stats(k.stats[:, i, :], k.x[:, i, :])
    step(last)
    for i in tiles:
        last = nc.vector.bn_aggr(k.mv[:, i, :], k.stats[:, i, :])
    step(last)
    nc.vector.tensor_scalar_add(k.var[:, TQ * q:TQ * (q + 1)], k.mv[:, TQ * q:TQ * (q + 1), 1],
                                EPS).then_inc(var_ready, 1)


def ln_tile_stats(nc, dve, step, k, i, var_ready):
    q = i // TQ
    last = nc.vector.bn_stats(k.stats[:, i, :], k.x[:, i, :])
    if i % TQ == TQ - 1:
        step(last)
        for n in range(TQ * q, TQ * (q + 1)):
            last = nc.vector.bn_aggr(k.mv[:, n, :], k.stats[:, n, :])
        step(last)
        nc.vector.tensor_scalar_add(k.var[:, TQ * q:TQ * (q + 1)], k.mv[:, TQ * q:TQ * (q + 1), 1],
                                    EPS).then_inc(var_ready, 1)


def ln_rstd(nc, pool, k, q, var_ready, rstd_ready):
    pool.wait_ge(var_ready, q + 1)
    s = slice(TQ * q, TQ * (q + 1))
    nc.gpsimd.tensor_tensor(k.rstd[:, s], k.var[:, s], k.mhalf[:, s], ALU.pow).then_inc(rstd_ready, 1)


def ln_apply(nc, dve, step, k, q, scale, shift, rstd_ready, h_ready):
    if rstd_ready is not None:
        dve.wait_ge(rstd_ready, q + 1)
    for i in range(TQ * q, TQ * (q + 1)):
        last = nc.vector.tensor_scalar(k.h[:, i, :], k.x[:, i, :], k.mv[:, i, 0:1], k.rstd[:, i:i + 1],
                                       ALU.subtract, ALU.mult)
    step(last)
    hq = quarter(k.h, q)
    step(nc.vector.tensor_tensor(hq, hq, bcast(scale, TQ), ALU.mult))
    nc.vector.tensor_tensor(hq, hq, bcast(shift, TQ), ALU.add).then_inc(h_ready, 1)


def ln_bias(nc, dve, k, q, rstd_ready, bias_ready):
    if rstd_ready is not None:
        dve.wait_ge(rstd_ready, q + 1)
    s = slice(TQ * q, TQ * (q + 1))
    nc.vector.scalar_tensor_tensor(k.nbias[:, s], k.mv[:, s, 0], -1.0, k.rstd[:, s],
                                   ALU.mult, ALU.mult).then_inc(bias_ready, 1)


def ln_normal(nc, act, k, q, bias_ready, norm_ready):
    act.wait_ge(bias_ready, q + 1)
    for i in range(TQ * q, TQ * (q + 1)):
        last = nc.scalar.activation(k.h[:, i, :], k.x[:, i, :], ACT.Identity, bias=k.nbias[:, i:i + 1],
                                    scale=k.rstd[:, i:i + 1])
    last.then_inc(norm_ready, 1)


def ln_modulate(nc, dve, step, k, q, scale, shift, norm_ready, h_ready):
    dve.wait_ge(norm_ready, q + 1)
    hq = quarter(k.h, q)
    step(nc.vector.tensor_tensor(hq, hq, bcast(scale, TQ), ALU.mult))
    nc.vector.tensor_tensor(hq, hq, bcast(shift, TQ), ALU.add).then_inc(h_ready, 1)


def transpose_quarter(nc, k, src, q, banks):
    out = []
    for half in range(KH):
        for i in range(TQ):
            last = nc.tensor.transpose(banks[half][:, P * i:P * (i + 1)],
                                       src[:, TQ * q + i, P * half:P * (half + 1)], k.ident[:, :])
        out.append(last)
    return out


def phase_setup(nc, k, a, sem):
    with nc.psum_tensor("p0_mod", [P, 2, MODS * D], FP) as mod_ps, \
            nc.sbuf_tensor("silu_c", [P, 2, KH, P], FP) as silu_c, \
            nc.sbuf_tensor("c_col", [P, 2, KH], FP) as c_col, \
            nc.sbuf_tensor("wmod", [P, 2, KH, MODS * D], FP) as wmod, \
            nc.sbuf_tensor("gate_mag", [P, 2, D], FP) as gate_mag, \
            nc.sbuf_tensor("gate_sgn", [P, 2, D], FP) as gate_sgn, \
            nc.Block() as block:
        x_in = sem("x_in")
        mod_in = sem("mod_in")
        silu_done = sem("silu_done")
        mod_done = sem("mod_done")
        mod_copied = sem("mod_copied")
        pool_step = sem("p0_pool_step")
        half_set = sem("half_set")
        var_ready = sem("p0_var_ready")
        rstd_ready = sem("p0_rstd_ready")
        const_in = sem("const_in")

        @block.sync
        def _(sp):
            for layer, c in enumerate((a.L0_c, a.L1_c)):
                sp.dma_start(c_col[:, layer, :], c.rearrange("a (t p) -> p (a t)", p=P),
                             allow_slow_non_contiguous=True).then_inc(mod_in, 16)
            for layer, w in enumerate((a.L0_wmod, a.L1_wmod)):
                sp.dma_start(wmod[:, layer, :, :], w.rearrange("(t p) n -> p t n", p=P)).then_inc(mod_in, 16)
            for w, dst in ((a.L0_attn_Wq, k.wq), (a.L0_attn_Wv, k.wv), (a.L0_attn_Wo, k.wo)):
                sp.dma_start(dst[:, :, :], w.rearrange("(t p) n -> p t n", p=P)).then_inc(const_in, 16)
            sp.dma_start(k.wk1[:, :, :], a.L0_attn_Wk.rearrange("(t p) n -> p t n", p=P)).then_inc(const_in, 16)
            sp.dma_start(k.bo[:, :], a.L0_attn_bo.partition_broadcast(P)).then_inc(const_in, 16)
            sp.dma_start(k.kpart[:, :], a.kpart).then_inc(const_in, 16)
            sp.wait_ge(const_in, 16 * 6)

        @block.scalar
        def _(act):
            xv = a.L0_attn_x[0, :, :].rearrange("(i p) d -> p i d", p=P)
            for q in range(NC):
                act.dma_start(quarter(k.x, q), xv[:, TQ * q:TQ * (q + 1), :]).then_inc(x_in, 16)
            act.wait_ge(mod_in, 16 * 4)
            nc.scalar.activation(silu_c[:, :, :, :].rearrange("p l t n -> p (l t) n"),
                                 last_bcast(c_col[:, :, :].rearrange("p l t -> p (l t)"), P),
                                 ACT.Silu).then_inc(silu_done, 1)
            for layer in range(2):
                act.wait_ge(mod_done, layer + 1)
                nc.scalar.copy(k.mod[:, layer, :, :].rearrange("p m d -> p (m d)"),
                               mod_ps[:, layer, :]).then_inc(mod_copied, 1)

        @block.tensor
        def _(pe):
            pe.wait_ge(silu_done, 1)
            for layer in range(2):
                for n in range(MODS * D // 512):
                    for t in range(KH):
                        last = nc.tensor.matmul(mod_ps[:, layer, 512 * n:512 * (n + 1)], silu_c[:, layer, t, :],
                                                wmod[:, layer, t, 512 * n:512 * (n + 1)],
                                                start=(t == 0), stop=(t == KH - 1))
                last.then_inc(mod_done, 1)

        @block.vector
        def _(dve):
            step = stepper(dve, k.dve_step, k.dve_steps)
            for q in range(NC):
                dve.wait_ge(x_in, 16 * NC)
                ln_stats(nc, dve, step, k, q, var_ready)
            for layer in range(2):
                dve.wait_ge(mod_copied, layer + 1)
                m = k.mod[:, layer, :, :].rearrange("p (b m) d -> p b m d", b=2)
                step(nc.vector.tensor_scalar_add(m[:, :, 1, :], m[:, :, 1, :], 1.0))
                gate = m[:, :, 2, :]
                step(nc.vector.tensor_scalar(gate_sgn[:, :, :], gate, 0.0, 2.0, ALU.is_ge, ALU.mult))
                step(nc.vector.scalar_tensor_tensor(gate_mag[:, :, :], gate, -1.0, gate, ALU.mult, ALU.max))
                step(nc.vector.tensor_scalar_max(gate_mag[:, :, :], gate_mag[:, :, :], 0.25))
                step(nc.vector.scalar_tensor_tensor(gate, gate_sgn[:, :, :], -1.0, gate_mag[:, :, :],
                                                    ALU.add, ALU.mult))
            dve.wait_ge(rstd_ready, NC)

        @block.gpsimd
        def _(pool):
            step = stepper(pool, pool_step, [0])
            nc.gpsimd.memset(k.mhalf[:, :], -0.5).then_inc(half_set, 1)
            nc.gpsimd.memset(k.vaug[:, :, :], 0.0)
            nc.gpsimd.memset(k.ident[:, :], 0.0)
            nc.gpsimd.memset(k.ones_bf[:, :], 1.0)
            step(nc.gpsimd.memset(k.maskq[:, :], 0.0))
            nc.gpsimd.memset(k.vaug[:, :, HD:HD + 1], 1.0)
            step(nc.gpsimd.affine_select(out=k.ident[:, :], in_=k.ident[:, :], compare_op=ALU.not_equal, fill=1.0,
                                         base=0, pattern=[[-1, P]], channel_multiplier=1))
            nc.gpsimd.tensor_copy(k.ident_bf[:, :], k.ident[:, :])
            nc.gpsimd.affine_select(out=k.maskq[:, :], in_=k.maskq[:, :], compare_op=ALU.is_ge, fill=NEG,
                                    base=0, pattern=[[-1, P]], channel_multiplier=1)
            step(nc.gpsimd.affine_select(out=k.before[:, :], in_=k.ones_bf[:, :], compare_op=ALU.is_gt, fill=0.0,
                                         base=0, pattern=[[1, P]], channel_multiplier=-1))
            pool.wait_ge(half_set, 1)
            for q in range(NC):
                ln_rstd(nc, pool, k, q, var_ready, rstd_ready)


def load_queries(sp, k, c):
    for row, part in enumerate((0, 0, 0, 1, 1, 2, 2)):
        sp.dma_start(k.qs[HD * row:HD * (row + 1), c, :, :],
                     k.q_dram[part, :, QC * c:QC * (c + 1)].rearrange("(h d) n -> d h n", d=HD)).then_inc(k.q_in[c], 16)


def phase_qkv(nc, k, a, sem):
    ctx = ExitStack()
    with ctx:
        tp = [[ctx.enter_context(nc.psum_tensor(f"p1_tp{s}{t}", [P, QC], FP)) for t in range(KH)] for s in range(2)]
        pj = [ctx.enter_context(nc.psum_tensor(f"p1_pj{j}", [P, QC], FP)) for j in range(3)]
        pv = ctx.enter_context(nc.psum_tensor("p1_v", [P, TQ, HD], FP))
        wk = ctx.enter_context(nc.sbuf_tensor("wk_rep", [P, KH, P], FP))
        hT = ctx.enter_context(nc.sbuf_tensor("hT0", [P, KH, T], FP))
        parts = ctx.enter_context(nc.sbuf_tensor("q_parts", [P, 3, KH, T], BF))
        kparts = ctx.enter_context(nc.sbuf_tensor("k_parts", [P, 3, QC], BF))
        rest = ctx.enter_context(nc.sbuf_tensor("rest", [P, 2, QC], FP))
        ksum = ctx.enter_context(nc.sbuf_tensor("ksum", [P, 2, QC], BF))
        h_ready = sem("p1_h_ready")
        tp_done = sem("p1_tp_done")
        hT_ready = sem("p1_hT_ready")
        wk_ready = sem("p1_wk_ready")
        pj_done = sem("p1_pj_done")
        hi_done = sem("p1_hi_done")
        rest_done = sem("p1_rest_done")
        mid_done = sem("p1_mid_done")
        low_done = sem("p1_low_done")
        v_done = sem("p1_v_done")
        v_copied = sem("p1_v_copied")
        spilled = sem("p1_spilled")
        k_sum = sem("p1_k_sum")
        block = ctx.enter_context(nc.Block())

        def part_of(n, part):
            c, j = divmod(n, 3)
            return kparts[:, part, :] if j == 2 else parts[:, part, j, QC * c:QC * (c + 1)]

        @block.vector
        def _(dve):
            step = stepper(dve, k.dve_step, k.dve_steps)

            def remainder(n):
                dve.wait_ge(hi_done, n + 1)
                if n >= 2:
                    dve.wait_ge(low_done, n - 1)
                nc.vector.tensor_tensor(rest[:, n % 2, :], pj[n % 3][:, :], part_of(n, 0),
                                        ALU.subtract).then_inc(rest_done, 1)

            def low(n):
                dve.wait_ge(mid_done, n + 1)
                dve.wait_ge(rest_done, n + 1)
                nc.vector.tensor_tensor(part_of(n, 2), rest[:, n % 2, :], part_of(n, 1),
                                        ALU.subtract).then_inc(low_done, 1)
                if n % 3 == 2:
                    c = n // 3
                    dve.wait_ge(low_done, n + 1)
                    step(nc.vector.tensor_scalar(ksum[:, 0, :], kparts[:, 0, :], k.kpart[:, 0:1], k.kpart[:, 3:4],
                                                 ALU.mult, ALU.add))
                    step(nc.vector.scalar_tensor_tensor(ksum[:, 1, :], kparts[:, 1, :], k.kpart[:, 1:2],
                                                        ksum[:, 0, :], ALU.mult, ALU.add))
                    nc.vector.scalar_tensor_tensor(k.ks[:, QC * c:QC * (c + 1)], kparts[:, 2, :],
                                                   k.kpart[:, 2:3], ksum[:, 1, :], ALU.mult, ALU.add).then_inc(k_sum, 1)

            def copy_v(c):
                dve.wait_ge(v_done, c + 1)
                nc.vector.tensor_copy(k.vaug[:, TQ * c:TQ * (c + 1), 0:HD], pv[:, :, :]).then_inc(v_copied, 1)

            def parts_of_chunk(c):
                for n in range(3 * c, 3 * c + 3):
                    remainder(n)
                    if n >= 1:
                        low(n - 1)
                copy_v(c)

            nc.vector.tensor_copy(wk[:, :, :].rearrange("p t (r d) -> p t r d", r=P // HD),
                                  k.wk1[:, :, :].unsqueeze(2).to_broadcast([P, KH, P // HD, HD])).then_inc(wk_ready, 1)
            for q in range(NC):
                ln_apply(nc, dve, step, k, q, k.mod[:, 0, CA, :], k.mod[:, 0, SA, :], None, h_ready)
                if q >= 2:
                    parts_of_chunk(q - 2)
            parts_of_chunk(NC - 2)
            parts_of_chunk(NC - 1)
            low(3 * NC - 1)

        @block.tensor
        def _(pe):
            pe.wait_ge(wk_ready, 1)

            def project(c):
                pe.wait_ge(hT_ready, 2 * c + 2)
                rhs = [hT[:, t, QC * c:QC * (c + 1)] for t in range(KH)]
                for j in range(3):
                    n = 3 * c + j
                    if n >= 3:
                        pe.wait_ge(rest_done, n - 2)
                    for t in range(KH):
                        w = wk[:, t, :] if j == 2 else k.wq[:, t, P * j:P * (j + 1)]
                        last = nc.tensor.matmul(pj[j][:, :], w, rhs[t], start=(t == 0), stop=(t == KH - 1))
                    last.then_inc(pj_done, 1)
                if c >= 1:
                    pe.wait_ge(v_copied, c)
                for i in range(TQ):
                    for t in range(KH):
                        last = nc.tensor.matmul(pv[:, i, :], hT[:, t, QC * c + P * i:QC * c + P * (i + 1)],
                                                k.wv[:, t, :], start=(t == 0), stop=(t == KH - 1))
                last.then_inc(v_done, 1)

            for q in range(NC):
                pe.wait_ge(h_ready, q + 1)
                if q >= 2:
                    pe.wait_ge(hT_ready, 2 * (q - 1))
                for last in transpose_quarter(nc, k, k.h, q, tp[q % 2]):
                    last.then_inc(tp_done, 1)
                if q >= 1:
                    project(q - 1)
            project(NC - 1)

        @block.scalar
        def _(act):
            def high(n):
                act.wait_ge(pj_done, n + 1)
                if n >= 3 and n % 3 == 2:
                    act.wait_ge(k_sum, n // 3)
                nc.scalar.copy(part_of(n, 0), pj[n % 3][:, :]).then_inc(hi_done, 1)

            def mid(n):
                act.wait_ge(rest_done, n + 1)
                nc.scalar.copy(part_of(n, 1), rest[:, n % 2, :]).then_inc(mid_done, 1)

            def parts_of_chunk(c):
                for n in range(3 * c, 3 * c + 3):
                    if n % 3 != 2:
                        high(n)
                        if n % 3 == 1:
                            mid(n - 1)
                    else:
                        mid(n - 1)
                        high(n)
                        mid(n)

            for q in range(NC):
                for half in range(KH):
                    act.wait_ge(tp_done, 2 * q + half + 1)
                    nc.scalar.copy(hT[:, half, QC * q:QC * (q + 1)], tp[q % 2][half][:, :]).then_inc(hT_ready, 1)
                if q >= 1:
                    parts_of_chunk(q - 1)
            parts_of_chunk(NC - 1)

        @block.sync
        def _(sp):
            for c in range(NC):
                s = slice(QC * c, QC * (c + 1))
                sp.wait_ge(low_done, 3 * c + 2)
                for part in range(3):
                    sp.dma_start(k.q_dram[part, :, s].rearrange("(t p) n -> p t n", p=P),
                                 parts[:, part, :, s]).then_inc(spilled, 16)
                sp.wait_ge(spilled, 16 * 3 * (c + 1))
                if c < NC - 1:
                    load_queries(sp, k, c)


def phase_attention(nc, k, a, sem):
    units = [(c, kt) for c in range(NC) for kt in range(TQ * (c + 1))]
    chunks = [(hs, qt, ck) for c in range(NC) for hs in range(GH) for qt in range(TQ * c, TQ * (c + 1))
              for ck in range(c + 1)]
    NU, NCH = len(units), len(chunks)
    PER_U = NCH // NU
    LEAD = NU // 2

    def ahead(g, u):
        G, v = (g, u + LEAD) if u + LEAD < NU else (g + 1, u + LEAD - NU)
        if type(G) is int and G == NG:
            return G, []
        return G, list(range(PER_U * v, PER_U * (v + 1)))
    NROWDMA = 8
    ctx = ExitStack()
    with ctx:
        sc = [ctx.enter_context(nc.psum_tensor(f"p2_s{s}", [P, 2, QC], FP)) for s in range(2)]
        p1 = [ctx.enter_context(nc.psum_tensor(f"p2_p1_{s}", [P, QC], FP)) for s in range(3)]
        ot = ctx.enter_context(nc.psum_tensor("p2_o", [P, QC], FP))
        prob = ctx.enter_context(nc.sbuf_tensor("prob", [P, 2, GH, QC], FP))
        mpart = ctx.enter_context(nc.sbuf_tensor("mpart", [P, GH, NT, NC], FP))
        mneg = ctx.enter_context(nc.sbuf_tensor("mneg", [P, GH, TQ], FP))
        m2 = ctx.enter_context(nc.sbuf_tensor("m2", [P, 2, GH, TQ], BF))
        m2t = ctx.enter_context(nc.sbuf_tensor("m2t", [P, NC, 32], BF))
        p1_done = sem("p2_p1_done")
        p1_used = sem("p2_p1_used")
        dve_step = sem("p2_dve_step")
        rows_ready = sem("p2_rows_ready")
        rows_in = [sem(f"p2_rows_in{c}") for c in range(NC)]
        s_done = sem("p2_s_done")
        e_done = sem("p2_e_done")
        pv_done = sem("p2_pv_done")
        ZW = 2560
        zeros = ctx.enter_context(nc.sbuf_tensor("zeros", [P, ZW], FP))
        zero_set = sem("p2_zero_set")
        zeroed = sem("p2_zeroed")
        o_copied = sem("p2_o_copied")
        block = ctx.enter_context(nc.Block())

        @block.tensor
        def _(pe):
            def first_pass(G, n):
                hs, qt, ck = chunks[n]
                diag = ck == qt // TQ
                w = (qt % TQ + 1) * P if diag else QC
                if n >= 3:
                    pe.wait_ge(p1_used, G * NCH + n - 2)
                elif not (type(G) is int and G == 0):
                    pe.wait_ge(p1_used, G * NCH)
                last = nc.tensor.matmul(p1[n % 3][:, 0:w], k.qs[0:KROWS, qt // TQ, GH * G + hs, P * (qt % TQ):P * (qt % TQ + 1)],
                                        k.ks[0:KROWS, QC * ck:QC * ck + w], start=True, stop=not diag)
                if diag:
                    last = nc.tensor.matmul(p1[n % 3][:, w - P:w], k.ident_bf[:, :], k.maskq[:, :],
                                            start=False, stop=True)
                last.then_inc(p1_done, 1)

            def scores(g, u, pair):
                c, kt = units[u]
                off = max(0, kt - TQ * c) * P
                pe.wait_ge(e_done, g * 2 * NU + 2 * u + pair + 1)
                for i in range(2):
                    last = nc.tensor.matmul(sc[pair][:, i, off:QC], k.ks[0:KALL, P * kt:P * (kt + 1)],
                                            k.qs[0:KALL, c, GH * g + 2 * pair + i, off:QC],
                                            start=True, stop=kt < TQ * c)
                    if kt >= TQ * c:
                        last = nc.tensor.matmul(sc[pair][:, i, off:off + P], k.maskq[:, :], k.ident_bf[:, :],
                                                start=False, stop=True)
                last.then_inc(s_done, 1)

            def values(g, u):
                c, kt = units[u]
                off = max(0, kt - TQ * c) * P
                pe.wait_ge(e_done, g * 2 * NU + 2 * u + 4)
                if kt == 0:
                    pe.wait_ge(o_copied, g * NC + c + 1)
                for j in range(GH):
                    last = nc.tensor.matmul(ot[32 * j:32 * (j + 1), off:QC], k.vaug[:, kt, :],
                                            prob[:, u % 2, j, off:QC], start=(kt == 0), stop=(kt == TQ * (c + 1) - 1),
                                            tile_position=(0, 32 * j))
                last.then_inc(pv_done, 1)

            def group(g):
                for u, (c, kt) in enumerate(units):
                    G, first = ahead(g, u)
                    if kt == 0:
                        pe.wait_ge(rows_in[c], g * 16 * NROWDMA + 16 * NROWDMA)
                    scores(g, u, 0)
                    for n in first[0:1]:
                        first_pass(G, n)
                    scores(g, u, 1)
                    for n in first[1:2]:
                        first_pass(G, n)
                    if u:
                        values(g, u - 1)
                    for n in first[2:]:
                        first_pass(G, n)
                values(g, NU - 1)

            for n in range(PER_U * LEAD):
                if n == 0 or chunks[n][1] // TQ != chunks[n - 1][1] // TQ:
                    pe.wait_ge(k.q_in[chunks[n][1] // TQ], 16 * PROD)
                first_pass(0, n)
            for c in range(NC):
                pe.wait_ge(k.q_in[c], 16 * PROD)
            with pe.Fori(0, NG - 1) as g:
                group(g)
            group(NG - 1)

        @block.scalar
        def _(act):
            act.sem_inc(e_done, 2)

            def group(g):
                for u, (c, kt) in enumerate(units):
                    off = max(0, kt - TQ * c) * P
                    act.wait_ge(pv_done, g * NU + u + 1)
                    for pair in range(2):
                        act.wait_ge(s_done, g * 2 * NU + 2 * u + pair + 1)
                        nc.scalar.activation(prob[:, u % 2, 2 * pair:2 * pair + 2, off:QC], sc[pair][:, :, off:QC],
                                             ACT.Exp, scale=HD ** -0.5).then_inc(e_done, 1)

            with act.Fori(0, NG - 1) as g:
                group(g)
            group(NG - 1)

        @block.vector
        def _(dve):
            dve.sem_inc(pv_done, 2)
            dve.sem_inc(o_copied, 1)
            dve.wait_ge(pv_done, 2)
            STEPS = 3
            nc.vector.memset(mpart[:, :, :, :], NEG).then_inc(dve_step, 1)
            dve.wait_ge(dve_step, 1)

            def maxima(G, n):
                hs, qt, ck = chunks[n]
                c = qt // TQ
                w = (qt % TQ + 1) * P if ck == c else QC
                dve.wait_ge(p1_done, G * NCH + n + 1)
                nc.vector.reduce_max(mpart[:, hs, qt, ck:ck + 1], p1[n % 3][:, 0:w], AX.X).then_inc(p1_used, 1)
                if (hs, qt % TQ, ck) == (GH - 1, TQ - 1, c):
                    base = G * (STEPS * NC) + STEPS * c + 1
                    dve.wait_ge(p1_used, G * NCH + n + 1)
                    nc.vector.tensor_reduce(mneg[:, :, :], mpart[:, :, TQ * c:TQ * (c + 1), :], axis=AX.X, op=ALU.max,
                                            negate=True).then_inc(dve_step, 1)
                    dve.wait_ge(dve_step, base + 1)
                    nc.vector.tensor_copy(m2[:, 0, :, :], mneg[:, :, :]).then_inc(dve_step, 1)
                    dve.wait_ge(dve_step, base + 2)
                    nc.vector.tensor_tensor(m2[:, 1, :, :], mneg[:, :, :], m2[:, 0, :, :],
                                            ALU.subtract).then_inc(dve_step, 1)
                    dve.wait_ge(dve_step, base + 3)
                    nc.vector.transpose(m2t[:, c, :], m2[:, :, :, :].rearrange("p s h t -> p (s h t)")).then_inc(rows_ready, 1)

            def copy_out(g, c):
                dve.wait_ge(pv_done, g * NU + sum(TQ * (x + 1) for x in range(c + 1)) + 2)
                nc.vector.tensor_copy(k.oT[:, g, QC * c:QC * (c + 1)], ot[:, :]).then_inc(o_copied, 1)

            def group(g):
                for u, (c, kt) in enumerate(units):
                    G, first = ahead(g, u)
                    for n in first:
                        maxima(G, n)
                    if kt == 0 and c:
                        copy_out(g, c - 1)
                copy_out(g, NC - 1)

            for n in range(PER_U * LEAD):
                maxima(0, n)
            with dve.Fori(0, NG - 1) as g:
                group(g)
            group(NG - 1)

        @block.sync
        def _(sp):
            load_queries(sp, k, NC - 1)
            sp.wait_ge(zero_set, 1)
            flat = k.disp[0:E * CAP, :].rearrange("(p r) d -> p (r d)", p=P)
            per = E * CAP // P * D
            for c0 in range(0, per, ZW):
                w = min(ZW, per - c0)
                sp.dma_start(flat[:, c0:c0 + w], zeros[:, 0:w]).then_inc(zeroed, 16)
            zeroing = -(-per // ZW)

            def rows(G, c):
                sp.wait_ge(rows_ready, G * NC + c + 1)
                for b in range(4):
                    for part in range(2):
                        dst = k.qs[BROW + part:BROW + part + 1, c, bass.ds(GH * G, GH), :]\
                            .rearrange("o h (t b r) -> o (h t) b r", b=4, r=32)[:, :, b, :]
                        src = m2t[32 * b + NT * part:32 * b + NT * (part + 1), c, :]
                        sp.dma_start(dst, src).then_inc(rows_in[c], 16)

            with sp.Fori(0, NG) as G:
                for c in range(NC):
                    rows(G, c)
            for c in range(NC):
                sp.wait_ge(rows_in[c], 16 * NROWDMA * NG)
            sp.wait_ge(zeroed, 16 * zeroing)

        @block.gpsimd
        def _(pool):
            nc.gpsimd.memset(zeros[:, :], 0.0).then_inc(zero_set, 1)
            gabo = k.bo
            done = sem("p2_pool_done")
            nc.gpsimd.tensor_tensor(gabo[:, :], k.bo[:, :], k.mod[:, 0, GA, :], ALU.mult).then_inc(done, 1)
            pool.wait_ge(done, 1)
            for q in range(NC):
                nc.gpsimd.tensor_tensor(quarter(k.x, q), quarter(k.x, q), bcast(gabo[:, :], TQ), ALU.add).then_inc(done, 1)
            pool.wait_ge(done, 1 + NC)


def phase_project(nc, k, a, sem):
    ctx = ExitStack()
    with ctx:
        pa = [ctx.enter_context(nc.psum_tensor(f"p3_a{s}", [P, NG * P], FP)) for s in range(2)]
        pb = [ctx.enter_context(nc.psum_tensor(f"p3_b{s}", [P, KH, P], FP)) for s in range(2)]
        pc = [ctx.enter_context(nc.psum_tensor(f"p3_c{s}", [P, D], FP)) for s in range(2)]
        inv = ctx.enter_context(nc.sbuf_tensor("inv_sum", [P, 2, H], FP))
        on = ctx.enter_context(nc.sbuf_tensor("o_norm", [P, 2, D], FP))
        onT = ctx.enter_context(nc.sbuf_tensor("o_normT", [P, 2, KH, P], FP))
        gated = ctx.enter_context(nc.sbuf_tensor("gated", [P, 2, D], FP))
        a_done = sem("p3_a_done")
        inv_done = sem("p3_inv_done")
        on_ready = sem("p3_on_ready")
        b_done = sem("p3_b_done")
        onT_ready = sem("p3_onT_ready")
        c_done = sem("p3_c_done")
        gated_ready = sem("p3_gated_ready")
        x_ready = sem("p3_x_ready")
        var_ready = sem("p3_var_ready")
        rstd_ready = sem("p3_rstd_ready")
        block = ctx.enter_context(nc.Block())

        @block.tensor
        def _(pe):
            for i in range(NT + 2):
                if i < NT:
                    if i >= 2:
                        pe.wait_ge(on_ready, i - 1)
                    for g in range(NG):
                        last = nc.tensor.transpose(pa[i % 2][:, P * g:P * (g + 1)], k.oT[:, g, P * i:P * (i + 1)],
                                                   k.ident[:, :])
                    last.then_inc(a_done, 1)
                if 1 <= i <= NT:
                    n = i - 1
                    pe.wait_ge(on_ready, n + 1)
                    if n >= 2:
                        pe.wait_ge(onT_ready, n - 1)
                    for t in range(KH):
                        last = nc.tensor.transpose(pb[n % 2][:, t, :], on[:, n % 2, P * t:P * (t + 1)], k.ident[:, :])
                    last.then_inc(b_done, 1)
                if i >= 2:
                    n = i - 2
                    pe.wait_ge(onT_ready, n + 1)
                    if n >= 2:
                        pe.wait_ge(gated_ready, n - 1)
                    for t in range(KH):
                        last = nc.tensor.matmul(pc[n % 2][:, :], onT[:, n % 2, t, :], k.wo[:, t, :],
                                                start=(t == 0), stop=(t == KH - 1))
                    last.then_inc(c_done, 1)

        @block.vector
        def _(dve):
            step = stepper(dve, k.dve_step, k.dve_steps)
            for i in range(NT + 4):
                if i < NT:
                    dve.wait_ge(a_done, i + 1)
                    if i >= 2:
                        dve.wait_ge(b_done, i - 1)
                    heads = pa[i % 2][:, :].rearrange("p (h d) -> p h d", d=32)
                    nc.vector.reciprocal(inv[:, i % 2, :], heads[:, :, HD]).then_inc(inv_done, 1)
                    dve.wait_ge(inv_done, i + 1)
                    nc.vector.tensor_tensor(on[:, i % 2, :].rearrange("p (h d) -> p h d", d=HD), heads[:, :, 0:HD],
                                            last_bcast(inv[:, i % 2, :], HD), ALU.mult).then_inc(on_ready, 1)
                if 2 <= i < NT + 2:
                    n = i - 2
                    dve.wait_ge(c_done, n + 1)
                    if n >= 2:
                        dve.wait_ge(x_ready, n - 1)
                    nc.vector.tensor_tensor(gated[:, n % 2, :], pc[n % 2][:, :], k.mod[:, 0, GA, :],
                                            ALU.mult).then_inc(gated_ready, 1)
                if i >= 4:
                    n = i - 4
                    dve.wait_ge(x_ready, n + 1)
                    ln_tile_stats(nc, dve, step, k, n, var_ready)
            dve.wait_ge(rstd_ready, NC)

        @block.scalar
        def _(act):
            for i in range(NT):
                act.wait_ge(b_done, i + 1)
                if i >= 2:
                    act.wait_ge(c_done, i - 1)
                nc.scalar.copy(onT[:, i % 2, :, :], pb[i % 2][:, :, :]).then_inc(onT_ready, 1)

        @block.gpsimd
        def _(pool):
            for i in range(NT):
                pool.wait_ge(gated_ready, i + 1)
                nc.gpsimd.tensor_tensor(k.x[:, i, :], k.x[:, i, :], gated[:, i % 2, :], ALU.add).then_inc(x_ready, 1)
                if i >= TQ + 2 and (i - TQ - 2) % TQ == 0:
                    ln_rstd(nc, pool, k, (i - TQ - 2) // TQ, var_ready, rstd_ready)
            ln_rstd(nc, pool, k, NC - 1, var_ready, rstd_ready)


def load_weights0(sp, k, a, e, s):
    sp.dma_start(k.wi[:, s, :, :], a.L0_ffn_wi[e, :, :].rearrange("(t p) n -> p t n", p=P)).then_inc(k.w_in0[s], 16)
    sp.dma_start(k.wo_e[:, s, :, :], a.L0_ffn_wo[e, :, :].rearrange("(t p) n -> p t n", p=P)).then_inc(k.w_in0[s], 16)


MIX_LOADS = 8


def load_mix(sp, k, a):
    def load(dst, src):
        sp.dma_start(dst, src).then_inc(k.mix_in, 16)

    load(k.gamma[:, :], a.L1_attn_gamma.partition_broadcast(P))
    load(k.beta[:, :], a.L1_attn_beta.partition_broadcast(P))
    load(k.w_in[:, :, :], a.L1_attn_W_in.rearrange("(t p) n -> p t n", p=P))
    load(k.b_kv[:, :], a.L1_attn_b_in[D:3 * D].partition_broadcast(P))
    load(k.rot_t[:, :, :, :], a.rot_t.rearrange("(i p) s n -> p i s n", p=P))
    load(k.w_out[:, :, :], a.L1_attn_W_out.rearrange("(t p) n -> p t n", p=P))
    load(k.b_out[:, :], a.L1_attn_b_out.partition_broadcast(P))
    sp.dma_start(k.bq[:, :], a.L1_attn_b_in[0:D].rearrange("(t p) -> p t", p=P),
                 allow_slow_non_contiguous=True).then_inc(k.mix_in, 16)


def phase_router(nc, k, a, sem, layer, gate_w):
    ctx = ExitStack()
    L = f"r{layer}_"
    with ctx:
        def sb(name, shape, dt=FP):
            return ctx.enter_context(nc.sbuf_tensor(L + name, shape, dt))

        tp = [[ctx.enter_context(nc.psum_tensor(f"{L}tp{s}{t}", [P, QC], FP)) for t in range(KH)] for s in range(2)]
        plog = ctx.enter_context(nc.psum_tensor(L + "plog", [P, NT, E], FP))
        prank = ctx.enter_context(nc.psum_tensor(L + "prank", [P, NT, E], FP))
        ptot = ctx.enter_context(nc.psum_tensor(L + "ptot", [P, NT, E], FP))
        gT = sb("gT", [P, KH, E])
        hT = sb("hT", [P, 2, KH, QC])
        plT = ctx.enter_context(nc.psum_tensor(L + "plT", [P, QC], FP))
        lT = sb("lT", [P, 2, QC])
        logits = sb("logits", [P, NT, E])
        top = sb("top", [P, NT, 8])
        top_i = sb("top_i", [P, NT, 8], U32)
        top_f = sb("top_f", [P, NT, 2])
        iota_e = sb("iota_e", [P, E])
        iota_b = sb("iota_b", [P, NB])
        tok = sb("tok", [P, NT])
        cont = sb("cont", [P, E, NT])
        one_hot = [sb(f"one_hot{j}", [P, NT, E]) for j in range(2)]
        chosen = sb("chosen", [P, NT, E])
        chosen_bf = sb("chosen_bf", [P, NT, E], BF)
        ex = [sb(f"ex{j}", [P, NT, E]) for j in range(2)]
        tmp = [sb(f"tmp{j}", [P, NT, E]) for j in range(4)]
        tot = sb("tot", [P, E, NT])
        run = sb("run", [P, E, NT])
        rank = sb("rank", [P, NT, E])
        small = [sb(f"small{j}", [P, NT]) for j in range(4)]
        cnt_i = sb("cnt_i", [P, E], mybir.dt.int32)
        blk = [sb(f"blk{j}", [P, E]) for j in range(3)]
        cmp_b = sb("cmp_b", [P, NB, E])
        blk_e = sb("blk_e", [P, NB])
        scat = sb("scat", [P, 2, NT], U32)
        if layer == 1:
            pos = sb("pos", [P, 2, NT])
            blk_of = sb("blk_of", [P, 2, NT])
            pos_i = sb("pos_i", [P, NT], mybir.dt.int32)
            iota_pos = sb("iota_pos", [P, BLK])
            iota_hi = sb("iota_hi", [P, 2, NT])
            iota_empty = sb("iota_empty", [P, NB])
            tok1 = sb("tok1", [P, 1])
            at_pos = sb("at_pos", [P, 2, NT, BLK], BF)
            at_blk = sb("at_blk", [P, NT, NB])
            code_of = sb("code_of", [P, 2, NT, 2, NB], BF)
            inv = sb("inv", [P, 2, NB])
            dec = [sb(f"dec{j}", [P, NB]) for j in range(3)]
            inv_ready = sem(L + "inv_ready")
            inv_done = sem(L + "inv_done")
            raw = sb("raw", [P, 2, 3, 1024])
            raw_in = [sem(f"{L}raw_in{s}") for s in range(2)]
            w_done = sem(L + "w_done")
            w_copied = sem(L + "w_copied")
        bias_ready = sem(L + "bias_ready")
        norm_ready = sem(L + "norm_ready")
        h_ready = sem(L + "h_ready")
        gate_in = sem(L + "gate_in")
        tp_done = sem(L + "tp_done")
        hT_ready = sem(L + "hT_ready")
        lT_done = sem(L + "lT_done")
        lT_ready = sem(L + "lT_ready")
        log_done = sem(L + "log_done")
        delta_ready = sem(L + "delta_ready")
        exp_done = sem(L + "exp_done")
        chosen_ready = sem(L + "chosen_ready")
        rank_done = sem(L + "rank_done")
        iota_ready = sem(L + "iota_ready")
        if layer == 0:
            slots_ready = sem(L + "slots_ready")
        sent = sem(L + "sent")
        block = ctx.enter_context(nc.Block())
        KSEL = layer + 1

        @block.sync
        def _(sp):
            with nc.allow_non_contiguous_dma(reason="2048 numbers, off the critical path"):
                for t in range(KH):
                    sp.dma_start(gT[:, t, :], gate_w[:, P * t:P * (t + 1)].rearrange("e p -> p e")).then_inc(gate_in, 16)
            if layer == 0:
                for e in range(2):
                    load_weights0(sp, k, a, e, e)
                load_mix(sp, k, a)
            else:
                for e in range(E):
                    s = e % 2
                    if e >= 2:
                        sp.wait_ge(w_copied, 6 * (e - 1))
                    for m, w in enumerate((a.L1_ffn_w1, a.L1_ffn_w3)):
                        sp.dma_start(raw[:, s, m, :].rearrange("p (f d) -> p f d", f=F1 // P),
                                     w[e, :, :].rearrange("(f p) d -> p f d", p=P)).then_inc(raw_in[s], 16)
                    sp.dma_start(raw[:, s, 2, :].rearrange("p (t f) -> p t f", t=KH),
                                 a.L1_ffn_w2[e, :, :].rearrange("(t p) f -> p t f", p=P)).then_inc(raw_in[s], 16)
            sp.wait_ge(gate_in, 16 * KH)

        @block.tensor
        def _(pe):
            def turn_weights(e):
                s = e % 2
                pe.wait_ge(raw_in[s], 48 * (e // 2 + 1))
                for m in range(3):
                    n = 3 * e + m
                    if n >= 2:
                        pe.wait_ge(w_copied, 2 * (n - 1))
                    for half in range(2):
                        for j in range(4):
                            if m < 2:
                                src = raw[:, s, m, D * j + P * half:D * j + P * (half + 1)]
                            else:
                                f0 = F1 * (j % 2) + P * (2 * half + j // 2)
                                src = raw[:, s, 2, f0:f0 + P]
                            last = nc.tensor.transpose(tp[n % 2][half][:, P * j:P * (j + 1)], src, k.ident[:, :])
                    last.then_inc(w_done, 1)

            def logit(q):
                pe.wait_ge(hT_ready, 2 * q + 2)
                if q >= 1:
                    pe.wait_ge(lT_ready, q)
                for t in range(KH):
                    last = nc.tensor.matmul(plT[0:E, :], gT[:, t, :], hT[:, q % 2, t, :],
                                            start=(t == 0), stop=(t == KH - 1))
                last.then_inc(lT_done, 1)

            def turn_logit(q):
                pe.wait_ge(lT_ready, q + 1)
                for i in range(TQ):
                    last = nc.tensor.transpose(plog[:, TQ * q + i, :], lT[0:E, q % 2, P * i:P * (i + 1)],
                                               k.ident[0:E, 0:E])
                last.then_inc(log_done, 1)

            pe.wait_ge(gate_in, 16 * KH)
            for q in range(NC):
                pe.wait_ge(h_ready, q + 1)
                if q >= 2:
                    pe.wait_ge(hT_ready, 2 * (q - 1))
                if layer == 1 and q == 2:
                    pe.wait_ge(w_copied, 6)
                for last in transpose_quarter(nc, k, k.h, q, tp[q % 2]):
                    last.then_inc(tp_done, 1)
                if q >= 1:
                    logit(q - 1)
                if q >= 2:
                    turn_logit(q - 2)
                if layer == 1 and q == 1:
                    pe.wait_ge(hT_ready, 2 * (q + 1))
                    turn_weights(0)
            logit(NC - 1)
            turn_logit(NC - 2)
            turn_logit(NC - 1)
            if layer == 1:
                pe.wait_ge(hT_ready, 2 * NC)
                turn_weights(1)
                turn_weights(2)
            pe.wait_ge(chosen_ready, 1)
            rhs = chosen_bf[:, :, :].rearrange("p i e -> p (i e)")
            nc.tensor.matmul(prank[:, :, :].rearrange("p i e -> p (i e)"), k.before[:, :], rhs, start=True, stop=True)
            nc.tensor.matmul(ptot[:, :, :].rearrange("p i e -> p (i e)"), k.ones_bf[:, :], rhs,
                             start=True, stop=True).then_inc(rank_done, 1)
            if layer == 1:
                for e in range(3, 6):
                    turn_weights(e)
                pe.wait_ge(inv_ready, 1)
                pe.wait_ge(lT_ready, NC)
                for n in range(2 * NT):
                    j, i = divmod(n, NT)
                    last = nc.tensor.matmul(plT[:, 0:2 * NB], at_pos[:, j, i, :],
                                            code_of[:, j, i, :, :].rearrange("p s b -> p (s b)"),
                                            start=(n == 0), stop=(n == 2 * NT - 1))
                last.then_inc(inv_done, 1)
                for e in range(6, E):
                    turn_weights(e)

        @block.scalar
        def _(act):
            def copy_weights(e):
                for m in range(3):
                    act.wait_ge(w_done, 3 * e + m + 1)
                    for half in range(2):
                        nc.scalar.copy(k.w1T[:, e, m, 512 * half:512 * (half + 1)],
                                       tp[(3 * e + m) % 2][half][:, :]).then_inc(w_copied, 1)

            ln_normal(nc, act, k, 0, bias_ready, norm_ready)
            ln_normal(nc, act, k, 1, bias_ready, norm_ready)
            def copy_logit(q):
                act.wait_ge(lT_done, q + 1)
                if q >= 2:
                    act.wait_ge(log_done, q - 1)
                nc.scalar.copy(lT[0:E, q % 2, :], plT[0:E, :]).then_inc(lT_ready, 1)

            for q in range(NC):
                if q >= 2:
                    act.wait_ge(lT_done, q - 1)
                for half in range(KH):
                    act.wait_ge(tp_done, 2 * q + half + 1)
                    nc.scalar.copy(hT[:, q % 2, half, :], tp[q % 2][half][:, :]).then_inc(hT_ready, 1)
                if q + 2 < NC:
                    ln_normal(nc, act, k, q + 2, bias_ready, norm_ready)
                if q >= 1:
                    copy_logit(q - 1)
                if layer == 1 and q == 1:
                    copy_weights(0)
            copy_logit(NC - 1)

            if layer == 1:
                copy_weights(1)
                copy_weights(2)
            for j in range(KSEL):
                act.wait_ge(delta_ready, j + 1)
                nc.scalar.activation(ex[j][:, :, :], tmp[j][:, :, :], ACT.Exp).then_inc(exp_done, 1)
            if layer == 1:
                for e in range(3, E):
                    copy_weights(e)

        @block.vector
        def _(dve):
            step = stepper(dve, k.dve_step, k.dve_steps)
            tt, ts = nc.vector.tensor_tensor, nc.vector.tensor_scalar
            nc.vector.memset(cont[:, :, :], 1.0)
            step(nc.vector.memset(one_hot[1][:, :, :], 0.0))
            step(nc.vector.memset(cont[:, :, 0], 0.0))
            for q in range(NC):
                ln_bias(nc, dve, k, q, None, bias_ready)
            for q in range(NC):
                ln_modulate(nc, dve, step, k, q, k.mod[:, layer, CB, :], k.mod[:, layer, SB, :], norm_ready, h_ready)
            dve.wait_ge(log_done, NC)
            dve.wait_ge(iota_ready, 3 if layer == 0 else 6)
            if layer == 1:
                step(ts(tok1[:, :], tok[:, 0:1], 1.0, None, ALU.add))
            step(nc.vector.tensor_copy(logits[:, :, :], plog[:, :, :]))
            for i in range(NT):
                last = nc.vector.max(top[:, i, :], logits[:, i, :])
            step(last)
            for i in range(NT):
                last = nc.vector.max_index(top_i[:, i, :], top[:, i, :], logits[:, i, :])
            step(last)
            step(nc.vector.tensor_copy(top_f[:, :, :], top_i[:, :, 0:2]))
            for j in range(KSEL):
                step(tt(one_hot[j][:, :, :], bcast(iota_e[:, :], NT), last_bcast(top_f[:, :, j], E), ALU.is_equal))
            if layer == 0:
                chosen_t = one_hot[0]
            else:
                chosen_t = chosen
                step(tt(chosen[:, :, :], one_hot[0][:, :, :], one_hot[1][:, :, :], ALU.add))
            nc.vector.tensor_copy(chosen_bf[:, :, :], chosen_t[:, :, :]).then_inc(chosen_ready, 1)
            for j in range(KSEL):
                step(tt(tmp[j][:, :, :], logits[:, :, :], last_bcast(top[:, :, j], E), ALU.subtract))
                nc.vector.tensor_scalar_min(tmp[j][:, :, :], tmp[j][:, :, :], 0.0).then_inc(delta_ready, 1)
            dve.wait_ge(rank_done, 1)
            step(nc.vector.tensor_copy(tot[:, :, :], ptot[:, :, :].rearrange("p i e -> p e i")))
            flat = "p e i -> p (e i)"
            step(nc.vector.tensor_tensor_scan(run[:, :, :].rearrange(flat), cont[:, :, :].rearrange(flat),
                                              tot[:, :, :].rearrange(flat), 0.0, ALU.mult, ALU.add))
            step(tt(tot[:, :, :], run[:, :, :], tot[:, :, :], ALU.subtract))
            step(tt(rank[:, :, :], tot[:, :, :].rearrange("p e i -> p i e"), prank[:, :, :], ALU.add))
            if layer == 0:
                step(ts(tmp[1][:, :, :], rank[:, :, :], float(CAP), None, ALU.is_lt))
                step(tt(tmp[1][:, :, :], tmp[1][:, :, :], one_hot[0][:, :, :], ALU.mult))
                kept = small[0]
                step(nc.vector.reduce_sum(kept[:, :], tmp[1][:, :, :], AX.X))
                step(ts(blk[0][:, :], iota_e[:, :], float(CAP), None, ALU.mult))
                step(tt(tmp[2][:, :, :], rank[:, :, :], bcast(blk[0][:, :], NT), ALU.add))
                step(tt(tmp[2][:, :, :], tmp[2][:, :, :], one_hot[0][:, :, :], ALU.mult))
                step(nc.vector.reduce_sum(small[1][:, :], tmp[2][:, :, :], AX.X))
                step(ts(small[2][:, :], tok[:, :], float(E * CAP), None, ALU.add))
                step(tt(small[3][:, :], small[1][:, :], small[2][:, :], ALU.subtract))
                step(tt(small[3][:, :], small[3][:, :], kept[:, :], ALU.mult))
                step(tt(small[3][:, :], small[3][:, :], small[2][:, :], ALU.add))
                nc.vector.tensor_copy(scat[:, 0, :], small[3][:, :]).then_inc(slots_ready, 1)
                step(tt(small[1][:, :], small[1][:, :], kept[:, :], ALU.mult))
                step(nc.vector.tensor_copy(k.slot[:, 0, :], small[1][:, :]))
                dve.wait_ge(exp_done, 1)
                step(nc.vector.reduce_sum(small[2][:, :], ex[0][:, :, :], AX.X))
                step(nc.vector.reciprocal(small[2][:, :], small[2][:, :]))
                step(tt(k.weight[:, 0, :], small[2][:, :], kept[:, :], ALU.mult))
            else:
                step(ts(blk[0][:, :], run[:, :, NT - 1], float(BLK - 1), None, ALU.add))
                step(nc.vector.tensor_copy(cnt_i[:, :], blk[0][:, :]))
                step(ts(cnt_i[:, :], cnt_i[:, :], 7, None, ALU.arith_shift_right))
                step(nc.vector.tensor_copy(blk[0][:, :], cnt_i[:, :]))
                step(nc.vector.tensor_tensor_scan(blk[1][:, :], cont[:, 0:1, 1:E + 1].rearrange(flat), blk[0][:, :], 0.0,
                                                  ALU.mult, ALU.add))
                step(tt(blk[2][:, :], blk[1][:, :], blk[0][:, :], ALU.subtract))
                step(ts(blk[2][:, :], blk[2][:, :], float(BLK), None, ALU.mult))
                step(tt(rank[:, :, :], rank[:, :, :], bcast(blk[2][:, :], NT), ALU.add))
                for j in range(2):
                    step(tt(tmp[2][:, :, :], rank[:, :, :], one_hot[j][:, :, :], ALU.mult))
                    step(nc.vector.reduce_sum(small[j][:, :], tmp[2][:, :, :], AX.X))
                    step(nc.vector.tensor_copy(pos_i[:, :], small[j][:, :]))
                    step(ts(pos_i[:, :], pos_i[:, :], 7, None, ALU.arith_shift_right))
                    step(nc.vector.tensor_copy(blk_of[:, j, :], pos_i[:, :]))
                    step(nc.vector.scalar_tensor_tensor(pos[:, j, :], blk_of[:, j, :], -float(BLK), small[j][:, :],
                                                        ALU.mult, ALU.add))
                    tt(at_pos[:, j, :, :], bcast(iota_pos[:, :], NT), last_bcast(pos[:, j, :], BLK), ALU.is_equal)
                    step(tt(at_blk[:, :, :], bcast(iota_b[:, :], NT), last_bcast(blk_of[:, j, :], NB), ALU.is_equal))
                    step(ts(code_of[:, j, :, 0, :], at_blk[:, :, :], tok1[:, 0:1], None, ALU.mult))
                    step(tt(code_of[:, j, :, 1, :], at_blk[:, :, :], last_bcast(iota_hi[:, j, :], NB), ALU.mult))
                dve.sem_inc(inv_ready, 1)
                step(tt(cmp_b[:, :, :], bcast(blk[1][:, :], NB), last_bcast(iota_b[:, :], E), ALU.is_le))
                step(nc.vector.reduce_sum(blk_e[:, :], cmp_b[:, :, :], AX.X))
                step(nc.vector.tensor_scalar_min(blk_e[:, :], blk_e[:, :], float(E - 1)))
                step(nc.vector.tensor_copy(k.block_expert[:, :], blk_e[:, :]))
                dve.wait_ge(inv_done, 1)
                step(nc.vector.tensor_copy(inv[:, :, :].rearrange("p s b -> p (s b)"), plT[:, 0:2 * NB]))
                code, taken, row = dec
                step(nc.vector.scalar_tensor_tensor(code[:, :], inv[:, 1, :], float(P), inv[:, 0, :], ALU.mult, ALU.add))
                step(ts(taken[:, :], code[:, :], 0.5, None, ALU.is_gt))
                step(ts(code[:, :], code[:, :], -1.0, None, ALU.add))
                step(tt(row[:, :], code[:, :], iota_empty[:, :], ALU.subtract))
                step(tt(row[:, :], row[:, :], taken[:, :], ALU.mult))
                step(tt(row[:, :], row[:, :], iota_empty[:, :], ALU.add))
                step(nc.vector.tensor_copy(k.row_of[:, :], row[:, :]))
                step(ts(taken[:, :], code[:, :], float(T), -float(T), ALU.is_ge, ALU.mult))
                step(tt(code[:, :], code[:, :], taken[:, :], ALU.add))
                step(nc.vector.tensor_scalar_max(code[:, :], code[:, :], 0.0))
                step(nc.vector.tensor_copy(k.tok_of[:, :], code[:, :]))
                step(nc.vector.scalar_tensor_tensor(tmp[3][:, :, :], logits[:, :, :], -1.0, logits[:, :, :],
                                                    ALU.mult, ALU.max))
                for j in range(2):
                    thr = last_bcast(top[:, :, j], E)
                    step(tt(tmp[2][:, :, :], tmp[3][:, :, :], thr, ALU.max))
                    step(ts(tmp[2][:, :, :], tmp[2][:, :, :], 0.02, None, ALU.mult))
                    dve.wait_ge(exp_done, j + 1)
                    step(tt(tmp[j][:, :, :], thr, logits[:, :, :], ALU.subtract))
                    step(tt(tmp[2][:, :, :], tmp[j][:, :, :], tmp[2][:, :, :], ALU.is_le))
                    step(tt(ex[j][:, :, :], ex[j][:, :, :], tmp[2][:, :, :], ALU.mult))
                    if j == 1:
                        step(ts(tmp[2][:, :, :], one_hot[0][:, :, :], -1.0, 1.0, ALU.mult, ALU.add))
                        step(tt(ex[j][:, :, :], ex[j][:, :, :], tmp[2][:, :, :], ALU.mult))
                    step(nc.vector.reduce_sum(small[2][:, :], ex[j][:, :, :], AX.X))
                    step(nc.vector.reciprocal(k.weight[:, j, :], small[2][:, :]))

        @block.gpsimd
        def _(pool):
            nc.gpsimd.iota(iota_e[:, :], pattern=[[1, E]], base=0, channel_multiplier=0,
                           allow_small_or_imprecise_dtypes=True).then_inc(iota_ready, 1)
            nc.gpsimd.iota(iota_b[:, :], pattern=[[1, NB]], base=0, channel_multiplier=0,
                           allow_small_or_imprecise_dtypes=True).then_inc(iota_ready, 1)
            nc.gpsimd.iota(tok[:, :], pattern=[[P, NT]], base=0, channel_multiplier=1,
                           allow_small_or_imprecise_dtypes=True).then_inc(iota_ready, 1)
            if layer == 1:
                nc.gpsimd.iota(iota_pos[:, :], pattern=[[1, BLK]], base=0, channel_multiplier=0,
                               allow_small_or_imprecise_dtypes=True).then_inc(iota_ready, 1)
                nc.gpsimd.iota(iota_hi[:, :, :].rearrange("p j i -> p (j i)"), pattern=[[1, 2 * NT]], base=0,
                               channel_multiplier=0, allow_small_or_imprecise_dtypes=True).then_inc(iota_ready, 1)
                nc.gpsimd.iota(iota_empty[:, :], pattern=[[BLK, NB]], base=2 * T, channel_multiplier=1,
                               allow_small_or_imprecise_dtypes=True).then_inc(iota_ready, 1)
            if layer == 0:
                pool.wait_ge(h_ready, NC)
                pool.wait_ge(slots_ready, 1)
                for i in range(NT):
                    nc.gpsimd.indirect_dma_start(
                        out=k.disp, out_offset=bass.IndirectOffsetOnAxis(ap=scat[:, 0, i:i + 1], axis=0),
                        in_=k.h[:, i, :], in_offset=None).then_inc(sent, 16)
                pool.wait_ge(sent, 16 * NT)
            else:
                rows = k.h_rows.rearrange("(i p) d -> p i d", p=P)
                for q in range(NC):
                    pool.wait_ge(h_ready, q + 1)
                    pool.dma_start(rows[:, TQ * q:TQ * (q + 1), :], quarter(k.h, q)).then_inc(sent, 16)
                pool.wait_ge(sent, 16 * NC)


def phase_experts0(nc, k, a, sem):
    NI = F0 // P
    RT = [(0, P), (P, P), (2 * P, CAP - 2 * P)]
    ctx = ExitStack()
    with ctx:
        pt = [ctx.enter_context(nc.psum_tensor(f"p5_t{t}", [P, CAP], FP)) for t in range(KH)]
        ph = [ctx.enter_context(nc.psum_tensor(f"p5_h{s}", [P, CAP], FP)) for s in range(2)]
        po = [ctx.enter_context(nc.psum_tensor(f"p5_o{s}", [P, D], FP)) for s in range(2)]
        wi, wo = k.wi, k.wo_e
        rows = ctx.enter_context(nc.sbuf_tensor("rows0", [P, 2, 3, D], FP))
        rowsT = ctx.enter_context(nc.sbuf_tensor("rowsT0", [P, 2, KH, CAP], FP))
        mid = ctx.enter_context(nc.sbuf_tensor("mid0", [P, NI, CAP], FP))
        outr = ctx.enter_context(nc.sbuf_tensor("outr0", [P, 2, 3, D], FP))
        slot_in = [sem(f"p5_slot_in{s}") for s in range(2)]
        slot_free = sem("p5_slot_free")
        t_done = sem("p5_t_done")
        rowsT_ready = sem("p5_rowsT_ready")
        h_done = sem("p5_h_done")
        gelu_done = sem("p5_gelu_done")
        o_done = sem("p5_o_done")
        o_copied = sem("p5_o_copied")
        stored = [sem(f"p5_stored{s}") for s in range(2)]
        block = ctx.enter_context(nc.Block())
        LOADS = 2
        STORES = 3
        src = k.disp[0:E * CAP, :].rearrange("(e r) d -> e r d", r=CAP)
        dst = k.eout[0][0:E * CAP, :].rearrange("(e r) d -> e r d", r=CAP)

        @block.sync
        def _(sp):
            def load_rows(e, s):
                sp.dma_start(rows[:, s, 0:2, :], src[e, 0:2 * P, :].rearrange("(r p) d -> p r d", p=P)).then_inc(slot_in[s], 16)
                sp.dma_start(rows[0:RT[2][1], s, 2, :], src[e, 2 * P:CAP, :]).then_inc(slot_in[s], 16)

            for s in range(2):
                load_rows(s, s)
            with sp.Fori(1, E // 2) as i:
                for s in range(2):
                    e = 2 * i + s
                    sp.wait_ge(slot_free, e - 1)
                    load_rows(e, s)
                    load_weights0(sp, k, a, e, s)

        @block.tensor
        def _(pe):
            def transposes(i, s):
                e = 2 * i + s
                pe.wait_ge(slot_in[s], i * 16 * LOADS + 16 * LOADS)
                if not (type(e) is int and e == 0):
                    pe.wait_ge(rowsT_ready, e)
                for t in range(KH):
                    for r, (r0, rn) in enumerate(RT):
                        last = nc.tensor.transpose(pt[t][:, r0:r0 + rn], rows[0:rn, s, r, P * t:P * (t + 1)],
                                                   k.ident[0:rn, 0:rn])
                last.then_inc(t_done, 1)

            def expert(i, s, more):
                e = 2 * i + s
                pe.wait_ge(rowsT_ready, e + 1)
                pe.wait_ge(k.w_in0[s], i * 16 * LOADS + 16 * LOADS)
                for n in range(NI):
                    pe.wait_ge(gelu_done, e * NI + n + 1)
                    for t in range(KH):
                        last = nc.tensor.matmul(ph[n % 2][:, :], wi[:, s, t, P * n:P * (n + 1)], rowsT[:, s, t, :],
                                                start=(t == 0), stop=(t == KH - 1))
                    last.then_inc(h_done, 1)
                if more:
                    transposes(i + s, 1 - s)
                pe.wait_ge(gelu_done, e * NI + NI + 2)
                for r, (r0, rn) in enumerate(RT):
                    b = (3 * s + r) % 2
                    pe.wait_ge(o_copied, e * 3 + r + 1)
                    for n in range(NI):
                        if rn == P:
                            last = nc.tensor.matmul(po[b][:, :], mid[:, n, r0:r0 + rn], wo[:, s, n, :],
                                                    start=(n == 0), stop=(n == NI - 1))
                        else:
                            for t in range(KH):
                                last = nc.tensor.matmul(po[b][rn * t:rn * (t + 1), 0:P], mid[:, n, r0:r0 + rn],
                                                        wo[:, s, n, P * t:P * (t + 1)], start=(n == 0),
                                                        stop=(n == NI - 1), tile_position=(0, rn * t))
                    last.then_inc(o_done, 1)
                pe.drain().then_inc(slot_free, 1)

            transposes(0, 0)
            with pe.Fori(0, E // 2 - 1) as i:
                expert(i, 0, True)
                expert(i, 1, True)
            expert(E // 2 - 1, 0, True)
            expert(E // 2 - 1, 1, False)

        @block.scalar
        def _(act):
            act.sem_inc(gelu_done, 2)
            with act.Fori(0, E // 2) as i:
                for s in range(2):
                    e = 2 * i + s
                    act.wait_ge(t_done, e + 1)
                    nc.scalar.copy(rowsT[:, s, 0, :], pt[0][:, :])
                    nc.scalar.copy(rowsT[:, s, 1, :], pt[1][:, :]).then_inc(rowsT_ready, 1)
                    for n in range(NI):
                        act.wait_ge(h_done, e * NI + n + 1)
                        nc.scalar.activation(mid[:, n, :], ph[n % 2][:, :], ACT.Gelu).then_inc(gelu_done, 1)

        @block.vector
        def _(dve):
            dve.sem_inc(o_copied, 2)

            def pair(i, first):
                for s in range(2):
                    e = 2 * i + s
                    if not first:
                        dve.wait_ge(stored[s], i * 16 * STORES)
                    for r, (r0, rn) in enumerate(RT):
                        dve.wait_ge(o_done, e * 3 + r + 1)
                        w = D if rn == P else P
                        nc.vector.tensor_copy(outr[:, s, r, 0:w], po[(3 * s + r) % 2][:, 0:w]).then_inc(o_copied, 1)

            pair(0, True)
            with dve.Fori(1, E // 2) as i:
                pair(i, False)

        @block.gpsimd
        def _(pool):
            with pool.Fori(0, E // 2) as i:
                for s in range(2):
                    e = 2 * i + s
                    pool.wait_ge(o_copied, e * 3 + 3 + 2)
                    pool.dma_start(dst[e, 0:2 * P, :].rearrange("(r p) d -> p r d", p=P), outr[:, s, 0:2, :]).then_inc(stored[s], 16)
                    for t in range(KH):
                        rn = RT[2][1]
                        pool.dma_start(dst[e, 2 * P:CAP, P * t:P * (t + 1)],
                                       outr[rn * t:rn * (t + 1), s, 2, 0:P]).then_inc(stored[s], 16)
            for s in range(2):
                pool.wait_ge(stored[s], 16 * STORES * (E // 2))


def phase_combine1(nc, k, sem, out):
    with nc.sbuf_tensor("c_got", [P, 2, NT, D], FP) as got, nc.sbuf_tensor("c_sum", [P, 2, D], FP) as acc, \
            nc.Block() as block:
        got_in = [sem(f"c_got_in{q}") for q in range(NC)]
        x_ready = sem("c_x_ready")
        written = sem("c_written")

        @block.vector
        def _(dve):
            step = stepper(dve, k.dve_step, k.dve_steps)
            for i in range(NT):
                dve.wait_ge(got_in[i // TQ], 16 * 2)
                step(nc.vector.scalar_tensor_tensor(acc[:, i % 2, :], got[:, 0, i, :], k.weight[:, 0, i:i + 1],
                                                    k.x[:, i, :], ALU.mult, ALU.add))
                nc.vector.scalar_tensor_tensor(k.x[:, i, :], got[:, 1, i, :], k.weight[:, 1, i:i + 1],
                                               acc[:, i % 2, :], ALU.mult, ALU.add).then_inc(x_ready, 1)

        def load(eng, q, j):
            rows = k.eout[1][T * j:T * (j + 1), :].rearrange("(i p) d -> p i d", p=P)
            eng.dma_start(quarter(got[:, j, :, :], q), rows[:, TQ * q:TQ * (q + 1), :]).then_inc(got_in[q], 16)

        @block.scalar
        def _(act):
            for q in range(NC):
                load(act, q, 1)

        @block.sync
        def _(sp):
            for q in range(NC):
                load(sp, q, 0)
            ov = out[0, :, :].rearrange("(i p) d -> p i d", p=P)
            for q in range(NC):
                sp.wait_ge(x_ready, TQ * (q + 1))
                sp.dma_start(ov[:, TQ * q:TQ * (q + 1), :], quarter(k.x, q)).then_inc(written, 16)
            sp.wait_ge(written, 16 * NC)


def phase_mix(nc, k, a, sem):
    ctx = ExitStack()
    with ctx:
        def sb(name, shape, dt=FP):
            return ctx.enter_context(nc.sbuf_tensor("m_" + name, shape, dt))

        def ps(name, shape):
            return ctx.enter_context(nc.psum_tensor("m_" + name, shape, FP))

        tp = [[ps(f"tp{s}{t}", [P, QC]) for t in range(KH)] for s in range(1)][0]
        pkv = [ps(f"kv{s}", [P, 2 * D]) for s in range(2)]
        pA = ps("pA", [P, D])
        pAt = ps("pAt", [P, KH])
        pw = [ps(f"w{s}", [P, 2 * D]) for s in range(2)]
        xn = sb("xn", [P, NT, D])
        xnT = sb("xnT", [P, KH, T])
        w_in = k.w_in
        w_out = k.w_out
        wqT = sb("wqT", [P, KH, D])
        w_sc = sb("w_sc", [P, KH, D])
        w_c = sb("w_c", [P, KH, D])
        b_kv = k.b_kv
        b_out = k.b_out
        bq = k.bq
        bq_rep = sb("bq_rep", [P, KH, P])
        gamma = k.gamma
        beta = k.beta
        rot_t = k.rot_t
        kv = sb("kv", [P, 2, 2, D])
        rc = sb("rc", [P, 2, 2, 2 * ROT])
        rs = sb("rs", [P, 2, 2, 2 * ROT])
        sq = sb("sq", [P, 4, D])
        norm2 = sb("norm2", [P, NT, 2])
        inv_n = sb("inv_n", [P, NT, 2])
        w_tok = sb("w_tok", [P, NT, 32])
        A_rows = sb("A_rows", [P, D])
        ones = sb("ones", [P, 1])
        A = sb("A", [P, KH])
        b_all = sb("b_all", [P, D])
        prods = sb("prods", [P, NT, D])
        mv2 = sb("mv2", [P, NT, 2])
        var2 = sb("var2", [P, NT])
        rstd2 = sb("rstd2", [P, NT])
        nbias2 = sb("nbias2", [P, NT])
        inner = Named()
        inner.x, inner.h, inner.stats, inner.mv = k.h, xn, k.stats, mv2
        inner.var, inner.rstd, inner.mhalf, inner.nbias = var2, rstd2, k.mhalf, nbias2
        got = prods
        got_in = [sem(f"m_got_in{q}") for q in range(NC)]
        scaled = sb("scaled", [P, TQ, D])
        var_ready = sem("m_var_ready")
        rstd_ready = sem("m_rstd_ready")
        var2_ready = sem("m_var2_ready")
        rstd2_ready = sem("m_rstd2_ready")
        h_ready = sem("m_h_ready")
        bias_ready = sem("m_bias_ready")
        norm_ready_x = sem("m_norm_ready_x")
        bias2_ready = sem("m_bias2_ready")
        norm_ready_h = sem("m_norm_ready_h")
        xn_ready = sem("m_xn_ready")
        weights_in = k.mix_in
        q_done = sem("m_q_done")
        wqT_ready = sem("m_wqT_ready")
        tp_done = sem("m_tp_done")
        xnT_ready = sem("m_xnT_ready")
        kv_done = sem("m_kv_done")
        kv_ready = sem("m_kv_ready")
        norm_ready = sem("m_norm_ready")
        rot_ready = sem("m_rot_ready")
        prod_ready = sem("m_prod_ready")
        inv_ready = sem("m_inv_ready")
        w_ready = sem("m_w_ready")
        A_done = sem("m_A_done")
        Arow_ready = sem("m_Arow_ready")
        wsc_ready = sem("m_wsc_ready")
        wc_done = sem("m_wc_done")
        wc_ready = sem("m_wc_ready")
        gh_ready = sem("m_gh_ready")
        hb_ready = sem("m_hb_ready")
        y_done = sem("m_y_done")
        y_used = sem("m_y_used")
        sum_ready = sem("m_sum_ready")
        var3_ready = sem("m_var3_ready")
        rstd3_ready = sem("m_rstd3_ready")
        block = ctx.enter_context(nc.Block())

        @block.gpsimd
        def _(pool):
            for q in range(NC):
                for i in range(TQ * q, TQ * (q + 1)):
                    nc.gpsimd.indirect_dma_start(
                        out=got[:, i, :], out_offset=None, in_=k.eout[0],
                        in_offset=bass.IndirectOffsetOnAxis(ap=k.slot[:, 0, i:i + 1], axis=0)).then_inc(got_in[q], 16)
            for q in range(NC + 2):
                if q < NC:
                    ln_rstd(nc, pool, k, q, var_ready, rstd_ready)
                if q >= 2:
                    ln_rstd(nc, pool, inner, q - 2, var2_ready, rstd2_ready)

            def invert(q):
                pool.wait_ge(norm_ready, 2 * TQ * (q + 1))
                s = slice(TQ * q, TQ * (q + 1))
                nc.gpsimd.tensor_tensor(inv_n[:, s, :].rearrange("p i s -> p (i s)"),
                                        norm2[:, s, :].rearrange("p i s -> p (i s)"),
                                        k.mhalf[:, 0:2 * TQ], ALU.pow).then_inc(inv_ready, 1)

            pool.wait_ge(weights_in, 16 * MIX_LOADS)
            for i in range(NT):
                pool.wait_ge(kv_ready, i + 1)
                if i >= 2:
                    pool.wait_ge(prod_ready, i - 1)
                pairs = kv[:, i % 2, :, 0:2 * ROT].rearrange("p s (n two) -> p s n two", two=2)
                sin = rot_t[:, i, 1, :].rearrange("p (n two) -> p n two", two=2)
                dst = rs[:, i % 2, :, :].rearrange("p s (n two) -> p s n two", two=2)
                for two in range(2):
                    last = nc.gpsimd.tensor_tensor(dst[:, :, :, two], pairs[:, :, :, 1 - two],
                                                   bcast(sin[:, :, two], 2), ALU.mult)
                last.then_inc(rot_ready, 1)
                if i % TQ == TQ - 1:
                    invert(i // TQ)
            for q in range(NC):
                nc.gpsimd.tensor_tensor(quarter(k.h, q), quarter(k.h, q), bcast(k.mod[:, 1, GA, :], TQ),
                                        ALU.mult).then_inc(gh_ready, 1)
                pool.wait_ge(gh_ready, q + 1)
                nc.gpsimd.tensor_tensor(quarter(k.x, q), quarter(k.x, q), quarter(k.h, q), ALU.add).then_inc(hb_ready, 1)
            for q in range(NC):
                ln_rstd(nc, pool, k, q, var3_ready, rstd3_ready)

        @block.vector
        def _(dve):
            step = stepper(dve, k.dve_step, k.dve_steps)
            tt = nc.vector.tensor_tensor
            nc.vector.memset(ones[:, :], 1.0)
            step(nc.vector.memset(w_tok[:, :, :], 0.0))

            def combine(q):
                dve.wait_ge(got_in[q], 16 * TQ)
                for n in range(TQ):
                    i = TQ * q + n
                    last = nc.vector.scalar_tensor_tensor(scaled[:, n, :], got[:, i, :], k.weight[:, 0, i:i + 1],
                                                          k.mod[:, 0, GB, :], ALU.mult, ALU.mult)
                step(last)
                step(tt(quarter(k.x, q), quarter(k.x, q), scaled[:, :, :], ALU.add))

            for q in range(NC + 2):
                if q < NC:
                    combine(q)
                    ln_stats(nc, dve, step, k, q, var_ready)
                if 1 <= q <= NC:
                    ln_bias(nc, dve, k, q - 1, rstd_ready, bias_ready)
                if q >= 2:
                    ln_modulate(nc, dve, step, k, q - 2, k.mod[:, 1, CA, :], k.mod[:, 1, SA, :], norm_ready_x, h_ready)
                    dve.wait_ge(h_ready, q - 1)
                    ln_stats(nc, dve, step, inner, q - 2, var2_ready)
                if q >= 3:
                    ln_bias(nc, dve, inner, q - 3, rstd2_ready, bias2_ready)
            dve.wait_ge(weights_in, 16 * MIX_LOADS)
            step(nc.vector.tensor_copy(bq_rep[:, :, :], last_bcast(bq[:, :], P)))
            ln_bias(nc, dve, inner, NC - 1, rstd2_ready, bias2_ready)
            for q in range(NC):
                ln_modulate(nc, dve, step, inner, q, gamma[:, :], beta[:, :], norm_ready_h, xn_ready)

            def products(i):
                s = i % 2
                x2 = kv[:, s, :, 0:2 * ROT]
                step(tt(rc[:, s, :, :], x2, bcast(rot_t[:, i, 0, :], 2), ALU.mult))
                dve.wait_ge(rot_ready, i + 1)
                step(tt(rc[:, s, :, :], rc[:, s, :, :], rs[:, s, :, :], ALU.add))
                tt(prods[:, i, 2 * ROT:D], kv[:, s, 0, 2 * ROT:D], kv[:, s, 1, 2 * ROT:D], ALU.mult)
                tt(prods[:, i, 0:2 * ROT], rc[:, s, 0, :], rc[:, s, 1, :], ALU.mult).then_inc(prod_ready, 1)

            for i in range(NT + 1):
                if i < NT:
                    dve.wait_ge(kv_done, i + 1)
                    if i >= 2:
                        dve.wait_ge(norm_ready, 2 * (i - 1))
                        dve.wait_ge(prod_ready, i - 1)
                    tt(kv[:, i % 2, :, :].rearrange("p s d -> p (s d)"), pkv[i % 2][:, :], b_kv[:, :],
                       ALU.add).then_inc(kv_ready, 1)
                if i >= 1:
                    dve.wait_ge(kv_ready, i)
                    products(i - 1)
                if i % TQ == 0 and i >= TQ:
                    q = i // TQ - 1
                    dve.wait_ge(inv_ready, q + 1)
                    tt(w_tok[:, TQ * q:TQ * (q + 1), 0], inv_n[:, TQ * q:TQ * (q + 1), 0],
                       inv_n[:, TQ * q:TQ * (q + 1), 1], ALU.mult).then_inc(w_ready, 1)
            gate = k.mod[:, 1, GA, :]
            step(tt(w_out[:, :, :], w_out[:, :, :], bcast(gate, KH), ALU.mult))
            step(tt(b_out[:, :], b_out[:, :], gate, ALU.mult))
            dve.wait_ge(A_done, 1)
            nc.vector.tensor_copy(A_rows[:, :], pA[:, :]).then_inc(Arow_ready, 1)
            dve.wait_ge(A_done, 2)
            step(nc.vector.tensor_scalar(A[:, :], pAt[:, :], 0.5, 0.5, ALU.mult, ALU.add))
            for t in range(KH):
                last = nc.vector.tensor_scalar(w_sc[:, t, :], w_out[:, t, :], A[:, t:t + 1], None, ALU.mult)
            last.then_inc(wsc_ready, 1)
            dve.wait_ge(wc_done, 1)
            nc.vector.tensor_copy(w_c[:, :, :].rearrange("p t n -> p (t n)"), pw[0][:, :]).then_inc(wc_ready, 1)
            dve.wait_ge(wc_done, 2)
            tt(b_all[:, :], pw[1][:, 0:D], b_out[:, :], ALU.add).then_inc(wc_ready, 1)
            dve.wait_ge(wc_ready, 2)
            for i in range(NT):
                if i % TQ == 0:
                    q = i // TQ
                    dve.wait_ge(hb_ready, q + 1)
                    tt(quarter(k.x, q), quarter(k.x, q), bcast(b_all[:, :], TQ), ALU.add).then_inc(sum_ready, 1)
                    dve.wait_ge(sum_ready, q + 1)
                dve.wait_ge(y_done, i + 1)
                tt(k.x[:, i, :], k.x[:, i, :], pkv[i % 2][:, 0:D], ALU.add).then_inc(y_used, 1)
                if i:
                    dve.wait_ge(y_used, i)
                    ln_tile_stats(nc, dve, step, k, i - 1, var3_ready)
            dve.wait_ge(y_used, NT)
            ln_tile_stats(nc, dve, step, k, NT - 1, var3_ready)
            dve.wait_ge(rstd3_ready, NC)

        @block.scalar
        def _(act):
            for q in range(NC + 2):
                if q < NC:
                    ln_normal(nc, act, k, q, bias_ready, norm_ready_x)
                if q >= 2:
                    ln_normal(nc, act, inner, q - 2, bias2_ready, norm_ready_h)
            act.wait_ge(q_done, 1)
            nc.scalar.copy(wqT[:, :, :].rearrange("p t n -> p (t n)"), pw[0][:, :]).then_inc(wqT_ready, 1)

            def squares(i):
                act.wait_ge(kv_ready, i + 1)
                for s in range(2):
                    n = 2 * i + s
                    if n >= 4:
                        act.wait_ge(norm_ready, n - 3)
                    nc.scalar.activation(sq[:, n % 4, :], kv[:, i % 2, s, :], ACT.Square,
                                         accum_out=norm2[:, i, s:s + 1]).then_inc(norm_ready, 1)

            for q in range(NC):
                for half in range(KH):
                    act.wait_ge(tp_done, 2 * q + half + 1)
                    nc.scalar.copy(xnT[:, half, QC * q:QC * (q + 1)], tp[half][:, :]).then_inc(xnT_ready, 1)
                if q >= 1:
                    for i in range(TQ * (q - 1), TQ * q):
                        squares(i)
            for i in range(TQ * (NC - 1), NT):
                squares(i)

        @block.tensor
        def _(pe):
            pe.wait_ge(weights_in, 16 * MIX_LOADS)
            for m in range(KH):
                for t in range(KH):
                    last = nc.tensor.transpose(pw[0][:, D * m + P * t:D * m + P * (t + 1)],
                                               w_in[:, t, P * m:P * (m + 1)], k.ident[:, :])
            last.then_inc(q_done, 1)

            def keys_values(i):
                pe.wait_ge(xnT_ready, 2 * (i // TQ) + 2)
                if i >= 2:
                    pe.wait_ge(kv_ready, i - 1)
                for t in range(KH):
                    last = nc.tensor.matmul(pkv[i % 2][:, :], xnT[:, t, P * i:P * (i + 1)], w_in[:, t, D:3 * D],
                                            start=(t == 0), stop=(t == KH - 1))
                last.then_inc(kv_done, 1)

            def sum_products(q):
                pe.wait_ge(prod_ready, TQ * (q + 1))
                pe.wait_ge(w_ready, q + 1)
                for j in range(TQ):
                    last = nc.tensor.matmul(pA[32 * j:32 * (j + 1), :], w_tok[:, TQ * q + j, :], prods[:, TQ * q + j, :],
                                            start=(q == 0), stop=(q == NC - 1), tile_position=(0, 32 * j))
                return last

            for q in range(NC):
                pe.wait_ge(xn_ready, q + 1)
                if q >= 1:
                    pe.wait_ge(xnT_ready, 2 * q)
                for last in transpose_quarter(nc, k, xn, q, tp):
                    last.then_inc(tp_done, 1)
                if q >= 1:
                    for i in range(TQ * (q - 1), TQ * q):
                        keys_values(i)
            for i in range(TQ * (NC - 1), NT):
                keys_values(i)
            for q in range(NC):
                last = sum_products(q)
            last.then_inc(A_done, 1)
            pe.wait_ge(Arow_ready, 1)
            for t in range(KH):
                last = nc.tensor.matmul(pAt[:, t:t + 1], A_rows[:, P * t:P * (t + 1)], ones[:, :], start=True, stop=True)
            last.then_inc(A_done, 1)
            pe.wait_ge(wqT_ready, 1)
            pe.wait_ge(wsc_ready, 1)
            for t in range(KH):
                for m in range(KH):
                    last = nc.tensor.matmul(pw[0][:, D * t:D * (t + 1)], wqT[:, m, P * t:P * (t + 1)], w_sc[:, m, :],
                                            start=(m == 0), stop=(m == KH - 1))
            last.then_inc(wc_done, 1)
            for m in range(KH):
                last = nc.tensor.matmul(pw[1][:, 0:D], bq_rep[:, m, :], w_sc[:, m, :], start=(m == 0), stop=(m == KH - 1))
            last.then_inc(wc_done, 1)
            pe.wait_ge(wc_ready, 1)
            pe.wait_ge(kv_ready, NT)
            for i in range(NT):
                if i >= 2:
                    pe.wait_ge(y_used, i - 1)
                for t in range(KH):
                    last = nc.tensor.matmul(pkv[i % 2][:, 0:D], xnT[:, t, P * i:P * (i + 1)], w_c[:, t, :],
                                            start=(t == 0), stop=(t == KH - 1))
                last.then_inc(y_done, 1)


def phase_experts1(nc, k, a, sem):
    FT = F1 // P
    ctx = ExitStack()
    with ctx:
        px = ctx.enter_context(nc.psum_tensor("e1_x", [P, KH, P], FP))
        pg = [ctx.enter_context(nc.psum_tensor(f"e1_g{s}", [P, F1], FP)) for s in range(2)]
        pu = [ctx.enter_context(nc.psum_tensor(f"e1_u{s}", [P, F1], FP)) for s in range(2)]
        pm = ctx.enter_context(nc.psum_tensor("e1_m", [P, F1], FP))
        py = ctx.enter_context(nc.psum_tensor("e1_y", [P, D], FP))
        xb = ctx.enter_context(nc.sbuf_tensor("xb", [P, 2, D], FP))
        xT = ctx.enter_context(nc.sbuf_tensor("xT1", [P, 2, KH, P], FP))
        g = ctx.enter_context(nc.sbuf_tensor("silu_g", [P, 2, F1], FP))
        m = ctx.enter_context(nc.sbuf_tensor("mid1", [P, 2, F1], FP))
        mT = ctx.enter_context(nc.sbuf_tensor("mid1T", [P, 2, F1], FP))
        y = ctx.enter_context(nc.sbuf_tensor("y1", [P, 2, D], FP))
        x_in = [sem(f"e1_x_in{s}") for s in range(2)]
        t_done = sem("e1_t_done")
        xT_ready = sem("e1_xT_ready")
        g_done = sem("e1_g_done")
        u_done = sem("e1_u_done")
        silu_ready = sem("e1_silu_ready")
        m_ready = sem("e1_m_ready")
        mt_done = sem("e1_mt_done")
        mT_ready = sem("e1_mT_ready")
        y_done = sem("e1_y_done")
        y_ready = sem("e1_y_ready")
        stored = [sem(f"e1_stored{s}") for s in range(2)]
        block = ctx.enter_context(nc.Block())
        assert NB % 2 == 1
        PAIRS = NB // 2

        @block.tensor
        def _(pe):
            def expert_of(b):
                return pe.value_load(k.block_expert[0:1, bass.ds(b, 1)], min_val=0, max_val=E - 1)

            def transpose_rows(i, s):
                b = 2 * i + s
                pe.wait_ge(x_in[s], i * 16 + 16)
                if not (type(b) is int and b == 0):
                    pe.wait_ge(xT_ready, b)
                for t in range(KH):
                    last = nc.tensor.transpose(px[:, t, :], xb[:, s, P * t:P * (t + 1)], k.ident[:, :])
                last.then_inc(t_done, 1)

            def product(out, s, e, mat, done):
                for t in range(KH):
                    last = nc.tensor.matmul(out[:, :], xT[:, s, t, :], k.w1T[:, e, mat, 512 * t:512 * (t + 1)],
                                            start=(t == 0), stop=(t == KH - 1))
                last.then_inc(done, 1)

            def back(i, s, first):
                b = 2 * i + s
                pe.wait_ge(m_ready, b + 1)
                if not (type(b) is int and b == 0):
                    pe.wait_ge(mT_ready, b)
                for f in range(FT):
                    last = nc.tensor.transpose(pm[:, P * f:P * (f + 1)], m[:, s, P * f:P * (f + 1)], k.ident[:, :])
                last.then_inc(mt_done, 1)

            def second(i, s, e, first):
                b = 2 * i + s
                pe.wait_ge(mT_ready, b + 1)
                if not (type(b) is int and b == 0):
                    pe.wait_ge(y_ready, b)
                for f in range(FT):
                    last = nc.tensor.matmul(py[:, :], mT[:, s, P * f:P * (f + 1)], k.w1T[:, e, 2, D * f:D * (f + 1)],
                                            start=(f == 0), stop=(f == FT - 1))
                last.then_inc(y_done, 1)

            def body(i, s, peeled, head=False, tail=False):
                b = 2 * i + s
                e = expert_of(b)
                pe.wait_ge(xT_ready, b + 1)
                if not peeled:
                    pe.wait_ge(m_ready, b - 1)
                product(pg[s], s, e, 0, g_done)
                if not head:
                    pi, psl = (i, 0) if s else (i - 1, 1)
                    ep = expert_of(b - 1)
                    back(pi, psl, peeled)
                product(pu[s], s, e, 1, u_done)
                if not tail:
                    transpose_rows(i + s, 1 - s)
                if not head:
                    second(pi, psl, ep, peeled)

            transpose_rows(0, 0)
            body(0, 0, True, head=True)
            body(0, 1, True)
            with pe.Fori(1, PAIRS) as i:
                body(i, 0, False)
                body(i, 1, False)
            body(PAIRS, 0, False, tail=True)
            e = expert_of(NB - 1)
            back(PAIRS, 0, False)
            second(PAIRS, 0, e, False)

        @block.scalar
        def _(act):
            def rows(i, s):
                b = 2 * i + s
                act.wait_ge(t_done, b + 1)
                nc.scalar.copy(xT[:, s, :, :], px[:, :, :]).then_inc(xT_ready, 1)

            def silu(i, s, peeled):
                b = 2 * i + s
                act.wait_ge(g_done, b + 1)
                if not peeled:
                    act.wait_ge(m_ready, b - 1)
                nc.scalar.activation(g[:, s, :], pg[s][:, :], ACT.Silu).then_inc(silu_ready, 1)

            def hidden(i, s):
                b = 2 * i + s
                act.wait_ge(mt_done, b + 1)
                nc.scalar.copy(mT[:, s, :], pm[:, :]).then_inc(mT_ready, 1)

            def body(i, s, peeled, head=False, tail=False):
                silu(i, s, peeled)
                if not head:
                    hidden(*((i, 0) if s else (i - 1, 1)))
                if not tail:
                    rows(i + s, 1 - s)

            rows(0, 0)
            body(0, 0, True, head=True)
            body(0, 1, True)
            with act.Fori(1, PAIRS) as i:
                body(i, 0, False)
                body(i, 1, False)
            body(PAIRS, 0, False, tail=True)
            hidden(PAIRS, 0)

        @block.vector
        def _(dve):
            def gate(i, s, peeled):
                b = 2 * i + s
                dve.wait_ge(silu_ready, b + 1)
                dve.wait_ge(u_done, b + 1)
                if not peeled:
                    dve.wait_ge(mt_done, b - 1)
                nc.vector.tensor_tensor(m[:, s, :], g[:, s, :], pu[s][:, :], ALU.mult).then_inc(m_ready, 1)

            def copy_y(i, s, peeled):
                b = 2 * i + s
                dve.wait_ge(y_done, b + 1)
                if not peeled:
                    dve.wait_ge(stored[s], i * 16)
                nc.vector.tensor_tensor(y[:, s, :], py[:, :], k.mod[:, 1, GB, :], ALU.mult).then_inc(y_ready, 1)

            gate(0, 0, True)
            gate(0, 1, True)
            copy_y(0, 0, True)
            gate(1, 0, False)
            copy_y(0, 1, True)
            gate(1, 1, False)
            copy_y(1, 0, False)
            with dve.Fori(2, PAIRS) as i:
                gate(i, 0, False)
                copy_y(i - 1, 1, False)
                gate(i, 1, False)
                copy_y(i, 0, False)
            gate(PAIRS, 0, False)
            copy_y(PAIRS - 1, 1, False)
            copy_y(PAIRS, 0, False)

        @block.gpsimd
        def _(pool):
            def gather(b, s, peeled=False):
                if not peeled:
                    pool.wait_ge(t_done, b - 1)
                nc.gpsimd.indirect_dma_start(
                    out=xb[:, s, :], out_offset=None, in_=k.h_rows,
                    in_offset=bass.IndirectOffsetOnAxis(ap=k.tok_of[:, b:b + 1], axis=0)).then_inc(x_in[s], 16)

            def scatter(b, s):
                pool.wait_ge(y_ready, b + 1)
                nc.gpsimd.indirect_dma_start(
                    out=k.eout[1], out_offset=bass.IndirectOffsetOnAxis(ap=k.row_of[:, b:b + 1], axis=0),
                    in_=y[:, s, :], in_offset=None).then_inc(stored[s], 16)

            for b in range(NB + 4):
                if b < NB:
                    gather(b, b % 2, b < 2)
                if b >= 4:
                    scatter(b - 4, b % 2)
            pool.wait_ge(stored[0], 16 * (PAIRS + 1))
            pool.wait_ge(stored[1], 16 * PAIRS)


def named_inputs(aps):
    a = Named()
    a.L0_attn_x = aps["L0_attn_x"]
    a.L0_attn_Wq = aps["L0_attn_Wq"]
    a.L0_attn_Wk = aps["L0_attn_Wk"]
    a.L0_attn_Wv = aps["L0_attn_Wv"]
    a.L0_attn_Wo = aps["L0_attn_Wo"]
    a.L0_attn_bo = aps["L0_attn_bo"]
    a.L0_ffn_gate_weight = aps["L0_ffn_gate_weight"]
    a.L0_ffn_wi = aps["L0_ffn_wi"]
    a.L0_ffn_wo = aps["L0_ffn_wo"]
    a.L0_c = aps["L0_c"]
    a.L0_wmod = aps["L0_wmod"]
    a.L1_attn_W_in = aps["L1_attn_W_in"]
    a.L1_attn_b_in = aps["L1_attn_b_in"]
    a.L1_attn_W_out = aps["L1_attn_W_out"]
    a.L1_attn_b_out = aps["L1_attn_b_out"]
    a.L1_attn_gamma = aps["L1_attn_gamma"]
    a.L1_attn_beta = aps["L1_attn_beta"]
    a.L1_ffn_gate_w = aps["L1_ffn_gate_w"]
    a.L1_ffn_w1 = aps["L1_ffn_w1"]
    a.L1_ffn_w2 = aps["L1_ffn_w2"]
    a.L1_ffn_w3 = aps["L1_ffn_w3"]
    a.L1_c = aps["L1_c"]
    a.L1_wmod = aps["L1_wmod"]
    a.kpart = aps["kpart"]
    a.rot_t = aps["rot_t"]
    return a


def build(nc, a, out, upto=99):
    ctx = ExitStack()
    with ctx:
        def sem(name):
            return ctx.enter_context(nc.semaphore(name))

        early = []

        def early_sem(name):
            early.append(nc.alloc_semaphore(name=name))
            return early[-1]

        def sbuf(stack, name, shape, dt=FP):
            return stack.enter_context(nc.sbuf_tensor("k_" + name, shape, dt))

        k = Named()
        k.disp = nc.dram_tensor("disp0", [E * CAP + T, D], FP).ap()
        k.h_rows = nc.dram_tensor("h_rows", [T, D], FP).ap()
        k.q_dram = nc.dram_tensor("q_dram", [3, D, T], BF).ap()
        k.dve_step = sem("dve_step")
        k.dve_steps = [0]
        k.q_in = [sem(f"q_in{c}") for c in range(NC)]
        k.eout = [nc.dram_tensor("eout0", [E * CAP, D], FP).ap(), nc.dram_tensor("eout1", [2 * T + NB * BLK, D], FP).ap()]
        k.tok_of = sbuf(ctx, "tok_of", [P, NB], U32)
        k.row_of = sbuf(ctx, "row_of", [P, NB], U32)
        k.x = sbuf(ctx, "x", [P, NT, D])
        k.h = sbuf(ctx, "h", [P, NT, D])
        k.mod = sbuf(ctx, "mod", [P, 2, MODS, D])
        k.mv = sbuf(ctx, "mv", [P, NT, 2])
        k.var = sbuf(ctx, "var", [P, NT])
        k.rstd = sbuf(ctx, "rstd", [P, NT])
        k.mhalf = sbuf(ctx, "mhalf", [P, NT])
        k.slot = sbuf(ctx, "slot", [P, 2, NT], U32)
        k.weight = sbuf(ctx, "weight", [P, 2, NT])
        k.block_expert = sbuf(ctx, "block_expert", [P, NB], U32)
        k.ident = sbuf(ctx, "ident", [P, P])
        k.ident_bf = sbuf(ctx, "ident_bf", [P, P], BF)
        k.maskq = sbuf(ctx, "maskq", [P, P], BF)
        k.before = sbuf(ctx, "before", [P, P], BF)
        k.ones_bf = sbuf(ctx, "ones_bf", [P, P], BF)
        k.nbias = sbuf(ctx, "nbias", [P, NT])
        k.stats = sbuf(ctx, "stats", [P, NT, 6])
        attn = ExitStack()
        with attn:
            k.wq = sbuf(attn, "wq", [P, KH, D])
            k.wk1 = sbuf(attn, "wk1", [P, KH, HD])
            k.wv = sbuf(attn, "wv", [P, KH, HD])
            k.wo = sbuf(attn, "wo", [P, KH, D])
            k.bo = sbuf(attn, "bo", [P, D])
            k.kpart = sbuf(attn, "kpart", [P, 4])
            k.ks = sbuf(attn, "ks", [P, T], BF)
            k.vaug = sbuf(attn, "vaug", [P, NT, 32])
            k.qs = sbuf(attn, "qs", [P, NC, H, QC], BF)
            phase_setup(nc, k, a, early_sem)
            if upto >= 1:
                phase_qkv(nc, k, a, early_sem)
            k.oT = sbuf(attn, "oT", [P, NG, T])
            if upto >= 2:
                phase_attention(nc, k, a, early_sem)
            if upto >= 3:
                phase_project(nc, k, a, early_sem)
        nc.clear_and_free_semaphores(early)
        nc.all_engine_barrier()
        mixer = ExitStack()
        k.w_in = sbuf(mixer, "w_in", [P, KH, 3 * D])
        k.w_out = sbuf(mixer, "w_out", [P, KH, D])
        k.b_kv = sbuf(mixer, "b_kv", [P, 2 * D])
        k.b_out = sbuf(mixer, "b_out", [P, D])
        k.bq = sbuf(mixer, "bq", [P, KH])
        k.gamma = sbuf(mixer, "gamma", [P, D])
        k.beta = sbuf(mixer, "beta", [P, D])
        k.rot_t = sbuf(mixer, "rot_t", [P, NT, 2, 2 * ROT])
        k.mix_in = sem("mix_in")
        experts0 = ExitStack()
        with experts0:
            k.wi = sbuf(experts0, "wi", [P, 2, KH, F0])
            k.wo_e = sbuf(experts0, "wo_e", [P, 2, F0 // P, D])
            k.w_in0 = [sem(f"w_in0_{s}") for s in range(2)]
            if upto >= 4:
                phase_router(nc, k, a, sem, 0, a.L0_ffn_gate_weight)
            if upto >= 5:
                phase_experts0(nc, k, a, sem)
        if upto >= 7:
            phase_mix(nc, k, a, sem)
        mixer.close()
        experts1 = ExitStack()
        with experts1:
            k.w1T = sbuf(experts1, "w1T", [P, E, 3, 1024])
            if upto >= 8:
                phase_router(nc, k, a, sem, 1, a.L1_ffn_gate_w)
            if upto >= 9:
                phase_experts1(nc, k, a, sem)
            if upto >= 10:
                phase_combine1(nc, k, sem, out)


def consts():
    import numpy as np
    kpart = np.zeros((P, 4), np.float32)
    for g, part in enumerate((0, 1, 2, 0, 1, 0, 1)):
        kpart[HD * g:HD * (g + 1), part] = 1.0
    kpart[BROW:KALL, 3] = 1.0
    inv = (np.float32(1.0) / np.float32(10000.0) ** (np.arange(0, 2 * ROT, 2, dtype=np.float32)
                                                     / np.float32(2 * ROT))).astype(np.float32)
    angle = np.arange(T, dtype=np.float32)[:, None] * inv[None, :]
    rot = np.zeros((T, 2, ROT, 2), np.float32)
    rot[:, 0, :, :] = np.cos(angle)[:, :, None]
    rot[:, 1, :, 0] = -np.sin(angle)
    rot[:, 1, :, 1] = np.sin(angle)
    return {"kpart": kpart, "rot_t": rot.reshape(T, 2, 2 * ROT)}


_INS = ['L0_attn_x', 'L0_attn_Wq', 'L0_attn_Wk', 'L0_attn_Wv', 'L0_attn_Wo', 'L0_attn_bo', 'L0_ffn_gate_weight',
        'L0_ffn_wi', 'L0_ffn_wo', 'L0_c', 'L0_wmod', 'L1_attn_W_in', 'L1_attn_b_in', 'L1_attn_W_out',
        'L1_attn_b_out', 'L1_attn_gamma', 'L1_attn_beta', 'L1_ffn_gate_w', 'L1_ffn_w1', 'L1_ffn_w2', 'L1_ffn_w3',
        'L1_c', 'L1_wmod']


def kernel(**inputs):
    import numpy as _np
    import concourse.bacc as _bacc
    from concourse import mybir as _mybir
    from concourse.bass_utils import run_bass_kernel_spmd as _run

    nc = _bacc.Bacc("TRN2", target_bir_lowering=False, num_devices=1)
    arrays, aps = {}, {}
    for name, value in [(n, inputs[n]) for n in _INS] + list(consts().items()):
        arr = _np.ascontiguousarray(value)
        arrays[f"in_{name}_dram"] = arr
        aps[name] = nc.dram_tensor(f"in_{name}_dram", arr.shape, _mybir.dt.from_np(arr.dtype), kind="ExternalInput").ap()
    out = nc.dram_tensor("out_0_dram", (1, T, D), FP, kind="ExternalOutput").ap()
    build(nc, named_inputs(aps), out)
    r = _run(nc, [arrays], core_ids=[0])
    return r.results[0]["out_0_dram"]
```
